# Optimizing a Trainium2 kernel written in Bass

```python
import numpy as np
import jax
import jax.numpy as jnp

def _softmax(x, axis=-1):
    return jax.nn.softmax(x, axis=axis)

def _gelu(x):
    return jax.nn.gelu(x, approximate=True)

def _silu(x):
    return jax.nn.silu(x)

def _sigmoid(x):
    return jax.nn.sigmoid(x)

def _layernorm(x, axis=-1, eps=1e-05):
    m = jnp.mean(x, axis=axis, keepdims=True)
    v = jnp.var(x, axis=axis, keepdims=True)
    return (x - m) / jnp.sqrt(v + eps)

def _scatter_add(tgt, idx, src, axis=0):
    return tgt.at[idx].add(src)

def _segment_sum(src, seg, n):
    return jax.ops.segment_sum(src, seg, n)
kernel_name = 'mk_perceiver_d1_seqx_r2_8a3b0b'

def setup_inputs(seed: int=0):
    np.random.seed(seed)
    _w = jnp.asarray

    def _rec_inputs():
        import jax
        import jax.numpy as jnp
        _rk = jax.random.key(seed)
        x = 7.22e-05 + 1 * jax.random.normal(jax.random.fold_in(_rk, 1), (32, 32, 512), jnp.float32)
        _lenS = 32 - jax.random.randint(jax.random.fold_in(_rk, 7), (32,), 0, max(1, 32 // 4) + 1, jnp.int32)
        _lenS2 = 257 - jax.random.randint(jax.random.fold_in(_rk, 8), (32,), 0, max(1, 257 // 4) + 1, jnp.int32)
        _ctx_768P = jax.random.normal(jax.random.fold_in(_rk, 11), (32, 16, 384), jnp.float32)
        _ctx_768c = jax.random.dirichlet(jax.random.fold_in(_rk, 511), 0.3 * jnp.ones((16,), jnp.float32), (32, 257))
        _ctx_768t = jnp.einsum('bsk,bkd->bsd', _ctx_768c, _ctx_768P)
        _ctx_768t = _ctx_768t * jax.lax.rsqrt(jnp.mean(jnp.square(_ctx_768t)) + 1e-12) * 0.953939
        ctx_768 = -0.000191848 + 0.999787 * (_ctx_768t + 0.3 * jax.random.normal(jax.random.fold_in(_rk, 611), (32, 257, 384), jnp.float32))
        return (x, ctx_768)
    x, ctx_768 = _rec_inputs()

    def _L0_xattn_setup():
        import jax, jax.numpy as jnp
        import numpy as np
        DIM = 512
        CTX_DIM = 384
        H = 16
        DH = 64
        INNER = H * DH
        EPS = 1e-05

        def layer_norm(x, gamma, beta):
            mu = jnp.mean(x, axis=-1, keepdims=True)
            var = jnp.mean(jnp.square(x - mu), axis=-1, keepdims=True)
            return (x - mu) * jax.lax.rsqrt(var + EPS) * gamma + beta
        key = jax.random.key(seed)
        ks = jax.random.split(key, 8)
        B, N, M = (4, 1024, 1024)
        x = jax.random.normal(ks[0], (B, N, DIM), dtype=jnp.float32)
        context = jax.random.normal(ks[1], (B, M, CTX_DIM), dtype=jnp.float32)
        g_x = jnp.ones((DIM,), jnp.float32)
        b_x = jnp.zeros((DIM,), jnp.float32)
        g_c = jnp.ones((CTX_DIM,), jnp.float32)
        b_c = jnp.zeros((CTX_DIM,), jnp.float32)
        Wq = jax.random.normal(ks[2], (DIM, INNER), dtype=jnp.float32) / np.sqrt(DIM)
        Wk = jax.random.normal(ks[3], (CTX_DIM, INNER), dtype=jnp.float32) / np.sqrt(CTX_DIM)
        Wv = jax.random.normal(ks[4], (CTX_DIM, INNER), dtype=jnp.float32) / np.sqrt(CTX_DIM)
        Wo = jax.random.normal(ks[5], (INNER, DIM), dtype=jnp.float32) / np.sqrt(INNER)
        return {'x': x, 'context': context, 'g_x': g_x, 'b_x': b_x, 'g_c': g_c, 'b_c': b_c, 'Wq': Wq, 'Wk': Wk, 'Wv': Wv, 'Wo': Wo}
    _L0_xattn_all = _L0_xattn_setup()
    _L0_xattn_in = {k: v for k, v in _L0_xattn_all.items() if k in ('g_x', 'b_x', 'g_c', 'b_c', 'Wq', 'Wk', 'Wv', 'Wo')}
    del _L0_xattn_all

    def _L0_attn_setup():
        import jax, jax.numpy as jnp
        import numpy as np
        B, N, F, H = (4, 1024, 512, 16)
        DH = F // H
        SQRT_D = float(DH) ** 0.5
        key = jax.random.key(seed)
        k1, k2, k3 = jax.random.split(key, 3)
        x = jax.random.normal(k1, (B, N, F), dtype=jnp.float32)
        W_qkv = jax.random.normal(k2, (F, F), dtype=jnp.float32) * (1.0 / np.sqrt(F))
        W_o = jax.random.normal(k3, (F, F), dtype=jnp.float32) * (1.0 / np.sqrt(F))
        return {'x': x, 'W_qkv': W_qkv, 'W_o': W_o}
    _L0_attn_all = _L0_attn_setup()
    _L0_attn_in = {k: v for k, v in _L0_attn_all.items() if k in ('W_qkv', 'W_o')}
    del _L0_attn_all

    def _L0_ffn_setup():
        import jax, jax.numpy as jnp
        import numpy as np
        TOP_K = 2
        TEMP = 0.9
        EPS = 1e-05
        B, S, D, F, E = (2, 1024, 512, 2048, 8)

        def _moe_forward(x, gate_w, gate_b, w1, b1, w2, b2, ln_g, ln_b):
            logits = (x @ gate_w + gate_b) / TEMP
            topk_vals, topk_idx = jax.lax.top_k(logits, TOP_K)
            keep = jax.nn.one_hot(topk_idx, E, dtype=jnp.bool_).any(-2)
            masked = jnp.where(keep, logits, -jnp.inf)
            gate_probs = jax.nn.softmax(masked, axis=-1)
            h = jnp.einsum('bsd,edf->bsef', x, w1) + b1
            h = jax.nn.gelu(h, approximate=False)
            expert_out = jnp.einsum('bsef,efd->bsed', h, w2) + b2
            out = jnp.einsum('bse,bsed->bsd', gate_probs, expert_out)
            mu = out.mean(-1, keepdims=True)
            var = out.var(-1, keepdims=True)
            out = (out - mu) / jnp.sqrt(var + EPS) * ln_g + ln_b
            return out
        key = jax.random.key(seed)
        ks = jax.random.split(key, 4)
        scale_in = 1.0 / np.sqrt(D)
        scale_ff = 1.0 / np.sqrt(F)
        return {'x': jax.random.normal(ks[0], (B, S, D), jnp.float32), 'gate_w': jax.random.normal(ks[1], (D, E), jnp.float32) * scale_in, 'gate_b': jnp.zeros((E,), jnp.float32), 'w1': jax.random.normal(ks[2], (E, D, F), jnp.float32) * scale_in, 'b1': jnp.zeros((E, F), jnp.float32), 'w2': jax.random.normal(ks[3], (E, F, D), jnp.float32) * scale_ff, 'b2': jnp.zeros((E, D), jnp.float32), 'ln_g': jnp.ones((D,), jnp.float32), 'ln_b': jnp.zeros((D,), jnp.float32)}
    _L0_ffn_all = _L0_ffn_setup()
    _L0_ffn_in = {k: v for k, v in _L0_ffn_all.items() if k in ('gate_w', 'gate_b', 'w1', 'b1', 'w2', 'b2', 'ln_g', 'ln_b')}
    del _L0_ffn_all
    return {'x': x, 'ctx_768': ctx_768, 'L0_xattn_g_x': _L0_xattn_in['g_x'], 'L0_xattn_b_x': _L0_xattn_in['b_x'], 'L0_xattn_g_c': _L0_xattn_in['g_c'], 'L0_xattn_b_c': _L0_xattn_in['b_c'], 'L0_xattn_Wq': _L0_xattn_in['Wq'], 'L0_xattn_Wk': _L0_xattn_in['Wk'], 'L0_xattn_Wv': _L0_xattn_in['Wv'], 'L0_xattn_Wo': _L0_xattn_in['Wo'], 'L0_attn_W_qkv': _L0_attn_in['W_qkv'], 'L0_attn_W_o': _L0_attn_in['W_o'], 'L0_ffn_gate_w': _L0_ffn_in['gate_w'], 'L0_ffn_gate_b': _L0_ffn_in['gate_b'], 'L0_ffn_w1': _L0_ffn_in['w1'], 'L0_ffn_b1': _L0_ffn_in['b1'], 'L0_ffn_w2': _L0_ffn_in['w2'], 'L0_ffn_b2': _L0_ffn_in['b2'], 'L0_ffn_ln_g': _L0_ffn_in['ln_g'], 'L0_ffn_ln_b': _L0_ffn_in['ln_b']}

def reference(x, ctx_768, L0_xattn_g_x, L0_xattn_b_x, L0_xattn_g_c, L0_xattn_b_c, L0_xattn_Wq, L0_xattn_Wk, L0_xattn_Wv, L0_xattn_Wo, L0_attn_W_qkv, L0_attn_W_o, L0_ffn_gate_w, L0_ffn_gate_b, L0_ffn_w1, L0_ffn_b1, L0_ffn_w2, L0_ffn_b2, L0_ffn_ln_g, L0_ffn_ln_b):
    import jax
    import jax.numpy as jnp

    def _L0_xattn_ref(x, context, g_x, b_x, g_c, b_c, Wq, Wk, Wv, Wo):
        import jax, jax.numpy as jnp
        import numpy as np
        DIM = 512
        CTX_DIM = 384
        H = 16
        DH = 64
        INNER = H * DH
        EPS = 1e-05

        def layer_norm(x, gamma, beta):
            mu = jnp.mean(x, axis=-1, keepdims=True)
            var = jnp.mean(jnp.square(x - mu), axis=-1, keepdims=True)
            return (x - mu) * jax.lax.rsqrt(var + EPS) * gamma + beta
        B, N, _ = x.shape
        M = context.shape[1]
        xn = layer_norm(x, g_x, b_x)
        cn = layer_norm(context, g_c, b_c)
        q = (xn @ Wq).reshape(B, N, H, DH).transpose(0, 2, 1, 3)
        k = (cn @ Wk).reshape(B, M, H, DH).transpose(0, 2, 1, 3)
        v = (cn @ Wv).reshape(B, M, H, DH).transpose(0, 2, 1, 3)
        scale = jnp.float32(1.0 / np.sqrt(DH))
        sim = jnp.einsum('bhid,bhjd->bhij', q, k) * scale
        attn = jax.nn.softmax(sim, axis=-1)
        out = jnp.einsum('bhij,bhjd->bhid', attn, v)
        out = out.transpose(0, 2, 1, 3).reshape(B, N, INNER)
        return out @ Wo

    def _L0_attn_ref(x, W_qkv, W_o):
        import jax, jax.numpy as jnp
        import numpy as np
        B, N, F, H = (4, 1024, 512, 16)
        DH = F // H
        SQRT_D = float(DH) ** 0.5
        b, n, _ = x.shape
        qkv = (x @ W_qkv.T).reshape(b, n, H, DH).transpose(0, 2, 1, 3)
        score = jax.nn.softmax(jnp.einsum('bhif,bhjf->bhij', qkv, qkv) / SQRT_D, axis=-1)
        attn = jnp.einsum('bhij,bhjf->bihf', score, qkv)
        out = attn.reshape(b, n, F) @ W_o.T
        return out

    def _L0_ffn_ref(x, gate_w, gate_b, w1, b1, w2, b2, ln_g, ln_b):
        import jax, jax.numpy as jnp
        import numpy as np
        TOP_K = 2
        TEMP = 0.9
        EPS = 1e-05
        B, S, D, F, E = (2, 1024, 512, 2048, 8)

        def _moe_forward(x, gate_w, gate_b, w1, b1, w2, b2, ln_g, ln_b):
            logits = (x @ gate_w + gate_b) / TEMP
            topk_vals, topk_idx = jax.lax.top_k(logits, TOP_K)
            keep = jax.nn.one_hot(topk_idx, E, dtype=jnp.bool_).any(-2)
            masked = jnp.where(keep, logits, -jnp.inf)
            gate_probs = jax.nn.softmax(masked, axis=-1)
            h = jnp.einsum('bsd,edf->bsef', x, w1) + b1
            h = jax.nn.gelu(h, approximate=False)
            expert_out = jnp.einsum('bsef,efd->bsed', h, w2) + b2
            out = jnp.einsum('bse,bsed->bsd', gate_probs, expert_out)
            mu = out.mean(-1, keepdims=True)
            var = out.var(-1, keepdims=True)
            out = (out - mu) / jnp.sqrt(var + EPS) * ln_g + ln_b
            return out
        return _moe_forward(x, gate_w, gate_b, w1, b1, w2, b2, ln_g, ln_b)
    x = x + _L0_xattn_ref(_layernorm(x, axis=-1), ctx_768, L0_xattn_g_x, L0_xattn_b_x, L0_xattn_g_c, L0_xattn_b_c, L0_xattn_Wq, L0_xattn_Wk, L0_xattn_Wv, L0_xattn_Wo)
    x = x + _L0_attn_ref(_layernorm(x, axis=-1), L0_attn_W_qkv, L0_attn_W_o)
    x = x + _L0_ffn_ref(_layernorm(x, axis=-1), L0_ffn_gate_w, L0_ffn_gate_b, L0_ffn_w1, L0_ffn_b1, L0_ffn_w2, L0_ffn_b2, L0_ffn_ln_g, L0_ffn_ln_b)
    return x

_drawn_inputs = setup_inputs


def setup_inputs(seed=0):
    import zlib

    import numpy as np

    out = dict(_drawn_inputs(seed))
    spreads = {'L0_xattn_g_x': (1.0, 0.2),
     'L0_xattn_b_x': (0.0, 0.1),
     'L0_xattn_g_c': (1.0, 0.2),
     'L0_xattn_b_c': (0.0, 0.1),
     'L0_ffn_gate_b': (0.0, 0.1),
     'L0_ffn_b1': (0.0, 0.1),
     'L0_ffn_b2': (0.0, 0.1),
     'L0_ffn_ln_g': (1.0, 0.2),
     'L0_ffn_ln_b': (0.0, 0.1)}
    factors = {}
    for name, (base, spread) in spreads.items():
        noise = np.random.default_rng([zlib.crc32(name.encode()), seed]).standard_normal(out[name].shape)
        drawn = base * np.exp(spread * noise) if base else spread * noise
        out[name] = jnp.asarray(drawn.astype(out[name].dtype))
    for name, factor in factors.items():
        out[name] = (out[name] * factor).astype(out[name].dtype)
    return out
```

```python
from contextlib import ExitStack

import concourse.bass as bass
from concourse import mybir

F32 = mybir.dt.float32
I32 = mybir.dt.int32
U32 = mybir.dt.uint32
ALU = mybir.AluOpType
ACT = mybir.ActivationFunctionType
AX = mybir.AxisListType.X

P = 128
BATCH, TOK, DIM = 32, 32, 512
KEYS, CTX = 257, 384
HEADS, HDIM = 16, 64
INNER = HEADS * HDIM
SHEADS, SDIM = 16, 32
EXPERTS, FF, TOPK = 8, 2048, 2
EPS = 1e-5
XSCALE = HDIM ** -0.5
SSCALE = SDIM ** -0.5
TEMP = 0.9

GB = P // TOK
GROUPS = BATCH // GB
KD = DIM // P
KC = CTX // P
KI = INNER // P
KF = FF // P
HG = HEADS // GB
PART = [86, 86, 85]
KOFF = [0, 86, 172]
FB = FF // 512
JOBS = BATCH * TOK * TOPK // P + EXPERTS - 1

QT_AT, QK_AT, UT_AT, O_AT, WO_AT, M_FILLS = 0, 2, 14, 26, 28, 30
TP_FIRST, TP_FILLS = 4, 25
TP_AT = {}
for _kind, _b in (("ct", 1), ("pt", 0), ("ct", 2), ("pt", 1), ("ct", 3), ("pt", 2), ("pt", 3), ("ct", 4)):
    for _k in range(3):
        TP_AT[_kind, _b, _k] = len(TP_AT)
TP_AT["xn"] = len(TP_AT)
YT_AT, KQ_AT, V_AT, SS_AT, PV_AT, WS_AT, YT2_AT, LG_AT, B_FILLS = 0, 1, 2, 3, 7, 8, 9, 10, 11


def at_least(eng, sem, n):
    if not isinstance(n, int) or n > 0:
        eng.wait_ge(sem, n)


def chain(eng, sem, before):
    count = [0]

    def link(instruction):
        count[0] += 1
        instruction.then_inc(sem, 1)
        eng.wait_ge(sem, before + count[0])

    return link


def perceiver_layer(nc, x, ctx_768, g_x, b_x, g_c, b_c, Wq, Wk, Wv, Wo, W_qkv, W_o,
                    gate_w, gate_b, w1, b1, w2, b2, ln_g, ln_b, out):
    with ExitStack() as stack:
        def sb(name, shape, dt=F32):
            return stack.enter_context(nc.sbuf_tensor(name, shape, dt))

        def sem(name):
            return stack.enter_context(nc.semaphore(name))

        xs_dram = nc.dram_tensor("xs_rows", (JOBS * P, DIM), F32).ap()
        ys_dram = nc.dram_tensor("ys_rows", (JOBS * P, DIM), F32).ap()

        moe_w = sb("moe_w", [P, 2, KD * FF + KF * DIM])
        moe_flat = moe_w[:, :, :].rearrange("p s n -> p (s n)")
        s0, s1 = moe_w[:, 0, :], moe_w[:, 1, :]
        qkT = s0[:, 0:6144].rearrange("p (c b r) -> p c b r", c=KC, b=GB)
        uT = s0[:, 6144:12288].rearrange("p (c h b t) -> p c h b t", c=KC, h=HEADS, b=GB)
        qT = s0[:, 12288:13312].rearrange("p (m t) -> p m t", m=KI)
        oT = s0[:, 13312:14336].rearrange("p (m t) -> p m t", m=KI)
        cnT = s0[:, 14336:14336 + 2 * KC * KEYS].rearrange("p (s c j) -> p s c j", s=2, c=KC)
        wk_rows = s0[:, 6144:9216].rearrange("p (c n) -> p c n", c=KC)
        qkv_rows = s0[:, 0:2048].rearrange("p (c n) -> p c n", c=KD)
        wos_rows = s0[:, 2048:4096].rearrange("p (c n) -> p c n", c=KD)
        wq = s1[:, 0:4096].rearrange("p (c n) -> p c n", c=KD)
        wkT = s1[:, 4096:7168].rearrange("p (m c) -> p m c", m=KI)
        wv = s1[:, 7168:10240].rearrange("p (c n) -> p c n", c=KC)
        wo = s1[:, 10240:14336].rearrange("p (m n) -> p m n", m=KI)
        wqkvT = s1[:, 14336:16384].rearrange("p (c n) -> p c n", c=KD)

        arena = sb("arena", [P, 8704])
        ctx = arena[:, 0:4608].rearrange("p (s k c) -> p s k c", s=GB, k=3)
        probs = arena[:, 4608:5636].rearrange("p (h j) -> p h j", h=HG)
        pT = arena[:, 5636:7172].rearrange("p (k r) -> p k r", k=3)
        xn = arena[:, 7172:7684]
        xnT = arena[:, 7684:8196].rearrange("p (c t) -> p c t", c=KD)
        b1_rows = arena[:, 0:4096]
        y_all = arena[:, 4096:8192].rearrange("p (g d) -> p g d", g=GROUPS)
        h_sb = arena[:, 4096:5120].rearrange("p (s f) -> p s f", s=2)
        hT_sb = arena[:, 5120:6144].rearrange("p (s c t) -> p s c t", s=2, c=KD)
        xs = arena[:, 6144:6656]
        xsT = arena[:, 6656:7168].rearrange("p (c t) -> p c t", c=KD)
        ys = arena[:, 7168:7680]

        x_all = sb("x_all", [P, GROUPS, DIM])
        wosT = sb("wosT", [P, KD, DIM])
        y = sb("y", [P, DIM])
        yT = sb("yT", [P, KD, P])
        kqT = sb("kqT", [P, KD, P])
        v_sb = sb("v_sb", [P, DIM])
        sS = sb("sS", [P, SHEADS, TOK])
        blocks = sb("blocks", [P, SHEADS, P])
        ident = sb("ident", [P, P])
        before = sb("before", [P, P])
        ones = sb("ones", [P, P])
        gate = sb("gate", [P, KD, EXPERTS])
        gcol = sb("gcol", [P, 2, KD])
        ccol = sb("ccol", [P, 2, KC])
        gate_bias = sb("gate_bias", [P, EXPERTS])
        half = sb("half", [P, 8])
        stats = sb("stats", [P, 6])
        mv = sb("mv", [P, 2])
        rstd = sb("rstd", [P, 1])
        y2mv = sb("y2mv", [P, GROUPS, 2])
        cstats = sb("cstats", [P, 3, 6])
        cmv = sb("cmv", [P, 3, 2])
        crstd = sb("crstd", [P, 3])
        mx = sb("mx", [P, HG])
        negm = sb("negm", [P, HG])
        rsum = sb("rsum", [P, HG])
        rinv = sb("rinv", [P, HG])
        smx = sb("smx", [P, SHEADS])
        ssum = sb("ssum", [P, SHEADS])
        logits = sb("logits", [P, GROUPS, EXPERTS])

        late = blocks[:, :, :].rearrange("p h t -> p (h t)")
        late_used = [0]

        def late_f32(*shape):
            at, size = late_used[0], 1
            for n in shape:
                size *= n
            late_used[0] += size
            piece = late[:, at:at + size]
            names = "abc"[:len(shape)]
            return piece.rearrange(f"p ({' '.join(names)}) -> p {' '.join(names)}", **dict(zip(names, shape)))

        top = late_f32(GROUPS, 8)
        topi = sb("topi", [P, GROUPS, 8], U32)
        topf = late_f32(GROUPS, TOPK)
        iota_e = sb("iota_e", [P, EXPERTS])
        iota_q = sb("iota_q", [P, 8])
        iota_j = sb("iota_j", [P, 24])
        hot = late_f32(GROUPS, TOPK, EXPERTS)
        mask = late_f32(GROUPS, EXPERTS)
        rank = late_f32(GROUPS, EXPERTS)
        tot = late_f32(GROUPS + 1, EXPERTS)
        cmp8 = late_f32(EXPERTS, 8)
        tiles = late_f32(EXPERTS)
        ends = late_f32(EXPERTS + 1)
        cmpj = late_f32(24, EXPERTS)
        jobf = late_f32(24)
        job_e = sb("job_e", [P, 24], I32)
        end_i = sb("end_i", [P, EXPERTS + 1], I32)
        prod = late_f32(GROUPS, TOPK, EXPERTS)
        slotf = late_f32(GROUPS, TOPK)
        slots = sb("slots", [P, GROUPS, TOPK], U32)
        gp = late_f32(GROUPS, TOPK)
        ge = late_f32(GROUPS)
        gs = late_f32(GROUPS)
        pe_all = late_f32(GROUPS, EXPERTS)
        zero1 = sb("zero1", [P, 1])
        pool_mark = sb("pool_mark", [P, 1])
        dve_mark = sb("dve_mark", [P, 1])
        pT8 = wosT[0:EXPERTS, 2:4, :].rearrange("e a (b n) -> e (a b) n", n=P)

        got = s0[:, 0:8192].rearrange("p (t k d) -> p t k d", t=GROUPS, k=TOPK)
        fin = s0[:, 8192:12288].rearrange("p (t d) -> p t d", t=GROUPS)
        lnrow = wosT[:, 0:2, :]
        b2_sb = sS[0:EXPERTS, :, :].rearrange("e h t -> e (h t)")

        bank = [stack.enter_context(nc.psum_tensor(f"bank{i}", [P, 512], F32)) for i in range(8)]
        TP, M, BK = bank[4], [bank[5], bank[6]], bank[7]

        x0_in = sem("x0_in")
        x_in, wk_in, wq_in, wv_in, wo_in = sem("x_in"), sem("wk_in"), sem("wq_in"), sem("wv_in"), sem("wo_in")
        qkv_in, wos_in, cols_in, rows_in, gate_in = sem("qkv_in"), sem("wos_in"), sem("cols_in"), sem("rows_in"), sem("gate_in")
        ctx_in = [sem(f"ctx_in{b}") for b in range(GB)]
        xs_zeroed = sem("xs_zeroed")
        consts, ident_ok, zeros_ok, memset_ok = sem("consts"), sem("ident_ok"), sem("zeros_ok"), sem("memset_ok")
        setup_full, setup_free = sem("setup_full"), [sem(f"setup_free{i}") for i in range(2)]
        ln_step, ln_var, ln_rstd = sem("ln_step"), sem("ln_var"), sem("ln_rstd")
        cn_step, cn_var, cn_rstd, cn_done = sem("cn_step"), sem("cn_var"), sem("cn_rstd"), sem("cn_done")
        xn_done, y_done, x1_done, x2_done = sem("xn_done"), sem("y_done"), sem("x1_done"), sem("x2_done")
        tp_full, tp_free = sem("tp_full"), sem("tp_free")
        m_full, m_free = sem("m_full"), [sem(f"m_free{i}") for i in range(2)]
        b_full, b_free = sem("b_full"), sem("b_free")
        s_full, max_done, neg_done, exp_done = sem("s_full"), sem("max_done"), sem("neg_done"), sem("exp_done")
        rinv_done, norm_done = sem("rinv_done"), sem("norm_done")
        ss_step, ss_ready, sexp_done, wb_done = sem("ss_step"), sem("ss_ready"), sem("sexp_done"), sem("wb_done")

        cmv_ok = sem("cmv_ok")
        kept_done = sem("kept_done")
        rt_step, mask_done, ranks_full, exps_ready, gexp_done = sem("rt_step"), sem("mask_done"), sem("ranks_full"), sem("exps_ready"), sem("gexp_done")
        slots_ready, jobs_ready, yall_ready, scattered = sem("slots_ready"), sem("jobs_ready"), sem("yall_ready"), sem("scattered")
        experts_in = sem("experts_in")
        w_even, w_odd = sem("w_even"), sem("w_odd")
        xs_in, xt_full, xt_out = sem("xs_in"), sem("xt_full"), sem("xt_out")
        h_full, h_biased, h_act = sem("h_full"), sem("h_biased"), sem("h_act")
        hT_full, hT_out, mm2_done, ys_out, ys_stored = sem("hT_full"), sem("hT_out"), sem("mm2_done"), sem("ys_out"), sem("ys_stored")
        pw_ready, pw_full, pw_out, xb_done = sem("pw_ready"), sem("pw_full"), sem("pw_out"), sem("xb_done")
        gathered = [sem(f"gathered{t}") for t in range(GROUPS)]
        b2_full, b2_used, fin_step, fin_var = sem("b2_full"), sem("b2_used"), sem("fin_step"), sem("fin_var")
        fin_rstd, fin_done, stored = sem("fin_rstd"), sem("fin_done"), sem("stored")

        block = stack.enter_context(nc.Block())

        ctx_rows = ctx_768.rearrange("b m c -> (b m) c")
        x_rows = x.rearrange("b t d -> (b t) d")
        out_rows = out.rearrange("b t d -> (b t) d")

        def tp(g, at):
            return TP_FIRST + TP_FILLS * g + TP_AT[at]

        Y, XT = bank[4], bank[5]

        def expert_load(eng, e, slot, done):
            one = bass.ds(e, 1)
            eng.dma_start(moe_w[:, slot, 0:8192].rearrange("p (c f) -> p c f", c=KD),
                          w1[one, :, :].rearrange("e (c p) f -> p (e c) f", p=P)).then_inc(done, 16)
            eng.dma_start(moe_w[:, slot, 8192:16384].rearrange("p (c d) -> p c d", c=KF),
                          w2[one, :, :].rearrange("e (c p) d -> p (e c) d", p=P)).then_inc(done, 16)
            eng.dma_start(b1_rows[:, slot * FF:(slot + 1) * FF], b1[one, :].to_broadcast([P, FF])).then_inc(done, 16)

        def moe_loads(sp):
            sp.wait_ge(b_full, B_FILLS * GROUPS)
            sp.dma_start(lnrow[:, 0, :], ln_g.rearrange("(o d) -> o d", o=1).to_broadcast([P, DIM])).then_inc(rows_in, 16)
            sp.dma_start(lnrow[:, 1, :], ln_b.rearrange("(o d) -> o d", o=1).to_broadcast([P, DIM])).then_inc(rows_in, 16)
            sp.dma_start(b2_sb[:, :], b2[:, :]).then_inc(rows_in, 16)

            def xs_load(j):
                sp.dma_start(xs, xs_dram[bass.ds(j * P, P), :]).then_inc(xs_in, 16)

            def ys_store(j):
                sp.wait_ge(ys_out, j + 1)
                sp.dma_start(ys_dram[bass.ds(j * P, P), :], ys).then_inc(ys_stored, 16)

            sp.wait_ge(scattered, 16 * GROUPS * TOPK)
            xs_load(0)
            sp.wait_ge(xt_full, 1)
            xs_load(1)
            with sp.Fori(2, JOBS) as j:
                sp.wait_ge(xt_full, j)
                xs_load(j)
                ys_store(j - 2)
            ys_store(JOBS - 2)
            ys_store(JOBS - 1)
            for t in range(GROUPS):
                sp.wait_ge(fin_done, t + 1)
                sp.dma_start(out_rows[t * P:(t + 1) * P, :], fin[:, t, :]).then_inc(stored, 16)
            sp.wait_ge(stored, 16 * GROUPS)

        def expert_landed(pool, e, slot):
            if not isinstance(e, int) or e > 0:
                pool.wait_ge(experts_in, e)
            pool.wait_ge((w_even, w_odd)[slot], 48 * ((e - slot) // 2 + 1))
            nc.gpsimd.tensor_tensor(pool_mark[:, :], half[:, 0:1], half[:, 0:1], ALU.add).then_inc(experts_in, 1)

        def moe_pool(pool):
            pool.wait_ge(xs_zeroed, 16 * JOBS)
            pool.wait_ge(slots_ready, 1)
            for t in range(GROUPS):
                pool.wait_ge(yall_ready, t + 1)
                for k in range(TOPK):
                    nc.gpsimd.indirect_dma_start(
                        out=xs_dram[:, :], out_offset=bass.IndirectOffsetOnAxis(ap=slots[:, t, k:k + 1], axis=0),
                        in_=y_all[:, t, :], in_offset=None).then_inc(scattered, 16)
            expert_landed(pool, 0, 0)
            pool.wait_ge(jobs_ready, 1)
            with pool.Fori(1, EXPERTS // 2) as i:
                for slot, done in ((0, w_even), (1, w_odd)):
                    e = 2 * i + slot
                    expert_landed(pool, e - 1, 1 - slot)
                    ended = pool.value_load(end_i[0:1, bass.ds(e - 1, 1)], min_val=1, max_val=1 + FB * JOBS)
                    pool.wait_ge(mm2_done, ended)
                    expert_load(pool, e, slot, done)
            expert_landed(pool, EXPERTS - 1, 1)
            pool.wait_ge(ys_stored, 16 * JOBS)
            for t in range(GROUPS):
                for k in range(TOPK):
                    nc.gpsimd.indirect_dma_start(
                        out=got[:, t, k, :], out_offset=None, in_=ys_dram[:, :],
                        in_offset=bass.IndirectOffsetOnAxis(ap=slots[:, t, k:k + 1], axis=0)).then_inc(gathered[t], 16)
                if t >= 2:
                    fin_pow(pool, t - 2)
            fin_pow(pool, GROUPS - 2)
            fin_pow(pool, GROUPS - 1)

        def fin_pow(pool, t):
            pool.wait_ge(fin_var, t + 1)
            nc.gpsimd.tensor_tensor(rstd[:, :], mv[:, 1:2], half[:, 0:1], ALU.pow).then_inc(fin_rstd, 1)

        def moe_act(act):
            act.wait_ge(exps_ready, 1)
            nc.scalar.activation(ge[:, :], gs[:, :], ACT.Exp).then_inc(gexp_done, 1)

            def xt_copy(j):
                act.wait_ge(xt_full, j + 1)
                if not isinstance(j, int) or j > 0:
                    act.wait_ge(h_full, FB * j)
                nc.scalar.copy(xsT.rearrange("p c t -> p (c t)"), XT[:, :]).then_inc(xt_out, 1)

            def gelu(j, fb):
                act.wait_ge(h_biased, FB * j + fb + 1)
                nc.scalar.activation(h_sb[:, fb % 2, :], h_sb[:, fb % 2, :], ACT.Gelu).then_inc(h_act, 1)

            xt_copy(0)
            with act.Fori(0, JOBS - 1) as j:
                for fb in range(FB):
                    gelu(j, fb)
                xt_copy(j + 1)
            for fb in range(FB):
                gelu(JOBS - 1, fb)

        def moe_dve(dve):
            dve.wait_ge(b_free, 1 + B_FILLS * GROUPS)
            dve.wait_ge(kept_done, GROUPS)
            dve.wait_ge(consts, 4)
            link = chain(dve, rt_step, 0)
            link(nc.vector.memset(tot[:, 0, :], 0.0))
            link(nc.vector.memset(ends[:, 0:1], 0.0))
            flat = logits[:, :, :].rearrange("p g e -> p (g e)")
            link(nc.vector.tensor_scalar(flat, flat, 1.0 / TEMP, None, ALU.mult))
            for t in range(GROUPS):
                last = nc.vector.max(top[:, t, :], logits[:, t, :])
            link(last)
            nc.vector.tensor_tensor(gs[:, :], top[:, :, 1], top[:, :, 0], ALU.subtract).then_inc(exps_ready, 1)
            for t in range(GROUPS):
                last = nc.vector.max_index(topi[:, t, :], top[:, t, :], logits[:, t, :])
            link(last)
            link(nc.vector.tensor_copy(topf[:, :, :], topi[:, :, 0:TOPK]))
            tk = [P, GROUPS * TOPK, EXPERTS]
            link(nc.vector.tensor_tensor(hot[:, :, :, :].rearrange("p t k e -> p (t k) e"),
                                         iota_e[:, :].unsqueeze(1).to_broadcast(tk),
                                         topf[:, :, :].rearrange("p t k -> p (t k)").unsqueeze(2).to_broadcast(tk),
                                         ALU.is_equal))
            nc.vector.tensor_tensor(mask[:, :, :], hot[:, :, 0, :], hot[:, :, 1, :], ALU.add).then_inc(mask_done, 1)
            for t in range(GROUPS):
                nc.vector.tensor_scalar(y_all[:, t, :], x_all[:, t, :], y2mv[:, t, 0:1], y2mv[:, t, 1:2],
                                        ALU.subtract, ALU.mult).then_inc(yall_ready, 1)
            dve.wait_ge(ranks_full, 1)
            for t in range(GROUPS):
                link(nc.vector.tensor_tensor(tot[:, t + 1, :], tot[:, t, :], bank[1][:, t * EXPERTS:(t + 1) * EXPERTS], ALU.add))
            nc.vector.tensor_tensor(rank[:, :, :], tot[:, 0:GROUPS, :],
                                    bank[0][:, 0:GROUPS * EXPERTS].rearrange("p (t e) -> p t e", e=EXPERTS), ALU.add)
            e8 = [P, EXPERTS, 8]
            link(nc.vector.tensor_tensor(cmp8[:, :, :], tot[:, GROUPS, :].unsqueeze(2).to_broadcast(e8),
                                         iota_q[:, :].unsqueeze(1).to_broadcast(e8), ALU.is_gt))
            link(nc.vector.reduce_sum(tiles[:, :], cmp8[:, :, :], AX))
            for e in range(EXPERTS):
                link(nc.vector.tensor_tensor(ends[:, e + 1:e + 2], ends[:, e:e + 1], tiles[:, e:e + 1], ALU.add))
            te = [P, GROUPS, EXPERTS]
            link(nc.vector.scalar_tensor_tensor(out=rank[:, :, :], in0=ends[:, 0:EXPERTS].unsqueeze(1).to_broadcast(te),
                                                scalar=float(P), in1=rank[:, :, :], op0=ALU.mult, op1=ALU.add))
            for k in range(TOPK):
                last = nc.vector.tensor_tensor(prod[:, :, k, :], hot[:, :, k, :], rank[:, :, :], ALU.mult)
            link(last)
            link(nc.vector.reduce_sum(slotf[:, :, :], prod[:, :, :, :], AX))
            nc.vector.tensor_copy(slots[:, :, :], slotf[:, :, :]).then_inc(slots_ready, 1)
            je = [P, 24, EXPERTS]
            link(nc.vector.tensor_tensor(cmpj[:, :, :], iota_j[:, :].unsqueeze(2).to_broadcast(je),
                                         ends[:, 1:EXPERTS + 1].unsqueeze(1).to_broadcast(je), ALU.is_ge))
            link(nc.vector.reduce_sum(jobf[:, :], cmpj[:, :, :], AX))
            nc.vector.tensor_scalar(end_i[:, :], ends[:, :], float(FB), 1.0, ALU.mult, ALU.add)
            link(nc.vector.tensor_scalar(job_e[:, :], jobf[:, :], float(EXPERTS - 1), None, ALU.min))
            nc.vector.memset(zero1[:, :], 0.0).then_inc(jobs_ready, 1)
            dve.wait_ge(gexp_done, 1)
            link(nc.vector.tensor_scalar(gs[:, :], ge[:, :], 1.0, None, ALU.add))
            link(nc.vector.reciprocal(gp[:, :, 0], gs[:, :]))
            link(nc.vector.tensor_tensor(gp[:, :, 1], ge[:, :], gp[:, :, 0], ALU.mult))
            for k in range(TOPK):
                last = nc.vector.tensor_tensor(prod[:, :, k, :], hot[:, :, k, :],
                                               gp[:, :, k:k + 1].to_broadcast(te), ALU.mult)
            link(last)
            nc.vector.tensor_tensor(pe_all[:, :, :], prod[:, :, 0, :], prod[:, :, 1, :], ALU.add).then_inc(pw_ready, 1)
            dve.wait_ge(pw_full, 1)
            for i in range(2):
                last = nc.vector.tensor_copy(pT8[:, 4 * i:4 * i + 4, :].rearrange("e t n -> e (t n)"), bank[2 + i][0:EXPERTS, :])
            last.then_inc(pw_out, 1)
            dve.wait_ge(rows_in, 48)
            for t in range(GROUPS):
                last = nc.vector.tensor_tensor(x_all[:, t, :], x_all[:, t, :], lnrow[:, 1, :], ALU.add)
            last.then_inc(xb_done, 1)

            def bias(j, fb, slot):
                dve.wait_ge(h_full, FB * j + fb + 1)
                if fb >= 2 or not isinstance(j, int) or j > 0:
                    dve.wait_ge(hT_full, FB * j + fb - 1)
                nc.vector.tensor_tensor(h_sb[:, fb % 2, :], bank[fb % 2][:, :],
                                        b1_rows[:, bass.ds(slot * FF + fb * 512, 512)], ALU.add).then_inc(h_biased, 1)

            def hT_copy(j, fb):
                dve.wait_ge(hT_full, FB * j + fb + 1)
                if fb >= 2 or not isinstance(j, int) or j > 0:
                    dve.wait_ge(mm2_done, 1 + FB * j + fb - 1)
                nc.vector.tensor_copy(hT_sb[:, fb % 2, :, :].rearrange("p c t -> p (c t)"), bank[2 + fb % 2][:, :]).then_inc(hT_out, 1)

            def y_copy(j):
                dve.wait_ge(mm2_done, 1 + FB * (j + 1))
                if not isinstance(j, int) or j > 0:
                    dve.wait_ge(ys_stored, 16 * j)
                nc.vector.tensor_copy(ys, Y[:, :]).then_inc(ys_out, 1)

            def job(j, first):
                slot = dve.value_load(job_e[0:1, bass.ds(j, 1)], min_val=0, max_val=EXPERTS - 1) % 2
                bias(j, 0, slot)
                if not first:
                    hT_copy(j - 1, 3)
                bias(j, 1, slot)
                hT_copy(j, 0)
                if not first:
                    y_copy(j - 1)
                bias(j, 2, slot)
                hT_copy(j, 1)
                bias(j, 3, slot)
                hT_copy(j, 2)

            job(0, True)
            job(1, False)
            with dve.Fori(2, JOBS) as j:
                job(j, False)
            hT_copy(JOBS - 1, 3)
            y_copy(JOBS - 1)

            dve.wait_ge(xb_done, 1)
            link = chain(dve, fin_step, 0)
            for t in range(GROUPS):
                f = fin[:, t, :]
                dve.wait_ge(gathered[t], 16 * TOPK)
                dve.wait_ge(b2_full, t + 1)
                nc.vector.scalar_tensor_tensor(out=f, in0=got[:, t, 0, :], scalar=gp[:, t, 0:1], in1=bank[t % 4][:, :],
                                               op0=ALU.mult, op1=ALU.add).then_inc(b2_used, 1)
                dve.wait_ge(b2_used, t + 1)
                link(nc.vector.scalar_tensor_tensor(out=f, in0=got[:, t, 1, :], scalar=gp[:, t, 1:2], in1=f,
                                                    op0=ALU.mult, op1=ALU.add))
                link(nc.vector.bn_stats(stats[:, :], f))
                link(nc.vector.bn_aggr(mv[:, :], stats[:, :]))
                nc.vector.tensor_scalar(mv[:, 1:2], mv[:, 1:2], EPS, None, ALU.add).then_inc(fin_var, 1)
                link(nc.vector.scalar_tensor_tensor(out=f, in0=f, scalar=mv[:, 0:1], in1=lnrow[:, 0, :],
                                                    op0=ALU.subtract, op1=ALU.mult))
                dve.wait_ge(fin_rstd, t + 1)
                nc.vector.scalar_tensor_tensor(out=f, in0=f, scalar=rstd[:, 0:1], in1=x_all[:, t, :],
                                               op0=ALU.mult, op1=ALU.add).then_inc(fin_done, 1)

        def moe_pe(pe):
            pe.wait_ge(mask_done, 1)
            m2 = mask[:, :, :].rearrange("p t e -> p (t e)")
            nc.tensor.matmul(bank[0][:, 0:GROUPS * EXPERTS], before[:, :], m2, start=True, stop=True).then_inc(mm2_done, 1)
            nc.tensor.matmul(bank[1][:, 0:GROUPS * EXPERTS], ones[:, :], m2, start=True, stop=True).then_inc(ranks_full, 1)
            pe.wait_ge(pw_ready, 1)
            for t in range(GROUPS):
                last = nc.tensor.transpose(bank[2 + t // 4][0:EXPERTS, (t % 4) * P:(t % 4 + 1) * P], pe_all[:, t, :], ident[:, :])
            last.then_inc(pw_full, 1)
            pe.wait_ge(pw_out, 1)

            def xt_fill(j):
                pe.wait_ge(xs_in, 16 * (j + 1))
                if not isinstance(j, int) or j > 0:
                    pe.wait_ge(xt_out, j)
                for c in range(KD):
                    last = nc.tensor.transpose(XT[:, c * P:(c + 1) * P], xs[:, c * P:(c + 1) * P], ident[:, :])
                last.then_inc(xt_full, 1)

            def mm1(j, fb, e):
                if fb == 0:
                    pe.wait_ge(xt_out, j + 1)
                    pe.wait_ge(experts_in, e + 1)
                if fb >= 2 or not isinstance(j, int) or j > 0:
                    pe.wait_ge(h_biased, FB * j + fb - 1)
                for k in range(KD):
                    last = nc.tensor.matmul(bank[fb % 2][:, :], xsT[:, k, :],
                                            moe_flat[:, bass.ds((e % 2) * 16384 + k * FF + fb * 512, 512)],
                                            start=(k == 0), stop=(k == KD - 1))
                last.then_inc(h_full, 1)

            def hT_fill(j, fb):
                pe.wait_ge(h_act, FB * j + fb + 1)
                if fb >= 2 or not isinstance(j, int) or j > 0:
                    pe.wait_ge(hT_out, FB * j + fb - 1)
                for c in range(4):
                    last = nc.tensor.transpose(bank[2 + fb % 2][:, c * P:(c + 1) * P], h_sb[:, fb % 2, c * P:(c + 1) * P], ident[:, :])
                last.then_inc(hT_full, 1)

            def mm2(j, fb, e):
                pe.wait_ge(hT_out, FB * j + fb + 1)
                if fb == 0 and (not isinstance(j, int) or j > 0):
                    pe.wait_ge(ys_out, j)
                for c in range(4):
                    last = nc.tensor.matmul(Y[:, :], hT_sb[:, fb % 2, c, :],
                                            moe_flat[:, bass.ds((e % 2) * 16384 + 8192 + (4 * fb + c) * DIM, DIM)],
                                            start=(fb == 0 and c == 0), stop=(fb == 3 and c == 3))
                last.then_inc(mm2_done, 1)

            def job(j, first, last):
                e = pe.value_load(job_e[0:1, bass.ds(j, 1)], min_val=0, max_val=EXPERTS - 1)
                mm1(j, 0, e)
                if not first:
                    before_e = pe.value_load(job_e[0:1, bass.ds(j - 1, 1)], min_val=0, max_val=EXPERTS - 1)
                    hT_fill(j - 1, 3)
                    mm2(j - 1, 2, before_e)
                mm1(j, 1, e)
                hT_fill(j, 0)
                if not first:
                    mm2(j - 1, 3, before_e)
                mm1(j, 2, e)
                hT_fill(j, 1)
                mm2(j, 0, e)
                mm1(j, 3, e)
                if not last:
                    xt_fill(j + 1)
                hT_fill(j, 2)
                mm2(j, 1, e)
                return e

            pe.wait_ge(jobs_ready, 1)
            xt_fill(0)
            job(0, True, False)
            with pe.Fori(1, JOBS - 1) as j:
                job(j, False, False)
            e = job(JOBS - 1, False, True)
            hT_fill(JOBS - 1, 3)
            mm2(JOBS - 1, 2, e)
            mm2(JOBS - 1, 3, e)
            pe.wait_ge(rows_in, 48)
            pe.wait_ge(h_biased, FB * JOBS)
            pe.wait_ge(hT_out, FB * JOBS)
            for t in range(GROUPS):
                if t >= 4:
                    pe.wait_ge(b2_used, t - 3)
                nc.tensor.matmul(bank[t % 4][:, :], pT8[:, t, :], b2_sb[:, :], start=True, stop=True).then_inc(b2_full, 1)

        def ctx_load(sp, g, b):
            row = (g * GB + b) * KEYS
            sp.dma_start(ctx[0:85, b, :, :].rearrange("p k c -> p (k c)"),
                         ctx_rows[bass.ds(row, 255), :].rearrange("(p k) c -> p (k c)", k=3)).then_inc(ctx_in[b], 16)
            sp.dma_start(ctx[85:86, b, 0:2, :].rearrange("p k c -> p (k c)"),
                         ctx_rows[bass.ds(row + 255, 2), :].rearrange("(p k) c -> p (k c)", k=2)).then_inc(ctx_in[b], 16)

        @block.sync
        def _(sp):
            sp.dma_start(x_all[:, 0, :], x_rows[0:P, :]).then_inc(x0_in, 16)
            ctx_load(sp, 0, 0)
            sp.dma_start(wk_rows, Wk.rearrange("(c p) n -> p c n", p=P)).then_inc(wk_in, 16)
            sp.dma_start(wq, Wq.rearrange("(c p) n -> p c n", p=P)).then_inc(wq_in, 16)
            sp.dma_start(x_all[:, 1:GROUPS, :],
                         x_rows[P:, :].rearrange("(g p) d -> p g d", p=P)).then_inc(x_in, 16)
            for b in range(1, GB):
                ctx_load(sp, 0, b)
            sp.dma_start(wv, Wv.rearrange("(c p) n -> p c n", p=P)).then_inc(wv_in, 16)
            sp.dma_start(wo, Wo.rearrange("(m p) n -> p m n", p=P)).then_inc(wo_in, 16)
            with sp.Fori(1, GROUPS) as g:
                for b in range(GB):
                    sp.wait_ge(m_full, M_FILLS * (g - 1) + UT_AT + 3 * b + 3)
                    ctx_load(sp, g, b)
            moe_loads(sp)

        @block.gpsimd
        def _(pool):
            nc.gpsimd.memset(ones[:, :], 1.0).then_inc(memset_ok, 1)
            nc.gpsimd.memset(half[:, :], -0.5).then_inc(memset_ok, 1)
            pool.wait_ge(memset_ok, 2)
            nc.gpsimd.affine_select(out=ident[:, :], in_=ones[:, :], compare_op=ALU.is_equal, fill=0.0, base=0,
                                    pattern=[[-1, P]], channel_multiplier=1).then_inc(ident_ok, 1)
            nc.gpsimd.affine_select(out=before[:, :], in_=ones[:, :], compare_op=ALU.is_gt, fill=0.0, base=0,
                                    pattern=[[1, P]], channel_multiplier=-1).then_inc(consts, 1)
            nc.gpsimd.iota(iota_e[:, :], pattern=[[1, EXPERTS]], base=0, channel_multiplier=0,
                           allow_small_or_imprecise_dtypes=True).then_inc(consts, 1)
            nc.gpsimd.iota(iota_q[:, :], pattern=[[P, 8]], base=0, channel_multiplier=0,
                           allow_small_or_imprecise_dtypes=True).then_inc(consts, 1)
            nc.gpsimd.iota(iota_j[:, :], pattern=[[1, 24]], base=0, channel_multiplier=0,
                           allow_small_or_imprecise_dtypes=True).then_inc(consts, 1)

            def ln_pow(n):
                pool.wait_ge(ln_var, n + 1)
                nc.gpsimd.tensor_tensor(rstd[:, :], mv[:, 1:2], half[:, 0:1], ALU.pow).then_inc(ln_rstd, 1)

            def cn_pow(n):
                pool.wait_ge(cn_var, n + 1)
                nc.gpsimd.tensor_tensor(crstd[0:86, :], cmv[0:86, :, 1], half[0:86, 0:3], ALU.pow).then_inc(cn_rstd, 1)

            def body(g, do_a, do_b, nxt):
                ln = 2 * g + 2 + 2 * (g - 1)
                if isinstance(g, int) and g == 0:
                    ln = 2
                if do_b:
                    ln_pow(ln)
                    ln = ln + 1
                if do_a:
                    cn_pow(GB * g + 2)
                    cn_pow(GB * g + 3)
                if nxt:
                    ln_pow(ln)
                    ln_pow(ln + 1)
                    ln = ln + 2
                    cn_pow(GB * g + 4)
                    cn_pow(GB * g + 5)
                if do_b:
                    ln_pow(ln)

            ln_pow(0)
            ln_pow(1)
            cn_pow(0)
            cn_pow(1)
            body(0, True, False, True)
            with pool.Fori(1, GROUPS - 1) as g:
                body(g, True, True, True)
            body(GROUPS - 1, True, True, False)
            body_8_ln = 2 * GROUPS + 2 * (GROUPS - 1)
            pool.wait_ge(m_full, M_FILLS * GROUPS)
            expert_load(pool, 0, 0, w_even)
            ln_pow(body_8_ln)
            pool.wait_ge(b_full, B_FILLS * (GROUPS - 1) + KQ_AT + 1)
            expert_load(pool, 1, 1, w_odd)
            ln_pow(body_8_ln + 1)
            moe_pool(pool)

        def setup_out(eng, copy, n):
            dst = (wkT[:, n, :] if n < 8 else wqkvT[:, n - 8, :] if n < 12 else wosT[:, n - 12, :])
            eng.wait_ge(setup_full, n + 1)
            copy(dst, bank[n % 4][:, 0:dst.shape[1]]).then_inc(setup_free[n % 2], 1)

        @block.scalar
        def _(act):
            act.dma_start(qkv_rows, W_qkv.rearrange("(c p) n -> p c n", p=P)).then_inc(qkv_in, 16)
            act.dma_start(wos_rows, W_o.rearrange("(c p) n -> p c n", p=P)).then_inc(wos_in, 16)
            act.dma_start(gate[:, :, :], gate_w.rearrange("(c p) e -> p c e", p=P)).then_inc(gate_in, 16)
            act.dma_start(gate_bias[:, :], gate_b.rearrange("(o e) -> o e", o=1).to_broadcast([P, EXPERTS])).then_inc(gate_in, 16)
            with nc.allow_non_contiguous_dma(reason="a few columns"):
                act.dma_start(gcol[:, 0, :], g_x.rearrange("(c p) -> p c", p=P)).then_inc(cols_in, 16)
                act.dma_start(gcol[:, 1, :], b_x.rearrange("(c p) -> p c", p=P)).then_inc(cols_in, 16)
                act.dma_start(ccol[:, 0, :], g_c.rearrange("(c p) -> p c", p=P)).then_inc(cols_in, 16)
                act.dma_start(ccol[:, 1, :], b_c.rearrange("(c p) -> p c", p=P)).then_inc(cols_in, 16)
            act.wait_ge(zeros_ok, 1)
            for j in range(JOBS):
                act.dma_start(xs_dram[j * P:(j + 1) * P, :],
                              blocks[:, 0:4, :].rearrange("p h t -> p (h t)")).then_inc(xs_zeroed, 16)

            act.wait_ge(cols_in, 64)

            def xn_out(n):
                act.wait_ge(tp_full, n + 1)
                for c in range(KD):
                    last = nc.scalar.activation(xnT[:, c, :], TP[:, c * P:(c + 1) * P], ACT.Identity,
                                                bias=gcol[:, 1, c:c + 1], scale=gcol[:, 0, c:c + 1])
                last.then_inc(tp_free, 1)

            def ct_out(n, b, c):
                act.wait_ge(tp_full, n + 1)
                nc.scalar.activation(cnT[:, b % 2, c, :], TP[:, 0:KEYS], ACT.Identity,
                                     bias=ccol[:, 1, c:c + 1], scale=ccol[:, 0, c:c + 1]).then_inc(tp_free, 1)

            def m_copy(g, at, dst, src):
                act.wait_ge(m_full, M_FILLS * g + at + 1)
                nc.scalar.copy(dst, src).then_inc(m_free[at % 2], 1)

            def exps(g, b):
                bt = GB * g + b
                act.wait_ge(neg_done, bt + 1)
                for h in range(HG):
                    nc.scalar.activation(probs[:, h, :], bank[h][:, 0:KEYS], ACT.Exp, bias=negm[:, h:h + 1],
                                         scale=XSCALE, accum_out=rsum[:, h:h + 1]).then_inc(exp_done, 1)

            def ut_out(g, b, c):
                at = UT_AT + 3 * b + c
                act.wait_ge(m_full, M_FILLS * g + at + 1)
                nc.scalar.activation(uT[:, c, :, b, :], M[at % 2][:, :].rearrange("p (h t) -> p h t", t=TOK), ACT.Identity,
                                     bias=ccol[:, 1, c:c + 1], scale=ccol[:, 0, c:c + 1]).then_inc(m_free[at % 2], 1)

            def b_copy(g, at, dst):
                act.wait_ge(b_full, B_FILLS * g + at + 1)
                nc.scalar.copy(dst, BK[:, :]).then_inc(b_free, 1)

            def body(g, do_a, do_b, nxt):
                if do_a:
                    m_copy(g, QT_AT + 1, qT[:, 4:8, :].rearrange("p m t -> p (m t)"), M[1][:, :])
                for n in range(0, 6):
                    if do_a:
                        c, hq = n // 2, n % 2
                        dst = qkT[:, c, :, :].rearrange("p b (h two t) -> p h two b t", two=2, t=TOK)[:, 4 * hq:4 * hq + 4, 1]
                        m_copy(g, QK_AT + 2 * n + 1, dst, M[1][:, :].rearrange("p (h b t) -> p h b t", h=4, b=GB))
                    if n == 3 and do_b:
                        b_copy(g - 1, KQ_AT, kqT[:, :, :].rearrange("p c t -> p (c t)"))
                if do_b:
                    b_copy(g - 1, V_AT, v_sb[:, :])
                for b in range(GB + 1):
                    if do_a:
                        if b == 0:
                            for c in range(KC):
                                ct_out(tp(g, ("ct", 1, c)), 1, c)
                        if b < GB:
                            exps(g, b)
                        for c in range(KC):
                            if b >= 1:
                                ut_out(g, b - 1, c)
                            if 1 <= b < 3 or (b == GB and nxt):
                                nb = b + 1 if b < GB else GB
                                ct_out(tp(g, ("ct", nb, c)), nb, c)
                    if do_b and b == 2:
                        act.wait_ge(ss_ready, g)
                        nc.scalar.activation(sS[:, :, :], sS[:, :, :], ACT.Exp, scale=SSCALE).then_inc(sexp_done, 1)
                    if do_b and b == 3:
                        b_copy(g - 1, PV_AT, kqT[:, :, :].rearrange("p c t -> p (c t)"))
                if nxt:
                    xn_out(tp(g, "xn"))
                if do_a:
                    m_copy(g, O_AT + 1, oT[:, 4:8, :].rearrange("p m t -> p (m t)"), M[1][:, :])

            xn_out(0)
            for c in range(KC):
                ct_out(1 + c, 0, c)
            for n in range(1, 16, 2):
                setup_out(act, nc.scalar.copy, n)
            body(0, True, False, True)
            with act.Fori(1, GROUPS - 1) as g:
                body(g, True, True, True)
            body(GROUPS - 1, True, True, False)
            body(GROUPS, False, True, False)
            moe_act(act)

        @block.vector
        def _(dve):
            nc.vector.memset(blocks[:, :, :], 0.0).then_inc(zeros_ok, 1)
            nc.vector.memset(cmv[:, :, :], 1.0).then_inc(cmv_ok, 1)
            nc.vector.memset(dve_mark[:, :], 0.0).then_inc(b_free, 1)
            dve.wait_ge(cmv_ok, 1)

            def carry_wait():
                nc.vector.memset(zero1[:, :], 0.0)

            def layernorm(n, src, dst, done):
                link = chain(dve, ln_step, 2 * n)
                carry_wait()
                link(nc.vector.bn_stats(stats[:, :], src))
                carry_wait()
                link(nc.vector.bn_aggr(mv[:, :], stats[:, :]))
                nc.vector.tensor_scalar(mv[:, 1:2], mv[:, 1:2], EPS, None, ALU.add).then_inc(ln_var, 1)
                dve.wait_ge(ln_rstd, n + 1)
                nc.vector.tensor_scalar(dst, src, mv[:, 0:1], rstd[:, 0:1], ALU.subtract, ALU.mult).then_inc(done, 1)

            def xn_norm(n, g):
                layernorm(n, x_all[:, bass.ds(g, 1), :].rearrange("p g d -> p (g d)"), xn, xn_done)
                dve.wait_ge(xn_done, 2 * g + 1)
                layernorm(n + 1, xn, xn, xn_done)

            def cn_norm(g, b):
                bt, slot = GB * g + b, b % GB
                dve.wait_ge(ctx_in[slot], 32 * (g + b // GB + 1))
                for k in range(3):
                    last = nc.vector.bn_stats(cstats[0:PART[k], k, :], ctx[0:PART[k], slot, k, :])
                link = chain(dve, cn_step, 2 * bt)
                link(last)
                carry_wait()
                for k in range(3):
                    last = nc.vector.bn_aggr(cmv[0:PART[k], k, :], cstats[0:PART[k], k, :])
                link(last)
                nc.vector.tensor_scalar(cmv[0:86, :, 1], cmv[0:86, :, 1], EPS, None, ALU.add).then_inc(cn_var, 1)
                dve.wait_ge(cn_rstd, bt + 1)
                for k in range(3):
                    c = ctx[0:PART[k], slot, k, :]
                    last = nc.vector.tensor_scalar(c, c, cmv[0:PART[k], k, 0:1], crstd[0:PART[k], k:k + 1],
                                                   ALU.subtract, ALU.mult)
                last.then_inc(cn_done, 1)

            def m_copy(g, at, dst, src):
                dve.wait_ge(m_full, M_FILLS * g + at + 1)
                nc.vector.tensor_copy(dst, src).then_inc(m_free[at % 2], 1)

            def b_copy(g, at, dst, src=BK[:, :]):
                dve.wait_ge(b_full, B_FILLS * g + at + 1)
                nc.vector.tensor_copy(dst, src).then_inc(b_free, 1)

            def row_max(g, b, h):
                n = HG * (GB * g + b) + h
                dve.wait_ge(s_full, n + 1)
                nc.vector.reduce_max(mx[:, h:h + 1], bank[h][:, 0:KEYS], AX).then_inc(max_done, 1)

            def neg_max(g, b):
                bt = GB * g + b
                dve.wait_ge(max_done, HG * (bt + 1))
                nc.vector.tensor_scalar(negm[:, :], mx[:, :], -XSCALE, None, ALU.mult).then_inc(neg_done, 1)

            def norm_probs(g, b):
                bt = GB * g + b
                dve.wait_ge(exp_done, HG * (bt + 1))
                nc.vector.reciprocal(rinv[:, :], rsum[:, :]).then_inc(rinv_done, 1)
                dve.wait_ge(rinv_done, bt + 1)
                for h in range(HG):
                    last = nc.vector.tensor_scalar(probs[:, h, :], probs[:, h, :], rinv[:, h:h + 1], None, ALU.mult)
                last.then_inc(norm_done, 1)

            def pt_out(g, b, k):
                dve.wait_ge(tp_full, tp(g, ("pt", b, k)) + 1)
                nc.vector.tensor_copy(pT[0:PART[k], k, :], TP[0:PART[k], :]).then_inc(tp_free, 1)

            def ss_out(g, hh):
                dve.wait_ge(b_full, B_FILLS * g + SS_AT + hh + 1)
                for q in range(GB):
                    rows = slice(TOK * q, TOK * (q + 1))
                    last = nc.vector.tensor_copy(
                        sS[rows, :, :].rearrange("p (m h) j -> p m h j", h=4)[:, :, hh, :],
                        BK[rows, :].rearrange("p (m j) -> p m j", m=4)[:, :, TOK * q:TOK * (q + 1)])
                last.then_inc(b_free, 1)

            def ss_sub(g):
                dve.wait_ge(b_free, 1 + B_FILLS * g + SS_AT + 4)
                link = chain(dve, ss_step, 4 * g)
                link(nc.vector.tensor_reduce(smx[:, :], sS[:, :, :], AX, ALU.max))
                nc.vector.tensor_tensor(sS[:, :, :], sS[:, :, :], smx[:, :].unsqueeze(2).to_broadcast([P, SHEADS, TOK]),
                                        ALU.subtract).then_inc(ss_ready, 1)

            def ss_norm(g):
                dve.wait_ge(sexp_done, g + 1)
                link = chain(dve, ss_step, 4 * g + 1)
                link(nc.vector.reduce_sum(ssum[:, :], sS[:, :, :], AX))
                link(nc.vector.reciprocal(ssum[:, :], ssum[:, :]))
                link(nc.vector.tensor_tensor(sS[:, :, :], sS[:, :, :], ssum[:, :].unsqueeze(2).to_broadcast([P, SHEADS, TOK]),
                                             ALU.mult))
                for q in range(GB):
                    rows = slice(TOK * q, TOK * (q + 1))
                    last = nc.vector.transpose(blocks[rows, :, TOK * q:TOK * (q + 1)], sS[rows, :, :])
                last.then_inc(wb_done, 1)

            def body(g, do_a, do_b, nxt):
                ln = 2 * g + 2 + 2 * (g - 1)
                if isinstance(g, int) and g == 0:
                    ln = 2
                if isinstance(g, int) and g == GROUPS:
                    ln = 2 * GROUPS + 2 * (GROUPS - 1)
                x_prev = x_all[:, bass.ds(g - 1, 1), :].rearrange("p g d -> p (g d)") if do_b else None
                if do_b:
                    for i in range(2):
                        dve.wait_ge(m_free[i], (M_FILLS // 2) * g)
                    layernorm(ln, x_prev, y[:, :], y_done)
                    ln = ln + 1
                if do_a:
                    m_copy(g, QT_AT, qT[:, 0:4, :].rearrange("p m t -> p (m t)"), M[0][:, :])
                for n in range(0, 6):
                    if do_a:
                        c, hq = n // 2, n % 2
                        dst = qkT[:, c, :, :].rearrange("p b (h two t) -> p h two b t", two=2, t=TOK)[:, 4 * hq:4 * hq + 4, 0]
                        m_copy(g, QK_AT + 2 * n, dst, M[0][:, :].rearrange("p (h b t) -> p h b t", h=4, b=GB))
                    if n == 1 and do_b:
                        b_copy(g - 1, YT_AT, yT[:, :, :].rearrange("p c t -> p (c t)"))
                for b in range(GB + 1):
                    for k in range(3):
                        if do_a:
                            if b >= 1:
                                pt_out(g, b - 1, k)
                            if b < GB:
                                row_max(g, b, k)
                        if do_b and b == GB and k == 0:
                            dve.wait_ge(b_full, B_FILLS * (g - 1) + WS_AT + 1)
                            nc.vector.tensor_tensor(x_prev, x_prev, BK[:, :], ALU.add).then_inc(b_free, 1)
                    if do_a and b < GB:
                        row_max(g, b, 3)
                        neg_max(g, b)
                    if do_b and b == 0:
                        ss_out(g - 1, 0)
                    if do_b and b == 2:
                        ss_out(g - 1, 3)
                    if do_a and b < GB:
                        norm_probs(g, b)
                    if b == 0 and do_a:
                        cn_norm(g, 2)
                    if b == 1:
                        if do_b:
                            ss_out(g - 1, 1)
                            ss_out(g - 1, 2)
                        if do_a:
                            cn_norm(g, 3)
                        if nxt:
                            xn_norm(ln, g + 1)
                            ln = ln + 2
                    if b == 2:
                        if do_b:
                            ss_sub(g - 1)
                        if nxt:
                            cn_norm(g, 4)
                    if b == 3:
                        if do_b:
                            ss_norm(g - 1)
                        if nxt:
                            cn_norm(g, 5)
                    if b == GB and do_b:
                        dve.wait_ge(b_free, 1 + B_FILLS * (g - 1) + WS_AT + 1)
                        layernorm(ln, x_prev, y[:, :], y_done)
                        kept = y2mv[:, bass.ds(g - 1, 1), :].rearrange("p g s -> p (g s)")
                        nc.vector.tensor_copy(kept[:, 0:1], mv[:, 0:1])
                        nc.vector.tensor_copy(kept[:, 1:2], rstd[:, :]).then_inc(kept_done, 1)
                        b_copy(g - 1, YT2_AT, yT[:, :, :].rearrange("p c t -> p (c t)"))
                if do_a:
                    m_copy(g, O_AT, oT[:, 0:4, :].rearrange("p m t -> p (m t)"), M[0][:, :])
                if do_b:
                    dve.wait_ge(b_full, B_FILLS * (g - 1) + LG_AT + 1)
                    nc.vector.tensor_tensor(logits[:, bass.ds(g - 1, 1), :].rearrange("p g e -> p (g e)"), BK[:, 0:EXPERTS],
                                            gate_bias[:, :], ALU.add).then_inc(b_free, 1)
                if do_a:
                    for j in range(2):
                        dve.wait_ge(m_full, M_FILLS * g + WO_AT + j + 1)
                        x_now = x_all[:, bass.ds(g, 1), j * 256:(j + 1) * 256].rearrange("p g d -> p (g d)")
                        nc.vector.tensor_tensor(x_now, x_now, M[j][:, 0:256], ALU.add).then_inc(m_free[j], 1)

            dve.wait_ge(x0_in, 16)
            xn_norm(0, 0)
            cn_norm(0, 0)
            for n in range(0, 16, 2):
                setup_out(dve, nc.vector.tensor_copy, n)
            cn_norm(0, 1)
            dve.wait_ge(x_in, 16)
            body(0, True, False, True)
            dve.wait_ge(gate_in, 32)
            dve.wait_ge(xs_zeroed, 16 * JOBS)
            with dve.Fori(1, GROUPS - 1) as g:
                body(g, True, True, True)
            body(GROUPS - 1, True, True, False)
            body(GROUPS, False, True, False)
            moe_dve(dve)

        @block.tensor
        def _(pe):
            def setup_fill(n):
                if n >= 4:
                    pe.wait_ge(setup_free[n % 2], (n - 4) // 2 + 1)
                if n < 8:
                    for c in range(KC):
                        last = nc.tensor.transpose(bank[n % 4][:, c * P:(c + 1) * P], wk_rows[:, c, n * P:(n + 1) * P], ident[:, :])
                else:
                    rows, m = (qkv_rows, n - 8) if n < 12 else (wos_rows, n - 12)
                    for c in range(KD):
                        last = nc.tensor.transpose(bank[n % 4][:, c * P:(c + 1) * P], rows[:, c, m * P:(m + 1) * P], ident[:, :])
                last.then_inc(setup_full, 1)

            def m_open(g, at):
                at_least(pe, m_free[at % 2], (M_FILLS // 2) * g + at // 2)
                return M[at % 2]

            def m_ready(g, at):
                pe.wait_ge(m_free[at % 2], (M_FILLS // 2) * g + at // 2 + 1)

            def b_open(g, at):
                pe.wait_ge(b_free, 1 + B_FILLS * g + at)

            def q_proj(g, i):
                ps = m_open(g, QT_AT + i)
                for m in range(4):
                    for k in range(KD):
                        last = nc.tensor.matmul(ps[:, m * P:(m + 1) * P], wq[:, k, (4 * i + m) * P:(4 * i + m + 1) * P],
                                                xnT[:, k, :], start=(k == 0), stop=(k == KD - 1))
                last.then_inc(m_full, 1)

            def qk_proj(g, n):
                c, hq = n // 2, n % 2
                for par in range(2):
                    m_open(g, QK_AT + 2 * n + par)
                if n == 0:
                    m_ready(g, QT_AT)
                    m_ready(g, QT_AT + 1)
                for s in range(4):
                    for par in range(2):
                        rows = slice(HDIM * par, HDIM * (par + 1))
                        last = nc.tensor.matmul(M[par][:, s * P:(s + 1) * P], wkT[rows, 4 * hq + s, c * P:(c + 1) * P],
                                                qT[rows, 4 * hq + s, :], start=True, stop=True)
                        if s == 3:
                            last.then_inc(m_full, 1)

            def scores(g, b, h):
                bt = GB * g + b
                if h == 0:
                    at_least(pe, tp_free, (TP_FIRST + TP_FILLS * g) if b == 0 else tp(g, ("ct", b, 2)) + 1)
                    if b == 0:
                        m_ready(g, QK_AT + 10)
                        m_ready(g, QK_AT + 11)
                at_least(pe, exp_done, HG * (bt - 1) + h + 1 if not isinstance(bt, int) or bt > 0 else 0)
                for c in range(KC):
                    last = nc.tensor.matmul(bank[h][:, 0:KEYS], qkT[:, c, b, h * P:(h + 1) * P], cnT[:, b % 2, c, :],
                                            start=(c == 0), stop=(c == KC - 1))
                last.then_inc(s_full, 1)

            def ct_fill(n, bt, b, c):
                pe.wait_ge(tp_free, n)
                if c == 0:
                    pe.wait_ge(cn_done, bt + 1)
                for k in range(3):
                    last = nc.tensor.transpose(TP[:, KOFF[k]:KOFF[k] + PART[k]], ctx[0:PART[k], b % GB, k, c * P:(c + 1) * P],
                                               ident[0:PART[k], 0:PART[k]])
                last.then_inc(tp_full, 1)

            def pt_fill(g, b, k):
                pe.wait_ge(tp_free, tp(g, ("pt", b, k)))
                if k == 0:
                    pe.wait_ge(norm_done, GB * g + b + 1)
                for h in range(HG):
                    last = nc.tensor.transpose(TP[0:PART[k], h * P:(h + 1) * P], probs[:, h, KOFF[k]:KOFF[k] + PART[k]], ident[:, :])
                last.then_inc(tp_full, 1)

            def av(g, b, c):
                at = UT_AT + 3 * b + c
                ps = m_open(g, at)
                if c == 0:
                    pe.wait_ge(tp_free, tp(g, ("pt", b, 2)) + 1)
                for k in range(3):
                    last = nc.tensor.matmul(ps[:, :], ctx[0:PART[k], b, k, c * P:(c + 1) * P], pT[0:PART[k], k, :],
                                            start=(k == 0), stop=(k == 2))
                last.then_inc(m_full, 1)

            def o_proj(g, i):
                ps = m_open(g, O_AT + i)
                if i == 0:
                    m_ready(g, UT_AT + 10)
                    m_ready(g, UT_AT + 11)
                for s in range(4):
                    for par in range(2):
                        h = 2 * (4 * i + s) + par
                        for c in range(KC):
                            last = nc.tensor.matmul(ps[HDIM * par:HDIM * (par + 1), s * P:(s + 1) * P],
                                                    wv[:, c, h * HDIM:(h + 1) * HDIM],
                                                    uT[:, c, h, :, :].rearrange("p b t -> p (b t)"),
                                                    start=(c == 0), stop=(c == KC - 1))
                last.then_inc(m_full, 1)

            def wo_proj(g, j):
                ps = m_open(g, WO_AT + j)
                if j == 0:
                    m_ready(g, O_AT)
                    m_ready(g, O_AT + 1)
                for m in range(KI):
                    last = nc.tensor.matmul(ps[:, 0:256], oT[:, m, :], wo[:, m, j * 256:(j + 1) * 256],
                                            start=(m == 0), stop=(m == KI - 1))
                last.then_inc(m_full, 1)

            def xn_fill(n, count):
                pe.wait_ge(tp_free, n)
                pe.wait_ge(xn_done, count)
                for c in range(KD):
                    last = nc.tensor.transpose(TP[:, c * P:(c + 1) * P], xn[:, c * P:(c + 1) * P], ident[:, :])
                last.then_inc(tp_full, 1)

            def y_fill(g, at, count):
                b_open(g, at)
                pe.wait_ge(y_done, count)
                for c in range(KD):
                    last = nc.tensor.transpose(BK[:, c * P:(c + 1) * P], y[:, c * P:(c + 1) * P], ident[:, :])
                last.then_inc(b_full, 1)

            def kq_fill(g):
                b_open(g, KQ_AT)
                for m in range(KD):
                    for k in range(KD):
                        last = nc.tensor.matmul(BK[:, m * P:(m + 1) * P], wqkvT[:, k, m * P:(m + 1) * P], yT[:, k, :],
                                                start=(k == 0), stop=(k == KD - 1))
                last.then_inc(b_full, 1)

            def v_fill(g):
                b_open(g, V_AT)
                for m in range(KD):
                    last = nc.tensor.transpose(BK[:, m * P:(m + 1) * P], kqT[:, m, :], ident[:, :])
                last.then_inc(b_full, 1)

            def ss_fill(g, hh):
                b_open(g, SS_AT + hh)
                rows = slice(SDIM * hh, SDIM * (hh + 1))
                for m in range(4):
                    last = nc.tensor.matmul(BK[:, m * P:(m + 1) * P], kqT[rows, m, :], kqT[rows, m, :], start=True, stop=True,
                                            tile_position=(SDIM * hh, 0))
                last.then_inc(b_full, 1)

            def pv_fill(g):
                b_open(g, PV_AT)
                pe.wait_ge(wb_done, g + 1)
                for m in range(4):
                    for hh in range(4):
                        h = 4 * m + hh
                        last = nc.tensor.matmul(BK[SDIM * hh:SDIM * (hh + 1), m * P:(m + 1) * P],
                                                v_sb[:, h * SDIM:(h + 1) * SDIM], blocks[:, h, :], start=True, stop=True,
                                                tile_position=(0, SDIM * hh))
                last.then_inc(b_full, 1)

            def ws_fill(g):
                b_open(g, WS_AT)
                for k in range(KD):
                    last = nc.tensor.matmul(BK[:, :], kqT[:, k, :], wosT[:, k, :], start=(k == 0), stop=(k == KD - 1))
                last.then_inc(b_full, 1)

            def lg_fill(g):
                b_open(g, LG_AT)
                for k in range(KD):
                    last = nc.tensor.matmul(BK[:, 0:EXPERTS], yT[:, k, :], gate[:, k, :], start=(k == 0), stop=(k == KD - 1))
                last.then_inc(b_full, 1)

            def body(g, do_a, do_b, nxt):
                if do_a:
                    at_least(pe, tp_free, TP_FIRST + TP_FILLS * g)
                    q_proj(g, 0)
                    q_proj(g, 1)
                for n in range(0, 6):
                    if do_a:
                        qk_proj(g, n)
                    if do_b and n == 1:
                        y_fill(g - 1, YT_AT, 2 * (g - 1) + 1)
                    if do_b and n == 3:
                        kq_fill(g - 1)
                if do_b:
                    v_fill(g - 1)
                for b in range(GB + 1):
                    for h in range(HG):
                        if do_a:
                            if b < GB:
                                scores(g, b, h)
                            if b == 0 and h < 3:
                                ct_fill(tp(g, ("ct", 1, h)), GB * g + 1, 1, h)
                            if b >= 1 and h < 3:
                                pt_fill(g, b - 1, h)
                        if do_b and b == GB and h == 0:
                            ws_fill(g - 1)
                    if do_b and b == 0:
                        ss_fill(g - 1, 0)
                    if do_b and b == 2:
                        ss_fill(g - 1, 3)
                    for c in range(KC):
                        if do_a and b >= 1:
                            av(g, b - 1, c)
                            if 1 <= b < 3 or (b == GB and nxt):
                                nb = b + 1 if b < GB else GB
                                ct_fill(tp(g, ("ct", nb, c)), GB * g + nb, nb, c)
                        if do_b and b == 1 and c < 2:
                            ss_fill(g - 1, 1 + c)
                    if do_b and b == 3:
                        pv_fill(g - 1)
                if nxt:
                    xn_fill(tp(g, "xn"), 2 * (g + 2))
                if do_b:
                    y_fill(g - 1, YT2_AT, 2 * g)
                if do_a:
                    o_proj(g, 0)
                    o_proj(g, 1)
                if do_b:
                    lg_fill(g - 1)
                if do_a:
                    wo_proj(g, 0)
                    wo_proj(g, 1)

            pe.wait_ge(ident_ok, 1)
            xn_fill(0, 2)
            for c in range(KC):
                ct_fill(1 + c, 0, 0, c)
            pe.wait_ge(wk_in, 16)
            for n in range(8):
                setup_fill(n)
            pe.wait_ge(qkv_in, 16)
            pe.wait_ge(wos_in, 16)
            for n in range(8, 16):
                setup_fill(n)
            for i in range(2):
                pe.wait_ge(setup_free[i], 8)
            pe.wait_ge(wq_in, 16)
            pe.wait_ge(wv_in, 16)
            pe.wait_ge(wo_in, 16)
            pe.wait_ge(gate_in, 32)
            body(0, True, False, True)
            with pe.Fori(1, GROUPS - 1) as g:
                body(g, True, True, True)
            body(GROUPS - 1, True, True, False)
            body(GROUPS, False, True, False)
            moe_pe(pe)


_INS = ['x', 'ctx_768', 'L0_xattn_g_x', 'L0_xattn_b_x', 'L0_xattn_g_c', 'L0_xattn_b_c', 'L0_xattn_Wq', 'L0_xattn_Wk',
        'L0_xattn_Wv', 'L0_xattn_Wo', 'L0_attn_W_qkv', 'L0_attn_W_o', 'L0_ffn_gate_w', 'L0_ffn_gate_b', 'L0_ffn_w1',
        'L0_ffn_b1', 'L0_ffn_w2', 'L0_ffn_b2', 'L0_ffn_ln_g', 'L0_ffn_ln_b']


def kernel(**inputs):
    import numpy as _np
    import concourse.bacc as _bacc
    from concourse.bass_utils import run_bass_kernel_spmd as _run

    nc = _bacc.Bacc("TRN2", target_bir_lowering=False, num_devices=1)
    arrays, args = {}, []
    for name in _INS:
        a = _np.ascontiguousarray(inputs[name])
        arrays[f"in_{name}_dram"] = a
        args.append(nc.dram_tensor(f"in_{name}_dram", a.shape, mybir.dt.from_np(a.dtype), kind="ExternalInput").ap())
    out = nc.dram_tensor("out_dram", (BATCH, TOK, DIM), F32, kind="ExternalOutput").ap()
    perceiver_layer(nc, *args, out)
    r = _run(nc, [arrays], core_ids=[0])
    return r.results[0]["out_dram"]
```

```python
from contextlib import ExitStack

import concourse.bass as bass
from concourse import mybir

F32 = mybir.dt.float32
F16 = mybir.dt.float16
I32 = mybir.dt.int32
U32 = mybir.dt.uint32
ALU = mybir.AluOpType
ACT = mybir.ActivationFunctionType
AX = mybir.AxisListType.X

P = 128
BATCH, TOK, DIM = 32, 32, 512
KEYS, CTX = 257, 384
HEADS, HDIM = 16, 64
INNER = HEADS * HDIM
SHEADS, SDIM = 16, 32
EXPERTS, FF, TOPK = 8, 2048, 2
EPS = 1e-5
XSCALE = HDIM ** -0.5
SSCALE = SDIM ** -0.5
TEMP = 0.9
N_SCALE = 2.0 ** 11
P_SCALE = 2.0 ** 14

GB = P // TOK
GROUPS = BATCH // GB
KD = DIM // P
KC = CTX // P
KI = INNER // P
KF = FF // P
HG = HEADS // GB
PART = [86, 86, 85]
KOFF = [0, 86, 172]
FB = FF // 512
JOBS = BATCH * TOK * TOPK // P + EXPERTS - 1

QT_AT, UT_AT, O_AT, WO_AT, M_FILLS = 0, 2, 2 + 4 * GB, 4 + 4 * GB, 6 + 4 * GB
QK_PAIRS = 2 * KC
TP_FIRST, TP_FILLS = 4, 19
TP_AT = {}
for _kind, _b in (("ct", 1), ("pt", 0), ("ct", 2), ("pt", 1), ("ct", 3), ("pt", 2), ("ct", 4)):
    for _k in ((0, 2) if _kind == "pt" else (0, 1, 2)):
        TP_AT[_kind, _b, _k] = len(TP_AT)
TP_AT["xn"] = len(TP_AT)
YT_AT, KQ_AT, V_AT, SS_AT, PV_AT, WS_AT, YT2_AT, LG_AT, B_FILLS = 0, 1, 2, 3, 7, 8, 9, 10, 11


def at_least(eng, sem, n):
    if not isinstance(n, int) or n > 0:
        eng.wait_ge(sem, n)


def chain(eng, sem, before):
    count = [0]

    def link(instruction):
        count[0] += 1
        instruction.then_inc(sem, 1)
        eng.wait_ge(sem, before + count[0])

    return link


def perceiver_layer(nc, x, ctx_768, g_x, b_x, g_c, b_c, Wq, Wk, Wv, Wo, W_qkv, W_o,
                    gate_w, gate_b, w1, b1, w2, b2, ln_g, ln_b, out):
    with ExitStack() as stack:
        def sb(name, shape, dt=F32):
            return stack.enter_context(nc.sbuf_tensor(name, shape, dt))

        def sem(name):
            return stack.enter_context(nc.semaphore(name))

        xs_dram = nc.dram_tensor("xs_rows", (JOBS * P, DIM), F32).ap()
        ys_dram = nc.dram_tensor("ys_rows", (JOBS * P, DIM), F32).ap()

        moe_w = sb("moe_w", [P, 2, KD * FF + KF * DIM])
        moe_flat = moe_w[:, :, :].rearrange("p s n -> p (s n)")
        s0, s1 = moe_w[:, 0, :], moe_w[:, 1, :]
        qkT = s0[:, 0:6144].rearrange("p (c b r) -> p c b r", c=KC, b=GB)
        uT = s0[:, 6144:12288].rearrange("p (c h b t) -> p c h b t", c=KC, h=HEADS, b=GB)
        qT = s0[:, 12288:13312].rearrange("p (m t) -> p m t", m=KI)
        oT = qT
        cnT = s0[:, 13312:13312 + 2 * KC * KEYS].rearrange("p (s c j) -> p s c j", s=2, c=KC)
        n_high = s0[:, 14856:14856 + 3 * CTX].bitcast(F16).rearrange("p (s k c) -> p s k c", s=2, k=3)
        wk_rows = s0[:, 6144:9216].rearrange("p (c n) -> p c n", c=KC)
        qkv_rows = s0[:, 0:2048].rearrange("p (c n) -> p c n", c=KD)
        wos_rows = s0[:, 2048:4096].rearrange("p (c n) -> p c n", c=KD)
        wq = s1[:, 0:4096].rearrange("p (c n) -> p c n", c=KD)
        wkT = s1[:, 4096:7168].rearrange("p (m c) -> p m c", m=KI)
        wv = s1[:, 7168:10240].rearrange("p (c n) -> p c n", c=KC)
        wo = s1[:, 10240:14336].rearrange("p (m n) -> p m n", m=KI)
        wqkvT = s1[:, 14336:16384].rearrange("p (c n) -> p c n", c=KD)

        arena = sb("arena", [P, 8704])
        ctx = arena[:, 0:4608].rearrange("p (s k c) -> p s k c", s=GB, k=3)
        probs = arena[:, 4608:5636].rearrange("p (h j) -> p h j", h=HG)
        n_low = arena[:, 0:4608].bitcast(F16).rearrange("p (s k c) -> p s k c", s=GB, k=3)[:, :, :, 0:CTX]
        pT_high, pT_low = [arena[:, 5636 + 768 * i:5636 + 768 * (i + 1)].bitcast(F16).rearrange("p (k r) -> p k r", k=3)
                           for i in range(2)]
        xn = arena[:, 7172:7684]
        xnT = arena[:, 7684:8196].rearrange("p (c t) -> p c t", c=KD)
        b1_rows = arena[:, 0:4096]
        y_all = arena[:, 4096:8192].rearrange("p (g d) -> p g d", g=GROUPS)
        h_sb = arena[:, 4096:5120].rearrange("p (s f) -> p s f", s=2)
        hT_sb = arena[:, 5120:6144].rearrange("p (s c t) -> p s c t", s=2, c=KD)
        xs = arena[:, 6144:6656]
        xsT = arena[:, 6656:7168].rearrange("p (c t) -> p c t", c=KD)
        ys = arena[:, 7168:7680]

        x_all = sb("x_all", [P, GROUPS, DIM])
        wosT = sb("wosT", [P, KD, DIM])
        y = sb("y", [P, DIM])
        yT = sb("yT", [P, KD, P])
        kqT = sb("kqT", [P, KD, P])
        v_sb = sb("v_sb", [P, DIM])
        sS = sb("sS", [P, SHEADS, TOK])
        blocks = sb("blocks", [P, SHEADS, P])
        ident = sb("ident", [P, P])
        before = sb("before", [P, P])
        ones = sb("ones", [P, P])
        gate = sb("gate", [P, KD, EXPERTS])
        gcol = sb("gcol", [P, 2, KD])
        ccol = sb("ccol", [P, 2, KC])
        ugain = sb("ugain", [P, KC])
        gate_bias = sb("gate_bias", [P, EXPERTS])
        half = sb("half", [P, 8])
        stats = sb("stats", [P, 6])
        mv = sb("mv", [P, 2])
        rstd = sb("rstd", [P, 1])
        y2mv = sb("y2mv", [P, GROUPS, 2])
        cstats = sb("cstats", [P, 3, 6])
        cmv = sb("cmv", [P, 3, 2])
        crstd = sb("crstd", [P, 3])
        mx = sb("mx", [P, HG])
        negm = sb("negm", [P, HG])
        rsum = sb("rsum", [P, HG])
        rinv = sb("rinv", [P, HG])
        smx = sb("smx", [P, SHEADS])
        ssum = sb("ssum", [P, SHEADS])
        logits = sb("logits", [P, GROUPS, EXPERTS])

        late = blocks[:, :, :].rearrange("p h t -> p (h t)")
        late_used = [0]

        def late_f32(*shape):
            at, size = late_used[0], 1
            for n in shape:
                size *= n
            late_used[0] += size
            piece = late[:, at:at + size]
            names = "abc"[:len(shape)]
            return piece.rearrange(f"p ({' '.join(names)}) -> p {' '.join(names)}", **dict(zip(names, shape)))

        top = late_f32(GROUPS, 8)
        topi = sb("topi", [P, GROUPS, 8], U32)
        topf = late_f32(GROUPS, TOPK)
        iota_e = sb("iota_e", [P, EXPERTS])
        iota_q = sb("iota_q", [P, 8])
        iota_j = sb("iota_j", [P, 24])
        hot = late_f32(GROUPS, TOPK, EXPERTS)
        mask = late_f32(GROUPS, EXPERTS)
        rank = late_f32(GROUPS, EXPERTS)
        tot = late_f32(GROUPS + 1, EXPERTS)
        cmp8 = late_f32(EXPERTS, 8)
        tiles = late_f32(EXPERTS)
        ends = late_f32(EXPERTS + 1)
        cmpj = late_f32(24, EXPERTS)
        jobf = late_f32(24)
        job_e = sb("job_e", [P, 24], I32)
        end_i = sb("end_i", [P, EXPERTS + 1], I32)
        prod = late_f32(GROUPS, TOPK, EXPERTS)
        slotf = late_f32(GROUPS, TOPK)
        slots = sb("slots", [P, GROUPS, TOPK], U32)
        gp = late_f32(GROUPS, TOPK)
        ge = late_f32(GROUPS)
        gs = late_f32(GROUPS)
        pe_all = late_f32(GROUPS, EXPERTS)
        zero1 = sb("zero1", [P, 1])
        pool_mark = sb("pool_mark", [P, 1])
        dve_mark = sb("dve_mark", [P, 1])
        pT8 = wosT[0:EXPERTS, 2:4, :].rearrange("e a (b n) -> e (a b) n", n=P)

        got = s0[:, 0:8192].rearrange("p (t k d) -> p t k d", t=GROUPS, k=TOPK)
        fin = s0[:, 8192:12288].rearrange("p (t d) -> p t d", t=GROUPS)
        lnrow = wosT[:, 0:2, :]
        b2_sb = sS[0:EXPERTS, :, :].rearrange("e h t -> e (h t)")

        bank = [stack.enter_context(nc.psum_tensor(f"bank{i}", [P, 512], F32)) for i in range(8)]
        TP, M, BK = bank[4], [bank[5], bank[6]], bank[7]

        x0_in = sem("x0_in")
        x_in, wk_in, wq_in, wv_in, wo_in = sem("x_in"), sem("wk_in"), sem("wq_in"), sem("wv_in"), sem("wo_in")
        qkv_in, wos_in, cols_in, rows_in, gate_in = sem("qkv_in"), sem("wos_in"), sem("cols_in"), sem("rows_in"), sem("gate_in")
        ctx_in = [sem(f"ctx_in{b}") for b in range(GB)]
        xs_zeroed = sem("xs_zeroed")
        consts, ident_ok, zeros_ok, memset_ok = sem("consts"), sem("ident_ok"), sem("zeros_ok"), sem("memset_ok")
        setup_full, setup_free = sem("setup_full"), [sem(f"setup_free{i}") for i in range(2)]
        ln_step, ln_var, ln_rstd = sem("ln_step"), sem("ln_var"), sem("ln_rstd")
        cn_step, cn_var, cn_rstd, cn_done = sem("cn_step"), sem("cn_var"), sem("cn_rstd"), sem("cn_done")
        xn_done, y_done, x1_done, x2_done = sem("xn_done"), sem("y_done"), sem("x1_done"), sem("x2_done")
        tp_full, tp_free = sem("tp_full"), sem("tp_free")
        m_full, m_free = sem("m_full"), [sem(f"m_free{i}") for i in range(2)]
        qk_full, qk_out = sem("qk_full"), [sem(f"qk_out{i}") for i in range(2)]
        pt3_full, pt3_out = sem("pt3_full"), sem("pt3_out")
        n_high_done, n_low_done, p_high_done, ugain_ok = sem("n_high_done"), sem("n_low_done"), sem("p_high_done"), sem("ugain_ok")
        b_full, b_free = sem("b_full"), sem("b_free")
        s_full, max_done, neg_done, exp_done = sem("s_full"), sem("max_done"), sem("neg_done"), sem("exp_done")
        rinv_done, norm_done = sem("rinv_done"), sem("norm_done")
        ss_step, ss_ready, sexp_done, wb_done = sem("ss_step"), sem("ss_ready"), sem("sexp_done"), sem("wb_done")

        cmv_ok = sem("cmv_ok")
        kept_done = sem("kept_done")
        rt_step, mask_done, ranks_full, exps_ready, gexp_done = sem("rt_step"), sem("mask_done"), sem("ranks_full"), sem("exps_ready"), sem("gexp_done")
        slots_ready, jobs_ready, yall_ready, scattered = sem("slots_ready"), sem("jobs_ready"), sem("yall_ready"), sem("scattered")
        experts_in = sem("experts_in")
        w_even, w_odd = sem("w_even"), sem("w_odd")
        xs_in, xt_full, xt_out = sem("xs_in"), sem("xt_full"), sem("xt_out")
        h_full, h_biased, h_act = sem("h_full"), sem("h_biased"), sem("h_act")
        hT_full, hT_out, mm2_done, ys_out, ys_stored = sem("hT_full"), sem("hT_out"), sem("mm2_done"), sem("ys_out"), sem("ys_stored")
        pw_ready, pw_full, pw_out, xb_done = sem("pw_ready"), sem("pw_full"), sem("pw_out"), sem("xb_done")
        gathered = [sem(f"gathered{t}") for t in range(GROUPS)]
        b2_full, b2_used, fin_step, fin_var = sem("b2_full"), sem("b2_used"), sem("fin_step"), sem("fin_var")
        fin_rstd, fin_done, stored = sem("fin_rstd"), sem("fin_done"), sem("stored")

        block = stack.enter_context(nc.Block())

        ctx_rows = ctx_768.rearrange("b m c -> (b m) c")
        x_rows = x.rearrange("b t d -> (b t) d")
        out_rows = out.rearrange("b t d -> (b t) d")

        def tp(g, at):
            return TP_FIRST + TP_FILLS * g + TP_AT[at]

        def ut_at(b, c):
            return UT_AT + 4 * b + 1 + c

        def pt_place(g, b, k):
            if k == 1:
                return M[0], m_full, M_FILLS * g + UT_AT + 4 * b + 1, m_free[0]
            if b < GB - 1:
                return TP, tp_full, tp(g, ("pt", b, k)) + 1, tp_free
            return bank[k], pt3_full, 2 * g + k // 2 + 1, pt3_out

        Y, XT = bank[4], bank[5]

        def expert_load(eng, e, slot, done):
            one = bass.ds(e, 1)
            eng.dma_start(moe_w[:, slot, 0:8192].rearrange("p (c f) -> p c f", c=KD),
                          w1[one, :, :].rearrange("e (c p) f -> p (e c) f", p=P)).then_inc(done, 16)
            eng.dma_start(moe_w[:, slot, 8192:16384].rearrange("p (c d) -> p c d", c=KF),
                          w2[one, :, :].rearrange("e (c p) d -> p (e c) d", p=P)).then_inc(done, 16)
            eng.dma_start(b1_rows[:, slot * FF:(slot + 1) * FF], b1[one, :].to_broadcast([P, FF])).then_inc(done, 16)

        def moe_loads(sp):
            sp.wait_ge(b_full, B_FILLS * GROUPS)
            sp.dma_start(lnrow[:, 0, :], ln_g.rearrange("(o d) -> o d", o=1).to_broadcast([P, DIM])).then_inc(rows_in, 16)
            sp.dma_start(lnrow[:, 1, :], ln_b.rearrange("(o d) -> o d", o=1).to_broadcast([P, DIM])).then_inc(rows_in, 16)
            sp.dma_start(b2_sb[:, :], b2[:, :]).then_inc(rows_in, 16)

            def xs_load(j):
                sp.dma_start(xs, xs_dram[bass.ds(j * P, P), :]).then_inc(xs_in, 16)

            def ys_store(j):
                sp.wait_ge(ys_out, j + 1)
                sp.dma_start(ys_dram[bass.ds(j * P, P), :], ys).then_inc(ys_stored, 16)

            sp.wait_ge(scattered, 16 * GROUPS * TOPK)
            xs_load(0)
            sp.wait_ge(xt_full, 1)
            xs_load(1)
            with sp.Fori(2, JOBS) as j:
                sp.wait_ge(xt_full, j)
                xs_load(j)
                ys_store(j - 2)
            ys_store(JOBS - 2)
            ys_store(JOBS - 1)
            for t in range(GROUPS):
                sp.wait_ge(fin_done, t + 1)
                sp.dma_start(out_rows[t * P:(t + 1) * P, :], fin[:, t, :]).then_inc(stored, 16)
            sp.wait_ge(stored, 16 * GROUPS)

        def expert_landed(pool, e, slot):
            if not isinstance(e, int) or e > 0:
                pool.wait_ge(experts_in, e)
            pool.wait_ge((w_even, w_odd)[slot], 48 * ((e - slot) // 2 + 1))
            nc.gpsimd.tensor_tensor(pool_mark[:, :], half[:, 0:1], half[:, 0:1], ALU.add).then_inc(experts_in, 1)

        def moe_pool(pool):
            pool.wait_ge(xs_zeroed, 16)
            pool.wait_ge(slots_ready, 1)
            for t in range(GROUPS):
                pool.wait_ge(yall_ready, t + 1)
                for k in range(TOPK):
                    nc.gpsimd.indirect_dma_start(
                        out=xs_dram[:, :], out_offset=bass.IndirectOffsetOnAxis(ap=slots[:, t, k:k + 1], axis=0),
                        in_=y_all[:, t, :], in_offset=None).then_inc(scattered, 16)
            expert_landed(pool, 0, 0)
            pool.wait_ge(jobs_ready, 1)
            with pool.Fori(1, EXPERTS // 2) as i:
                for slot, done in ((0, w_even), (1, w_odd)):
                    e = 2 * i + slot
                    expert_landed(pool, e - 1, 1 - slot)
                    ended = pool.value_load(end_i[0:1, bass.ds(e - 1, 1)], min_val=1, max_val=1 + FB * JOBS)
                    pool.wait_ge(mm2_done, ended)
                    expert_load(pool, e, slot, done)
            expert_landed(pool, EXPERTS - 1, 1)
            pool.wait_ge(ys_stored, 16 * JOBS)
            for t in range(GROUPS):
                for k in range(TOPK):
                    nc.gpsimd.indirect_dma_start(
                        out=got[:, t, k, :], out_offset=None, in_=ys_dram[:, :],
                        in_offset=bass.IndirectOffsetOnAxis(ap=slots[:, t, k:k + 1], axis=0)).then_inc(gathered[t], 16)
                if t >= 2:
                    fin_pow(pool, t - 2)
            fin_pow(pool, GROUPS - 2)
            fin_pow(pool, GROUPS - 1)

        def fin_pow(pool, t):
            pool.wait_ge(fin_var, t + 1)
            nc.gpsimd.tensor_tensor(rstd[:, :], mv[:, 1:2], half[:, 0:1], ALU.pow).then_inc(fin_rstd, 1)

        def moe_act(act):
            act.wait_ge(exps_ready, 1)
            nc.scalar.activation(ge[:, :], gs[:, :], ACT.Exp).then_inc(gexp_done, 1)

            def xt_copy(j):
                act.wait_ge(xt_full, j + 1)
                if not isinstance(j, int) or j > 0:
                    act.wait_ge(h_full, FB * j)
                nc.scalar.copy(xsT.rearrange("p c t -> p (c t)"), XT[:, :]).then_inc(xt_out, 1)

            def gelu(j, fb):
                act.wait_ge(h_biased, FB * j + fb + 1)
                nc.scalar.activation(h_sb[:, fb % 2, :], h_sb[:, fb % 2, :], ACT.Gelu).then_inc(h_act, 1)

            xt_copy(0)
            with act.Fori(0, JOBS - 1) as j:
                for fb in range(FB):
                    gelu(j, fb)
                xt_copy(j + 1)
            for fb in range(FB):
                gelu(JOBS - 1, fb)

        def moe_dve(dve):
            dve.wait_ge(b_free, 1 + B_FILLS * GROUPS)
            dve.wait_ge(kept_done, GROUPS)
            dve.wait_ge(consts, 4)
            link = chain(dve, rt_step, 0)
            link(nc.vector.memset(tot[:, 0, :], 0.0))
            link(nc.vector.memset(ends[:, 0:1], 0.0))
            flat = logits[:, :, :].rearrange("p g e -> p (g e)")
            link(nc.vector.tensor_scalar(flat, flat, 1.0 / TEMP, None, ALU.mult))
            for t in range(GROUPS):
                last = nc.vector.max(top[:, t, :], logits[:, t, :])
            link(last)
            nc.vector.tensor_tensor(gs[:, :], top[:, :, 1], top[:, :, 0], ALU.subtract).then_inc(exps_ready, 1)
            for t in range(GROUPS):
                last = nc.vector.max_index(topi[:, t, :], top[:, t, :], logits[:, t, :])
            link(last)
            link(nc.vector.tensor_copy(topf[:, :, :], topi[:, :, 0:TOPK]))
            tk = [P, GROUPS * TOPK, EXPERTS]
            link(nc.vector.tensor_tensor(hot[:, :, :, :].rearrange("p t k e -> p (t k) e"),
                                         iota_e[:, :].unsqueeze(1).to_broadcast(tk),
                                         topf[:, :, :].rearrange("p t k -> p (t k)").unsqueeze(2).to_broadcast(tk),
                                         ALU.is_equal))
            nc.vector.tensor_tensor(mask[:, :, :], hot[:, :, 0, :], hot[:, :, 1, :], ALU.add).then_inc(mask_done, 1)
            for t in range(GROUPS):
                nc.vector.tensor_scalar(y_all[:, t, :], x_all[:, t, :], y2mv[:, t, 0:1], y2mv[:, t, 1:2],
                                        ALU.subtract, ALU.mult).then_inc(yall_ready, 1)
            dve.wait_ge(ranks_full, 1)
            for t in range(GROUPS):
                link(nc.vector.tensor_tensor(tot[:, t + 1, :], tot[:, t, :], bank[1][:, t * EXPERTS:(t + 1) * EXPERTS], ALU.add))
            nc.vector.tensor_tensor(rank[:, :, :], tot[:, 0:GROUPS, :],
                                    bank[0][:, 0:GROUPS * EXPERTS].rearrange("p (t e) -> p t e", e=EXPERTS), ALU.add)
            e8 = [P, EXPERTS, 8]
            link(nc.vector.tensor_tensor(cmp8[:, :, :], tot[:, GROUPS, :].unsqueeze(2).to_broadcast(e8),
                                         iota_q[:, :].unsqueeze(1).to_broadcast(e8), ALU.is_gt))
            link(nc.vector.reduce_sum(tiles[:, :], cmp8[:, :, :], AX))
            for e in range(EXPERTS):
                link(nc.vector.tensor_tensor(ends[:, e + 1:e + 2], ends[:, e:e + 1], tiles[:, e:e + 1], ALU.add))
            te = [P, GROUPS, EXPERTS]
            link(nc.vector.scalar_tensor_tensor(out=rank[:, :, :], in0=ends[:, 0:EXPERTS].unsqueeze(1).to_broadcast(te),
                                                scalar=float(P), in1=rank[:, :, :], op0=ALU.mult, op1=ALU.add))
            for k in range(TOPK):
                last = nc.vector.tensor_tensor(prod[:, :, k, :], hot[:, :, k, :], rank[:, :, :], ALU.mult)
            link(last)
            link(nc.vector.reduce_sum(slotf[:, :, :], prod[:, :, :, :], AX))
            nc.vector.tensor_copy(slots[:, :, :], slotf[:, :, :]).then_inc(slots_ready, 1)
            je = [P, 24, EXPERTS]
            link(nc.vector.tensor_tensor(cmpj[:, :, :], iota_j[:, :].unsqueeze(2).to_broadcast(je),
                                         ends[:, 1:EXPERTS + 1].unsqueeze(1).to_broadcast(je), ALU.is_ge))
            link(nc.vector.reduce_sum(jobf[:, :], cmpj[:, :, :], AX))
            nc.vector.tensor_scalar(end_i[:, :], ends[:, :], float(FB), 1.0, ALU.mult, ALU.add)
            link(nc.vector.tensor_scalar(job_e[:, :], jobf[:, :], float(EXPERTS - 1), None, ALU.min))
            nc.vector.memset(zero1[:, :], 0.0).then_inc(jobs_ready, 1)
            dve.wait_ge(gexp_done, 1)
            link(nc.vector.tensor_scalar(gs[:, :], ge[:, :], 1.0, None, ALU.add))
            link(nc.vector.reciprocal(gp[:, :, 0], gs[:, :]))
            link(nc.vector.tensor_tensor(gp[:, :, 1], ge[:, :], gp[:, :, 0], ALU.mult))
            for k in range(TOPK):
                last = nc.vector.tensor_tensor(prod[:, :, k, :], hot[:, :, k, :],
                                               gp[:, :, k:k + 1].to_broadcast(te), ALU.mult)
            link(last)
            nc.vector.tensor_tensor(pe_all[:, :, :], prod[:, :, 0, :], prod[:, :, 1, :], ALU.add).then_inc(pw_ready, 1)
            dve.wait_ge(pw_full, 1)
            for i in range(2):
                last = nc.vector.tensor_copy(pT8[:, 4 * i:4 * i + 4, :].rearrange("e t n -> e (t n)"), bank[2 + i][0:EXPERTS, :])
            last.then_inc(pw_out, 1)
            dve.wait_ge(rows_in, 48)
            for t in range(GROUPS):
                last = nc.vector.tensor_tensor(x_all[:, t, :], x_all[:, t, :], lnrow[:, 1, :], ALU.add)
            last.then_inc(xb_done, 1)

            def bias(j, fb, slot):
                dve.wait_ge(h_full, FB * j + fb + 1)
                if fb >= 2 or not isinstance(j, int) or j > 0:
                    dve.wait_ge(hT_full, FB * j + fb - 1)
                nc.vector.tensor_tensor(h_sb[:, fb % 2, :], bank[fb % 2][:, :],
                                        b1_rows[:, bass.ds(slot * FF + fb * 512, 512)], ALU.add).then_inc(h_biased, 1)

            def hT_copy(j, fb):
                dve.wait_ge(hT_full, FB * j + fb + 1)
                if fb >= 2 or not isinstance(j, int) or j > 0:
                    dve.wait_ge(mm2_done, 1 + FB * j + fb - 1)
                nc.vector.tensor_copy(hT_sb[:, fb % 2, :, :].rearrange("p c t -> p (c t)"), bank[2 + fb % 2][:, :]).then_inc(hT_out, 1)

            def y_copy(j):
                dve.wait_ge(mm2_done, 1 + FB * (j + 1))
                if not isinstance(j, int) or j > 0:
                    dve.wait_ge(ys_stored, 16 * j)
                nc.vector.tensor_copy(ys, Y[:, :]).then_inc(ys_out, 1)

            def job(j, first):
                slot = dve.value_load(job_e[0:1, bass.ds(j, 1)], min_val=0, max_val=EXPERTS - 1) % 2
                bias(j, 0, slot)
                if not first:
                    hT_copy(j - 1, 3)
                bias(j, 1, slot)
                hT_copy(j, 0)
                if not first:
                    y_copy(j - 1)
                bias(j, 2, slot)
                hT_copy(j, 1)
                bias(j, 3, slot)
                hT_copy(j, 2)

            job(0, True)
            job(1, False)
            with dve.Fori(2, JOBS) as j:
                job(j, False)
            hT_copy(JOBS - 1, 3)
            y_copy(JOBS - 1)

            dve.wait_ge(xb_done, 1)
            link = chain(dve, fin_step, 0)
            for t in range(GROUPS):
                f = fin[:, t, :]
                dve.wait_ge(gathered[t], 16 * TOPK)
                dve.wait_ge(b2_full, t + 1)
                nc.vector.scalar_tensor_tensor(out=f, in0=got[:, t, 0, :], scalar=gp[:, t, 0:1], in1=bank[t % 4][:, :],
                                               op0=ALU.mult, op1=ALU.add).then_inc(b2_used, 1)
                dve.wait_ge(b2_used, t + 1)
                link(nc.vector.scalar_tensor_tensor(out=f, in0=got[:, t, 1, :], scalar=gp[:, t, 1:2], in1=f,
                                                    op0=ALU.mult, op1=ALU.add))
                link(nc.vector.bn_stats(stats[:, :], f))
                link(nc.vector.bn_aggr(mv[:, :], stats[:, :]))
                nc.vector.tensor_scalar(mv[:, 1:2], mv[:, 1:2], EPS, None, ALU.add).then_inc(fin_var, 1)
                link(nc.vector.scalar_tensor_tensor(out=f, in0=f, scalar=mv[:, 0:1], in1=lnrow[:, 0, :],
                                                    op0=ALU.subtract, op1=ALU.mult))
                dve.wait_ge(fin_rstd, t + 1)
                nc.vector.scalar_tensor_tensor(out=f, in0=f, scalar=rstd[:, 0:1], in1=x_all[:, t, :],
                                               op0=ALU.mult, op1=ALU.add).then_inc(fin_done, 1)

        def moe_pe(pe):
            pe.wait_ge(mask_done, 1)
            m2 = mask[:, :, :].rearrange("p t e -> p (t e)")
            nc.tensor.matmul(bank[0][:, 0:GROUPS * EXPERTS], before[:, :], m2, start=True, stop=True).then_inc(mm2_done, 1)
            nc.tensor.matmul(bank[1][:, 0:GROUPS * EXPERTS], ones[:, :], m2, start=True, stop=True).then_inc(ranks_full, 1)
            pe.wait_ge(pw_ready, 1)
            for t in range(GROUPS):
                last = nc.tensor.transpose(bank[2 + t // 4][0:EXPERTS, (t % 4) * P:(t % 4 + 1) * P], pe_all[:, t, :], ident[:, :])
            last.then_inc(pw_full, 1)
            pe.wait_ge(pw_out, 1)

            def xt_fill(j):
                pe.wait_ge(xs_in, 16 * (j + 1))
                if not isinstance(j, int) or j > 0:
                    pe.wait_ge(xt_out, j)
                for c in range(KD):
                    last = nc.tensor.transpose(XT[:, c * P:(c + 1) * P], xs[:, c * P:(c + 1) * P], ident[:, :])
                last.then_inc(xt_full, 1)

            def mm1(j, fb, e):
                if fb == 0:
                    pe.wait_ge(xt_out, j + 1)
                    pe.wait_ge(experts_in, e + 1)
                if fb >= 2 or not isinstance(j, int) or j > 0:
                    pe.wait_ge(h_biased, FB * j + fb - 1)
                for k in range(KD):
                    last = nc.tensor.matmul(bank[fb % 2][:, :], xsT[:, k, :],
                                            moe_flat[:, bass.ds((e % 2) * 16384 + k * FF + fb * 512, 512)],
                                            start=(k == 0), stop=(k == KD - 1))
                last.then_inc(h_full, 1)

            def hT_fill(j, fb):
                pe.wait_ge(h_act, FB * j + fb + 1)
                if fb >= 2 or not isinstance(j, int) or j > 0:
                    pe.wait_ge(hT_out, FB * j + fb - 1)
                for c in range(4):
                    last = nc.tensor.transpose(bank[2 + fb % 2][:, c * P:(c + 1) * P], h_sb[:, fb % 2, c * P:(c + 1) * P], ident[:, :])
                last.then_inc(hT_full, 1)

            def mm2(j, fb, e):
                pe.wait_ge(hT_out, FB * j + fb + 1)
                if fb == 0 and (not isinstance(j, int) or j > 0):
                    pe.wait_ge(ys_out, j)
                for c in range(4):
                    last = nc.tensor.matmul(Y[:, :], hT_sb[:, fb % 2, c, :],
                                            moe_flat[:, bass.ds((e % 2) * 16384 + 8192 + (4 * fb + c) * DIM, DIM)],
                                            start=(fb == 0 and c == 0), stop=(fb == 3 and c == 3))
                last.then_inc(mm2_done, 1)

            def job(j, first, last):
                e = pe.value_load(job_e[0:1, bass.ds(j, 1)], min_val=0, max_val=EXPERTS - 1)
                mm1(j, 0, e)
                if not first:
                    before_e = pe.value_load(job_e[0:1, bass.ds(j - 1, 1)], min_val=0, max_val=EXPERTS - 1)
                    hT_fill(j - 1, 3)
                    mm2(j - 1, 2, before_e)
                mm1(j, 1, e)
                hT_fill(j, 0)
                if not first:
                    mm2(j - 1, 3, before_e)
                mm1(j, 2, e)
                hT_fill(j, 1)
                mm2(j, 0, e)
                mm1(j, 3, e)
                if not last:
                    xt_fill(j + 1)
                hT_fill(j, 2)
                mm2(j, 1, e)
                return e

            pe.wait_ge(jobs_ready, 1)
            xt_fill(0)
            job(0, True, False)
            with pe.Fori(1, JOBS - 1) as j:
                job(j, False, False)
            e = job(JOBS - 1, False, True)
            hT_fill(JOBS - 1, 3)
            mm2(JOBS - 1, 2, e)
            mm2(JOBS - 1, 3, e)
            pe.wait_ge(rows_in, 48)
            pe.wait_ge(h_biased, FB * JOBS)
            pe.wait_ge(hT_out, FB * JOBS)
            for t in range(GROUPS):
                if t >= 4:
                    pe.wait_ge(b2_used, t - 3)
                nc.tensor.matmul(bank[t % 4][:, :], pT8[:, t, :], b2_sb[:, :], start=True, stop=True).then_inc(b2_full, 1)

        def ctx_load(sp, g, b):
            row = (g * GB + b) * KEYS
            sp.dma_start(ctx[0:85, b, :, :].rearrange("p k c -> p (k c)"),
                         ctx_rows[bass.ds(row, 255), :].rearrange("(p k) c -> p (k c)", k=3)).then_inc(ctx_in[b], 16)
            sp.dma_start(ctx[85:86, b, 0:2, :].rearrange("p k c -> p (k c)"),
                         ctx_rows[bass.ds(row + 255, 2), :].rearrange("(p k) c -> p (k c)", k=2)).then_inc(ctx_in[b], 16)

        @block.sync
        def _(sp):
            sp.dma_start(x_all[:, 0, :], x_rows[0:P, :]).then_inc(x0_in, 16)
            ctx_load(sp, 0, 0)
            sp.dma_start(wk_rows, Wk.rearrange("(c p) n -> p c n", p=P)).then_inc(wk_in, 16)
            sp.dma_start(wq, Wq.rearrange("(c p) n -> p c n", p=P)).then_inc(wq_in, 16)
            sp.dma_start(qkv_rows, W_qkv.rearrange("(c p) n -> p c n", p=P)).then_inc(qkv_in, 16)
            sp.dma_start(wos_rows, W_o.rearrange("(c p) n -> p c n", p=P)).then_inc(wos_in, 16)
            ctx_load(sp, 0, 1)
            ctx_load(sp, 0, 2)
            sp.dma_start(x_all[:, 1:GROUPS, :],
                         x_rows[P:, :].rearrange("(g p) d -> p g d", p=P)).then_inc(x_in, 16)
            ctx_load(sp, 0, 3)
            sp.dma_start(wv, Wv.rearrange("(c p) n -> p c n", p=P)).then_inc(wv_in, 16)
            sp.dma_start(wo, Wo.rearrange("(m p) n -> p m n", p=P)).then_inc(wo_in, 16)
            sp.dma_start(gate[:, :, :], gate_w.rearrange("(c p) e -> p c e", p=P)).then_inc(gate_in, 16)
            sp.dma_start(gate_bias[:, :], gate_b.rearrange("(o e) -> o e", o=1).to_broadcast([P, EXPERTS])).then_inc(gate_in, 16)
            sp.wait_ge(zeros_ok, 1)
            sp.dma_start(xs_dram.rearrange("(j p) d -> p j d", p=P),
                         blocks[:, 0:4, :].rearrange("p h t -> p (h t)").unsqueeze(1).to_broadcast([P, JOBS, DIM])).then_inc(xs_zeroed, 16)
            with sp.Fori(1, GROUPS) as g:
                for b in range(GB):
                    sp.wait_ge(m_full, M_FILLS * (g - 1) + ut_at(b, 2) + 1)
                    ctx_load(sp, g, b)
            moe_loads(sp)

        @block.gpsimd
        def _(pool):
            nc.gpsimd.memset(ones[:, :], 1.0).then_inc(memset_ok, 1)
            nc.gpsimd.memset(half[:, :], -0.5).then_inc(memset_ok, 1)
            pool.wait_ge(memset_ok, 2)
            nc.gpsimd.affine_select(out=ident[:, :], in_=ones[:, :], compare_op=ALU.is_equal, fill=0.0, base=0,
                                    pattern=[[-1, P]], channel_multiplier=1).then_inc(ident_ok, 1)
            nc.gpsimd.affine_select(out=before[:, :], in_=ones[:, :], compare_op=ALU.is_gt, fill=0.0, base=0,
                                    pattern=[[1, P]], channel_multiplier=-1).then_inc(consts, 1)
            nc.gpsimd.iota(iota_e[:, :], pattern=[[1, EXPERTS]], base=0, channel_multiplier=0,
                           allow_small_or_imprecise_dtypes=True).then_inc(consts, 1)
            nc.gpsimd.iota(iota_q[:, :], pattern=[[P, 8]], base=0, channel_multiplier=0,
                           allow_small_or_imprecise_dtypes=True).then_inc(consts, 1)
            nc.gpsimd.iota(iota_j[:, :], pattern=[[1, 24]], base=0, channel_multiplier=0,
                           allow_small_or_imprecise_dtypes=True).then_inc(consts, 1)

            def ln_pow(n):
                pool.wait_ge(ln_var, n + 1)
                nc.gpsimd.tensor_tensor(rstd[:, :], mv[:, 1:2], half[:, 0:1], ALU.pow).then_inc(ln_rstd, 1)

            def cn_pow(n):
                pool.wait_ge(cn_var, n + 1)
                nc.gpsimd.tensor_tensor(crstd[0:86, :], cmv[0:86, :, 1], half[0:86, 0:3], ALU.pow).then_inc(cn_rstd, 1)

            def body(g, do_a, do_b, nxt):
                ln = 2 * g + 2 + 2 * (g - 1)
                if isinstance(g, int) and g == 0:
                    ln = 2
                if do_b:
                    ln_pow(ln)
                    ln = ln + 1
                if nxt:
                    ln_pow(ln)
                if isinstance(g, int) and g == 0:
                    cn_pow(2)
                if do_a:
                    cn_pow(GB * g + 3)
                if nxt:
                    cn_pow(GB * g + 4)
                    cn_pow(GB * g + 5)
                    cn_pow(GB * g + 6)
                    ln_pow(ln + 1)
                    ln = ln + 2
                if do_b:
                    ln_pow(ln)

            ln_pow(0)
            ln_pow(1)
            cn_pow(0)
            cn_pow(1)
            body(0, True, False, True)
            with pool.Fori(1, GROUPS - 1) as g:
                body(g, True, True, True)
            body(GROUPS - 1, True, True, False)
            body_8_ln = 2 * GROUPS + 2 * (GROUPS - 1)
            pool.wait_ge(m_full, M_FILLS * GROUPS)
            expert_load(pool, 0, 0, w_even)
            ln_pow(body_8_ln)
            pool.wait_ge(b_full, B_FILLS * (GROUPS - 1) + KQ_AT + 1)
            expert_load(pool, 1, 1, w_odd)
            ln_pow(body_8_ln + 1)
            moe_pool(pool)

        def setup_out(eng, copy, n):
            dst = (wkT[:, n, :] if n < 8 else wqkvT[:, n - 8, :] if n < 12 else wosT[:, n - 12, :])
            eng.wait_ge(setup_full, n + 1)
            copy(dst, bank[n % 4][:, 0:dst.shape[1]]).then_inc(setup_free[n % 2], 1)

        def qk_copy(eng, copy, g, i, par):
            hq, c = i // KC, i % KC
            dst = qkT[:, c, :, :].rearrange("p b (h two t) -> p h two b t", two=2, t=TOK)[:, 4 * hq:4 * hq + 4, par]
            eng.wait_ge(qk_full, 2 * QK_PAIRS * g + 2 * i + par + 1)
            copy(dst, bank[(2 * i + par) % 4][:, :].rearrange("p (h b t) -> p h b t", h=4, b=GB)).then_inc(qk_out[par], 1)

        @block.scalar
        def _(act):
            with nc.allow_non_contiguous_dma(reason="a few columns"):
                act.dma_start(gcol[:, 0, :], g_x.rearrange("(c p) -> p c", p=P)).then_inc(cols_in, 16)
                act.dma_start(gcol[:, 1, :], b_x.rearrange("(c p) -> p c", p=P)).then_inc(cols_in, 16)
                act.dma_start(ccol[:, 0, :], g_c.rearrange("(c p) -> p c", p=P)).then_inc(cols_in, 16)
                act.dma_start(ccol[:, 1, :], b_c.rearrange("(c p) -> p c", p=P)).then_inc(cols_in, 16)
            act.wait_ge(cols_in, 64)
            nc.scalar.activation(ugain[:, :], ccol[:, 0, :], ACT.Identity, scale=1.0 / (N_SCALE * P_SCALE)).then_inc(ugain_ok, 1)

            def xn_out(n):
                act.wait_ge(tp_full, n + 1)
                for c in range(KD):
                    last = nc.scalar.activation(xnT[:, c, :], TP[:, c * P:(c + 1) * P], ACT.Identity,
                                                bias=gcol[:, 1, c:c + 1], scale=gcol[:, 0, c:c + 1])
                last.then_inc(tp_free, 1)

            def ct_out(n, b, c):
                act.wait_ge(tp_full, n + 1)
                nc.scalar.activation(cnT[:, b % 2, c, :], TP[:, 0:KEYS], ACT.Identity,
                                     bias=ccol[:, 1, c:c + 1], scale=ccol[:, 0, c:c + 1]).then_inc(tp_free, 1)

            def m_copy(g, at, dst, src):
                act.wait_ge(m_full, M_FILLS * g + at + 1)
                nc.scalar.copy(dst, src).then_inc(m_free[at % 2], 1)

            def exps(g, b):
                bt = GB * g + b
                for h in range(HG):
                    act.wait_ge(neg_done, HG * bt + h + 1)
                    nc.scalar.activation(probs[:, h, :], bank[h][:, 0:KEYS], ACT.Exp, bias=negm[:, h:h + 1],
                                         scale=XSCALE, accum_out=rsum[:, h:h + 1]).then_inc(exp_done, 1)

            def ut_out(g, b, c):
                at = ut_at(b, c)
                act.wait_ge(m_full, M_FILLS * g + at + 1)
                nc.scalar.activation(uT[:, c, :, b, :], M[at % 2][:, :].rearrange("p (h t) -> p h t", t=TOK), ACT.Identity,
                                     bias=ccol[:, 1, c:c + 1], scale=ugain[:, c:c + 1]).then_inc(m_free[at % 2], 1)

            def n_hi(g, b):
                act.wait_ge(cn_done, GB * g + b + 1)
                for k in range(3):
                    last = nc.scalar.activation(n_high[0:PART[k], b % 2, k, :], ctx[0:PART[k], b, k, :], ACT.Identity, scale=N_SCALE)
                last.then_inc(n_high_done, 1)

            def pt_hi(g, b, k):
                src, full, count, _ = pt_place(g, b, k)
                act.wait_ge(full, count)
                nc.scalar.copy(pT_high[0:PART[k], k, :], src[0:PART[k], :]).then_inc(p_high_done, 1)

            def b_copy(g, at, dst):
                act.wait_ge(b_full, B_FILLS * g + at + 1)
                nc.scalar.copy(dst, BK[:, :]).then_inc(b_free, 1)

            def body(g, do_a, do_b, nxt):
                if do_a:
                    m_copy(g, QT_AT + 1, qT[:, 4:8, :].rearrange("p m t -> p (m t)"), M[1][:, :])
                if isinstance(g, int) and g == 0:
                    for n in range(9, 16, 2):
                        setup_out(act, nc.scalar.copy, n)
                for i in range(QK_PAIRS):
                    if do_a:
                        qk_copy(act, nc.scalar.copy, g, i, 1)
                    if i == 3 and do_b:
                        b_copy(g - 1, KQ_AT, kqT[:, :, :].rearrange("p c t -> p (c t)"))
                if do_b:
                    b_copy(g - 1, V_AT, v_sb[:, :])
                for b in range(GB + 1):
                    if do_a:
                        if b < GB:
                            n_hi(g, b)
                        for k in range(3):
                            if b == 0:
                                ct_out(tp(g, ("ct", 1, k)), 1, k)
                            else:
                                pt_hi(g, b - 1, k)
                        if b < GB:
                            exps(g, b)
                    for c in range(KC):
                        if do_a:
                            if 1 <= b < 3 or (b == GB and nxt):
                                nb = b + 1 if b < GB else GB
                                ct_out(tp(g, ("ct", nb, c)), nb, c)
                            if b >= 1:
                                ut_out(g, b - 1, c)
                        if do_b and b == GB and c == 1:
                            b_copy(g - 1, PV_AT, kqT[:, :, :].rearrange("p c t -> p (c t)"))
                    if do_b and b == 2:
                        act.wait_ge(ss_ready, g)
                        nc.scalar.activation(sS[:, :, :], sS[:, :, :], ACT.Exp, scale=SSCALE).then_inc(sexp_done, 1)
                if do_a:
                    m_copy(g, O_AT + 1, oT[:, 4:8, :].rearrange("p m t -> p (m t)"), M[1][:, :])
                if nxt:
                    xn_out(tp(g, "xn"))

            xn_out(0)
            for c in range(KC):
                ct_out(1 + c, 0, c)
            for n in range(1, 8, 2):
                setup_out(act, nc.scalar.copy, n)
            body(0, True, False, True)
            with act.Fori(1, GROUPS - 1) as g:
                body(g, True, True, True)
            body(GROUPS - 1, True, True, False)
            body(GROUPS, False, True, False)
            moe_act(act)

        @block.vector
        def _(dve):
            nc.vector.memset(blocks[:, :, :], 0.0).then_inc(zeros_ok, 1)
            nc.vector.memset(cmv[:, :, :], 1.0).then_inc(cmv_ok, 1)
            nc.vector.memset(dve_mark[:, :], 0.0).then_inc(b_free, 1)
            dve.wait_ge(cmv_ok, 1)

            def carry_wait():
                nc.vector.memset(zero1[:, :], 0.0)

            def layernorm(n, src, dst, done):
                link = chain(dve, ln_step, 2 * n)
                carry_wait()
                link(nc.vector.bn_stats(stats[:, :], src))
                carry_wait()
                link(nc.vector.bn_aggr(mv[:, :], stats[:, :]))
                nc.vector.tensor_scalar(mv[:, 1:2], mv[:, 1:2], EPS, None, ALU.add).then_inc(ln_var, 1)
                dve.wait_ge(ln_rstd, n + 1)
                nc.vector.tensor_scalar(dst, src, mv[:, 0:1], rstd[:, 0:1], ALU.subtract, ALU.mult).then_inc(done, 1)

            def xn_norm(n, g, second):
                if second:
                    dve.wait_ge(xn_done, 2 * g + 1)
                    layernorm(n, xn, xn, xn_done)
                else:
                    layernorm(n, x_all[:, bass.ds(g, 1), :].rearrange("p g d -> p (g d)"), xn, xn_done)

            def cn_stats(g, b):
                bt, slot = GB * g + b, b % GB
                dve.wait_ge(ctx_in[slot], 32 * (g + b // GB + 1))
                for k in range(3):
                    last = nc.vector.bn_stats(cstats[0:PART[k], k, :], ctx[0:PART[k], slot, k, :])
                link = chain(dve, cn_step, 2 * bt)
                link(last)
                carry_wait()
                for k in range(3):
                    last = nc.vector.bn_aggr(cmv[0:PART[k], k, :], cstats[0:PART[k], k, :])
                link(last)
                nc.vector.tensor_scalar(cmv[0:86, :, 1], cmv[0:86, :, 1], EPS, None, ALU.add).then_inc(cn_var, 1)

            def cn_apply(g, b):
                bt, slot = GB * g + b, b % GB
                dve.wait_ge(cn_rstd, bt + 1)
                for k in range(3):
                    c = ctx[0:PART[k], slot, k, :]
                    last = nc.vector.tensor_scalar(c, c, cmv[0:PART[k], k, 0:1], crstd[0:PART[k], k:k + 1],
                                                   ALU.subtract, ALU.mult)
                last.then_inc(cn_done, 1)

            def m_copy(g, at, dst, src):
                dve.wait_ge(m_full, M_FILLS * g + at + 1)
                nc.vector.tensor_copy(dst, src).then_inc(m_free[at % 2], 1)

            def b_copy(g, at, dst, src=BK[:, :]):
                dve.wait_ge(b_full, B_FILLS * g + at + 1)
                nc.vector.tensor_copy(dst, src).then_inc(b_free, 1)

            def row_max(g, b, h):
                n = HG * (GB * g + b) + h
                dve.wait_ge(s_full, n + 1)
                nc.vector.reduce_max(mx[:, h:h + 1], bank[h][:, 0:KEYS], AX).then_inc(max_done, 1)
                dve.wait_ge(max_done, n + 1)
                nc.vector.tensor_scalar(negm[:, h:h + 1], mx[:, h:h + 1], -XSCALE, None, ALU.mult).then_inc(neg_done, 1)

            def norm_probs(g, b):
                bt = GB * g + b
                dve.wait_ge(exp_done, HG * (bt + 1))
                nc.vector.reciprocal(rinv[:, :], rsum[:, :]).then_inc(rinv_done, 1)
                dve.wait_ge(rinv_done, bt + 1)
                for h in range(HG):
                    last = nc.vector.tensor_scalar(probs[:, h, :], probs[:, h, :], rinv[:, h:h + 1], P_SCALE, ALU.mult, ALU.mult)
                last.then_inc(norm_done, 1)

            def pt_lo(g, b, k):
                dve.wait_ge(p_high_done, 3 * (GB * g + b) + k + 1)
                src, _, _, emptied = pt_place(g, b, k)
                nc.vector.tensor_tensor(pT_low[0:PART[k], k, :], src[0:PART[k], :], pT_high[0:PART[k], k, :],
                                        ALU.subtract).then_inc(emptied, 1)

            def n_lo(g, b):
                dve.wait_ge(n_high_done, GB * g + b + 1)
                for k in range(3):
                    last = nc.vector.scalar_tensor_tensor(out=n_low[0:PART[k], b, k, :], in0=ctx[0:PART[k], b, k, :],
                                                          scalar=N_SCALE, in1=n_high[0:PART[k], b % 2, k, :],
                                                          op0=ALU.mult, op1=ALU.subtract)
                last.then_inc(n_low_done, 1)

            def ss_out(g, hh):
                dve.wait_ge(b_full, B_FILLS * g + SS_AT + hh + 1)
                for q in range(GB):
                    rows = slice(TOK * q, TOK * (q + 1))
                    last = nc.vector.tensor_copy(
                        sS[rows, :, :].rearrange("p (m h) j -> p m h j", h=4)[:, :, hh, :],
                        BK[rows, :].rearrange("p (m j) -> p m j", m=4)[:, :, TOK * q:TOK * (q + 1)])
                last.then_inc(b_free, 1)

            def ss_sub(g):
                dve.wait_ge(b_free, 1 + B_FILLS * g + SS_AT + 4)
                link = chain(dve, ss_step, 4 * g)
                link(nc.vector.tensor_reduce(smx[:, :], sS[:, :, :], AX, ALU.max))
                nc.vector.tensor_tensor(sS[:, :, :], sS[:, :, :], smx[:, :].unsqueeze(2).to_broadcast([P, SHEADS, TOK]),
                                        ALU.subtract).then_inc(ss_ready, 1)

            def ss_norm(g):
                dve.wait_ge(sexp_done, g + 1)
                link = chain(dve, ss_step, 4 * g + 1)
                link(nc.vector.reduce_sum(ssum[:, :], sS[:, :, :], AX))
                link(nc.vector.reciprocal(ssum[:, :], ssum[:, :]))
                link(nc.vector.tensor_tensor(sS[:, :, :], sS[:, :, :], ssum[:, :].unsqueeze(2).to_broadcast([P, SHEADS, TOK]),
                                             ALU.mult))
                for q in range(GB):
                    rows = slice(TOK * q, TOK * (q + 1))
                    last = nc.vector.transpose(blocks[rows, :, TOK * q:TOK * (q + 1)], sS[rows, :, :])
                last.then_inc(wb_done, 1)

            def body(g, do_a, do_b, nxt):
                ln = 2 * g + 2 + 2 * (g - 1)
                if isinstance(g, int) and g == 0:
                    ln = 2
                if isinstance(g, int) and g == GROUPS:
                    ln = 2 * GROUPS + 2 * (GROUPS - 1)
                x_prev = x_all[:, bass.ds(g - 1, 1), :].rearrange("p g d -> p (g d)") if do_b else None
                if do_b:
                    for i in range(2):
                        dve.wait_ge(m_free[i], (M_FILLS // 2) * g)
                    layernorm(ln, x_prev, y[:, :], y_done)
                    ln = ln + 1
                if do_a:
                    m_copy(g, QT_AT, qT[:, 0:4, :].rearrange("p m t -> p (m t)"), M[0][:, :])
                if isinstance(g, int) and g == 0:
                    for n in range(8, 16, 2):
                        setup_out(dve, nc.vector.tensor_copy, n)
                    cn_stats(0, 1)
                    cn_apply(0, 1)
                for i in range(QK_PAIRS):
                    if do_a:
                        qk_copy(dve, nc.vector.tensor_copy, g, i, 0)
                    if i == 1 and do_b:
                        b_copy(g - 1, YT_AT, yT[:, :, :].rearrange("p c t -> p (c t)"))
                if isinstance(g, int) and g == 0:
                    dve.wait_ge(x_in, 16)
                if nxt:
                    xn_norm(ln, g + 1, 0)
                if do_a:
                    n_lo(g, 0)
                for b in range(GB):
                    ahead = (do_a and b == 1) or (nxt and b >= 2)
                    if do_a:
                        for k in range(HG):
                            if b >= 1 and k < 3:
                                pt_lo(g, b - 1, k)
                            row_max(g, b, k)
                    if do_b and b == 2:
                        ss_out(g - 1, 3)
                    if do_a and b > 0:
                        n_lo(g, b)
                    if ahead:
                        cn_stats(g, b + 2)
                    if do_b and b == 1:
                        ss_out(g - 1, 1)
                    if do_a:
                        norm_probs(g, b)
                    if do_b and b == 0:
                        ss_out(g - 1, 0)
                    if ahead:
                        cn_apply(g, b + 2)
                    if isinstance(g, int) and g == 0 and b == 0:
                        cn_stats(0, 2)
                        cn_apply(0, 2)
                    if do_b and b == 1:
                        ss_out(g - 1, 2)
                    if do_b and b == 2:
                        ss_sub(g - 1)
                if do_a:
                    for k in range(3):
                        pt_lo(g, GB - 1, k)
                if do_b:
                    ss_norm(g - 1)
                if nxt:
                    cn_stats(g, 6)
                    cn_apply(g, 6)
                    xn_norm(ln + 1, g + 1, 1)
                    ln = ln + 2
                if do_b:
                    dve.wait_ge(b_full, B_FILLS * (g - 1) + WS_AT + 1)
                    nc.vector.tensor_tensor(x_prev, x_prev, BK[:, :], ALU.add).then_inc(b_free, 1)
                    dve.wait_ge(b_free, 1 + B_FILLS * (g - 1) + WS_AT + 1)
                    layernorm(ln, x_prev, y[:, :], y_done)
                    kept = y2mv[:, bass.ds(g - 1, 1), :].rearrange("p g s -> p (g s)")
                    nc.vector.tensor_copy(kept[:, 0:1], mv[:, 0:1])
                    nc.vector.tensor_copy(kept[:, 1:2], rstd[:, :]).then_inc(kept_done, 1)
                if do_a:
                    m_copy(g, O_AT, oT[:, 0:4, :].rearrange("p m t -> p (m t)"), M[0][:, :])
                if do_b:
                    b_copy(g - 1, YT2_AT, yT[:, :, :].rearrange("p c t -> p (c t)"))
                if do_a:
                    x1_add(g, 0)
                if do_b:
                    dve.wait_ge(b_full, B_FILLS * (g - 1) + LG_AT + 1)
                    nc.vector.tensor_tensor(logits[:, bass.ds(g - 1, 1), :].rearrange("p g e -> p (g e)"), BK[:, 0:EXPERTS],
                                            gate_bias[:, :], ALU.add).then_inc(b_free, 1)
                if do_a:
                    x1_add(g, 1)

            def x1_add(g, j):
                dve.wait_ge(m_full, M_FILLS * g + WO_AT + j + 1)
                x_now = x_all[:, bass.ds(g, 1), j * 256:(j + 1) * 256].rearrange("p g d -> p (g d)")
                nc.vector.tensor_tensor(x_now, x_now, M[j][:, 0:256], ALU.add).then_inc(m_free[j], 1)

            dve.wait_ge(x0_in, 16)
            xn_norm(0, 0, 0)
            xn_norm(1, 0, 1)
            cn_stats(0, 0)
            cn_apply(0, 0)
            for n in range(0, 8, 2):
                setup_out(dve, nc.vector.tensor_copy, n)
            body(0, True, False, True)
            dve.wait_ge(gate_in, 32)
            dve.wait_ge(xs_zeroed, 16)
            with dve.Fori(1, GROUPS - 1) as g:
                body(g, True, True, True)
            body(GROUPS - 1, True, True, False)
            body(GROUPS, False, True, False)
            moe_dve(dve)

        @block.tensor
        def _(pe):
            def setup_fill(n):
                if n >= 4:
                    pe.wait_ge(setup_free[n % 2], (n - 4) // 2 + 1)
                if n < 8:
                    for c in range(KC):
                        last = nc.tensor.transpose(bank[n % 4][:, c * P:(c + 1) * P], wk_rows[:, c, n * P:(n + 1) * P], ident[:, :])
                else:
                    rows, m = (qkv_rows, n - 8) if n < 12 else (wos_rows, n - 12)
                    for c in range(KD):
                        last = nc.tensor.transpose(bank[n % 4][:, c * P:(c + 1) * P], rows[:, c, m * P:(m + 1) * P], ident[:, :])
                last.then_inc(setup_full, 1)

            def m_open(g, at):
                at_least(pe, m_free[at % 2], (M_FILLS // 2) * g + at // 2)
                return M[at % 2]

            def m_ready(g, at):
                pe.wait_ge(m_free[at % 2], (M_FILLS // 2) * g + at // 2 + 1)

            def b_open(g, at):
                pe.wait_ge(b_free, 1 + B_FILLS * g + at)

            def q_proj(g, i):
                ps = m_open(g, QT_AT + i)
                for m in range(4):
                    for k in range(KD):
                        last = nc.tensor.matmul(ps[:, m * P:(m + 1) * P], wq[:, k, (4 * i + m) * P:(4 * i + m + 1) * P],
                                                xnT[:, k, :], start=(k == 0), stop=(k == KD - 1))
                last.then_inc(m_full, 1)

            def qk_proj(g, i):
                hq, c = i // KC, i % KC
                if i == 0 and isinstance(g, int) and g == 0:
                    for n in range(2):
                        pe.wait_ge(setup_free[n], 8)
                if i < 2:
                    at_least(pe, exp_done, HG * GB * g)
                    at_least(pe, pt3_out, 2 * g)
                else:
                    for par in range(2):
                        pe.wait_ge(qk_out[par], QK_PAIRS * g + i - 1)
                if c == 0:
                    m_ready(g, QT_AT + hq)
                for s in range(4):
                    for par in range(2):
                        rows = slice(HDIM * par, HDIM * (par + 1))
                        last = nc.tensor.matmul(bank[(2 * i + par) % 4][:, s * P:(s + 1) * P],
                                                wkT[rows, 4 * hq + s, c * P:(c + 1) * P],
                                                qT[rows, 4 * hq + s, :], start=True, stop=True)
                        if s == 3:
                            last.then_inc(qk_full, 1)

            def scores(g, b, h):
                bt = GB * g + b
                if h == 0:
                    at_least(pe, tp_free, (TP_FIRST + TP_FILLS * g) if b == 0 else tp(g, ("ct", b, 2)) + 1)
                if b > 0:
                    pe.wait_ge(exp_done, HG * (bt - 1) + h + 1)
                elif h == 0:
                    for par in range(2):
                        pe.wait_ge(qk_out[par], QK_PAIRS * (g + 1))
                for c in range(KC):
                    last = nc.tensor.matmul(bank[h][:, 0:KEYS], qkT[:, c, b, h * P:(h + 1) * P], cnT[:, b % 2, c, :],
                                            start=(c == 0), stop=(c == KC - 1))
                last.then_inc(s_full, 1)

            def ct_fill(n, bt, b, c):
                pe.wait_ge(tp_free, n)
                if c == 0:
                    pe.wait_ge(cn_done, bt + 1)
                for k in range(3):
                    last = nc.tensor.transpose(TP[:, KOFF[k]:KOFF[k] + PART[k]], ctx[0:PART[k], b % GB, k, c * P:(c + 1) * P],
                                               ident[0:PART[k], 0:PART[k]])
                last.then_inc(tp_full, 1)

            def pt_fill(g, b, k):
                into, full, count, _ = pt_place(g, b, k)
                if k == 1:
                    m_open(g, UT_AT + 4 * b)
                elif b < GB - 1:
                    pe.wait_ge(tp_free, count - 1)
                if k == 0:
                    pe.wait_ge(norm_done, GB * g + b + 1)
                for h in range(HG):
                    last = nc.tensor.transpose(into[0:PART[k], h * P:(h + 1) * P], probs[:, h, KOFF[k]:KOFF[k] + PART[k]], ident[:, :])
                last.then_inc(full, 1)

            def av(g, b, c):
                at, n = ut_at(b, c), GB * g + b
                ps = m_open(g, at)
                if c == 0:
                    pe.wait_ge(p_high_done, 3 * (n + 1))
                    pe.wait_ge(n_low_done, n + 1)
                for i, (n_part, p_part) in enumerate(((n_high[:, b % 2], pT_high), (n_low[:, b], pT_high), (n_high[:, b % 2], pT_low))):
                    if c == 0 and i == 2:
                        m_ready(g, UT_AT + 4 * b)
                        if b < GB - 1:
                            pe.wait_ge(tp_free, tp(g, ("pt", b, 2)) + 1)
                        else:
                            pe.wait_ge(pt3_out, 2 * (g + 1))
                    for k in range(3):
                        last = nc.tensor.matmul(ps[:, :], n_part[0:PART[k], k, c * P:(c + 1) * P], p_part[0:PART[k], k, :],
                                                start=(k == 0 and i == 0), stop=(k == 2 and i == 2))
                last.then_inc(m_full, 1)

            def o_proj(g, i):
                ps = m_open(g, O_AT + i)
                if i == 0:
                    m_ready(g, ut_at(GB - 1, 1))
                    m_ready(g, ut_at(GB - 1, 2))
                for s in range(4):
                    for par in range(2):
                        h = 2 * (4 * i + s) + par
                        for c in range(KC):
                            last = nc.tensor.matmul(ps[HDIM * par:HDIM * (par + 1), s * P:(s + 1) * P],
                                                    wv[:, c, h * HDIM:(h + 1) * HDIM],
                                                    uT[:, c, h, :, :].rearrange("p b t -> p (b t)"),
                                                    start=(c == 0), stop=(c == KC - 1))
                last.then_inc(m_full, 1)

            def wo_proj(g, j):
                ps = m_open(g, WO_AT + j)
                if j == 0:
                    m_ready(g, O_AT)
                    m_ready(g, O_AT + 1)
                for m in range(KI):
                    last = nc.tensor.matmul(ps[:, 0:256], oT[:, m, :], wo[:, m, j * 256:(j + 1) * 256],
                                            start=(m == 0), stop=(m == KI - 1))
                last.then_inc(m_full, 1)

            def xn_fill(n, count):
                pe.wait_ge(tp_free, n)
                pe.wait_ge(xn_done, count)
                for c in range(KD):
                    last = nc.tensor.transpose(TP[:, c * P:(c + 1) * P], xn[:, c * P:(c + 1) * P], ident[:, :])
                last.then_inc(tp_full, 1)

            def y_fill(g, at, count):
                b_open(g, at)
                pe.wait_ge(y_done, count)
                for c in range(KD):
                    last = nc.tensor.transpose(BK[:, c * P:(c + 1) * P], y[:, c * P:(c + 1) * P], ident[:, :])
                last.then_inc(b_full, 1)

            def kq_fill(g):
                b_open(g, KQ_AT)
                for m in range(KD):
                    for k in range(KD):
                        last = nc.tensor.matmul(BK[:, m * P:(m + 1) * P], wqkvT[:, k, m * P:(m + 1) * P], yT[:, k, :],
                                                start=(k == 0), stop=(k == KD - 1))
                last.then_inc(b_full, 1)

            def v_fill(g):
                b_open(g, V_AT)
                for m in range(KD):
                    last = nc.tensor.transpose(BK[:, m * P:(m + 1) * P], kqT[:, m, :], ident[:, :])
                last.then_inc(b_full, 1)

            def ss_fill(g, hh):
                b_open(g, SS_AT + hh)
                rows = slice(SDIM * hh, SDIM * (hh + 1))
                for m in range(4):
                    last = nc.tensor.matmul(BK[:, m * P:(m + 1) * P], kqT[rows, m, :], kqT[rows, m, :], start=True, stop=True,
                                            tile_position=(SDIM * hh, 0))
                last.then_inc(b_full, 1)

            def pv_fill(g):
                b_open(g, PV_AT)
                pe.wait_ge(wb_done, g + 1)
                for m in range(4):
                    for hh in range(4):
                        h = 4 * m + hh
                        last = nc.tensor.matmul(BK[SDIM * hh:SDIM * (hh + 1), m * P:(m + 1) * P],
                                                v_sb[:, h * SDIM:(h + 1) * SDIM], blocks[:, h, :], start=True, stop=True,
                                                tile_position=(0, SDIM * hh))
                last.then_inc(b_full, 1)

            def ws_fill(g):
                b_open(g, WS_AT)
                for k in range(KD):
                    last = nc.tensor.matmul(BK[:, :], kqT[:, k, :], wosT[:, k, :], start=(k == 0), stop=(k == KD - 1))
                last.then_inc(b_full, 1)

            def lg_fill(g):
                b_open(g, LG_AT)
                for k in range(KD):
                    last = nc.tensor.matmul(BK[:, 0:EXPERTS], yT[:, k, :], gate[:, k, :], start=(k == 0), stop=(k == KD - 1))
                last.then_inc(b_full, 1)

            def body(g, do_a, do_b, nxt):
                if do_a:
                    at_least(pe, tp_free, TP_FIRST + TP_FILLS * g)
                    q_proj(g, 0)
                    q_proj(g, 1)
                if isinstance(g, int) and g == 0:
                    pe.wait_ge(qkv_in, 16)
                    pe.wait_ge(wos_in, 16)
                    for n in range(8, 16):
                        setup_fill(n)
                for i in range(QK_PAIRS):
                    if do_a:
                        qk_proj(g, i)
                    if do_b and i == 1:
                        y_fill(g - 1, YT_AT, 2 * (g - 1) + 1)
                    if do_b and i == 3:
                        kq_fill(g - 1)
                if do_b:
                    v_fill(g - 1)
                for b in range(GB + 1):
                    if do_a:
                        for h in range(HG):
                            if b < GB:
                                scores(g, b, h)
                            if b == 0 and h < 3:
                                ct_fill(tp(g, ("ct", 1, h)), GB * g + 1, 1, h)
                            if b >= 1 and h < 3:
                                pt_fill(g, b - 1, h)
                    if do_b and b == 0:
                        ss_fill(g - 1, 0)
                    if do_b and b == 2:
                        ss_fill(g - 1, 3)
                    for c in range(KC):
                        if do_a and (1 <= b < 3 or (b == GB and nxt)):
                            nb = b + 1 if b < GB else GB
                            ct_fill(tp(g, ("ct", nb, c)), GB * g + nb, nb, c)
                        if do_a and b >= 1:
                            av(g, b - 1, c)
                        if do_b and b == 1 and c != 1:
                            ss_fill(g - 1, 1 + c // 2)
                        if do_b and b == GB and c == 1:
                            pv_fill(g - 1)
                if do_b:
                    ws_fill(g - 1)
                if isinstance(g, int) and g == 0:
                    pe.wait_ge(wv_in, 16)
                    pe.wait_ge(wo_in, 16)
                    pe.wait_ge(gate_in, 32)
                if do_a:
                    o_proj(g, 0)
                    o_proj(g, 1)
                if nxt:
                    xn_fill(tp(g, "xn"), 2 * (g + 2))
                if do_b:
                    y_fill(g - 1, YT2_AT, 2 * g)
                if do_a:
                    wo_proj(g, 0)
                if do_b:
                    lg_fill(g - 1)
                if do_a:
                    wo_proj(g, 1)

            pe.wait_ge(ident_ok, 1)
            xn_fill(0, 2)
            for c in range(KC):
                ct_fill(1 + c, 0, 0, c)
            pe.wait_ge(wk_in, 16)
            for n in range(8):
                setup_fill(n)
            pe.wait_ge(wq_in, 16)
            body(0, True, False, True)
            with pe.Fori(1, GROUPS - 1) as g:
                body(g, True, True, True)
            body(GROUPS - 1, True, True, False)
            body(GROUPS, False, True, False)
            moe_pe(pe)


_INS = ['x', 'ctx_768', 'L0_xattn_g_x', 'L0_xattn_b_x', 'L0_xattn_g_c', 'L0_xattn_b_c', 'L0_xattn_Wq', 'L0_xattn_Wk',
        'L0_xattn_Wv', 'L0_xattn_Wo', 'L0_attn_W_qkv', 'L0_attn_W_o', 'L0_ffn_gate_w', 'L0_ffn_gate_b', 'L0_ffn_w1',
        'L0_ffn_b1', 'L0_ffn_w2', 'L0_ffn_b2', 'L0_ffn_ln_g', 'L0_ffn_ln_b']


def kernel(**inputs):
    import numpy as _np
    import concourse.bacc as _bacc
    from concourse.bass_utils import run_bass_kernel_spmd as _run

    nc = _bacc.Bacc("TRN2", target_bir_lowering=False, num_devices=1)
    arrays, args = {}, []
    for name in _INS:
        a = _np.ascontiguousarray(inputs[name])
        arrays[f"in_{name}_dram"] = a
        args.append(nc.dram_tensor(f"in_{name}_dram", a.shape, mybir.dt.from_np(a.dtype), kind="ExternalInput").ap())
    out = nc.dram_tensor("out_dram", (BATCH, TOK, DIM), F32, kind="ExternalOutput").ap()
    perceiver_layer(nc, *args, out)
    r = _run(nc, [arrays], core_ids=[0])
    return r.results[0]["out_dram"]
```

```python
from contextlib import ExitStack

import concourse.bass as bass
from concourse import mybir

F32 = mybir.dt.float32
F16 = mybir.dt.float16
I32 = mybir.dt.int32
U32 = mybir.dt.uint32
ALU = mybir.AluOpType
ACT = mybir.ActivationFunctionType
AX = mybir.AxisListType.X

P = 128
BATCH, TOK, DIM = 32, 32, 512
TOKENS = BATCH * TOK
KEYS, CTX = 257, 384
HEADS, HDIM = 16, 64
INNER = HEADS * HDIM
SHEADS, SDIM = 16, 32
EXPERTS, FF, TOPK = 8, 2048, 2
EPS = 1e-5
XSCALE = HDIM ** -0.5
SSCALE = SDIM ** -0.5
TEMP = 0.9
N_SCALE = 2.0 ** 11
P_SCALE = 2.0 ** 14

GB = P // TOK
GROUPS = BATCH // GB
KD = DIM // P
KC = CTX // P
KI = INNER // P
KF = FF // P
HG = HEADS // GB
PART = [86, 86, 85]
KOFF = [0, 86, 172]
ZERO_FIRST = 3
FB = FF // 512
JOBS = TOKENS * TOPK // P + EXPERTS - 1
TILES = TOKENS // P
ROWS = EXPERTS * TOKENS + P

QT_AT, UT_AT, O_AT, WO_AT, M_FILLS = 0, 2, 2 + 4 * GB, 4 + 4 * GB, 6 + 4 * GB
QK_PAIRS = 2 * KC
TP_FIRST, TP_FILLS = 4, 19
TP_AT = {}
for _kind, _b in (("ct", 1), ("pt", 0), ("ct", 2), ("pt", 1), ("ct", 3), ("pt", 2), ("ct", 4)):
    for _k in ((0, 2) if _kind == "pt" else (0, 1, 2)):
        TP_AT[_kind, _b, _k] = len(TP_AT)
TP_AT["xn"] = len(TP_AT)
YT_AT, KQ_AT, V_AT, SS_AT, PV_AT, WS_AT, YT2_AT, LG_AT, RK_AT, B_FILLS = 0, 1, 2, 3, 7, 8, 9, 10, 11, 12
RT_LINKS = 7


def at_least(eng, sem, n):
    if not isinstance(n, int) or n > 0:
        eng.wait_ge(sem, n)


def chain(eng, sem, before):
    count = [0]

    def link(instruction):
        count[0] += 1
        instruction.then_inc(sem, 1)
        eng.wait_ge(sem, before + count[0])

    return link


def perceiver_layer(nc, x, ctx_768, g_x, b_x, g_c, b_c, Wq, Wk, Wv, Wo, W_qkv, W_o,
                    gate_w, gate_b, w1, b1, w2, b2, ln_g, ln_b, out):
    with ExitStack() as stack:
        def sb(name, shape, dt=F32):
            return stack.enter_context(nc.sbuf_tensor(name, shape, dt))

        def sem(name):
            return stack.enter_context(nc.semaphore(name))

        xs_dram = nc.dram_tensor("xs_rows", (ROWS, DIM), F32).ap()
        ys_dram = nc.dram_tensor("ys_rows", (JOBS * P, DIM), F32).ap()

        moe_w = sb("moe_w", [P, 2, KD * FF + KF * DIM])
        moe_flat = moe_w[:, :, :].rearrange("p s n -> p (s n)")
        s0, s1 = moe_w[:, 0, :], moe_w[:, 1, :]
        qkT = s0[:, 0:6144].rearrange("p (c b r) -> p c b r", c=KC, b=GB)
        uT = s0[:, 6144:12288].rearrange("p (c h b t) -> p c h b t", c=KC, h=HEADS, b=GB)
        qT = s0[:, 12288:13312].rearrange("p (m t) -> p m t", m=KI)
        oT = qT
        cnT = s0[:, 13312:13312 + 2 * KC * KEYS].rearrange("p (s c j) -> p s c j", s=2, c=KC)
        n_high = s0[:, 14856:14856 + 3 * CTX].bitcast(F16).rearrange("p (s k c) -> p s k c", s=2, k=3)
        wk_rows = s0[:, 6144:9216].rearrange("p (c n) -> p c n", c=KC)
        qkv_rows = s0[:, 0:2048].rearrange("p (c n) -> p c n", c=KD)
        wos_rows = s0[:, 2048:4096].rearrange("p (c n) -> p c n", c=KD)
        wq = s1[:, 0:4096].rearrange("p (c n) -> p c n", c=KD)
        wkT = s1[:, 4096:7168].rearrange("p (m c) -> p m c", m=KI)
        wv = s1[:, 7168:10240].rearrange("p (c n) -> p c n", c=KC)
        wo = s1[:, 10240:14336].rearrange("p (m n) -> p m n", m=KI)
        wqkvT = s1[:, 14336:16384].rearrange("p (c n) -> p c n", c=KD)

        arena = sb("arena", [P, 8708])
        ctx = arena[:, 0:4608].rearrange("p (s k c) -> p s k c", s=GB, k=3)
        probs = arena[:, 4608:5636].rearrange("p (h j) -> p h j", h=HG)
        n_low = arena[:, 0:4608].bitcast(F16).rearrange("p (s k c) -> p s k c", s=GB, k=3)[:, :, :, 0:CTX]
        pT_high, pT_low = [arena[:, 5636 + 768 * i:5636 + 768 * (i + 1)].bitcast(F16).rearrange("p (k r) -> p k r", k=3)
                           for i in range(2)]
        xn = arena[:, 7172:7684]
        xnT = arena[:, 7684:8196].rearrange("p (c t) -> p c t", c=KD)
        y2 = arena[:, 8196:8708]
        b1_rows = arena[:, 0:4096]
        h_sb = arena[:, 4096:5120].rearrange("p (s f) -> p s f", s=2)
        hT_sb = arena[:, 5120:6144].rearrange("p (s c t) -> p s c t", s=2, c=KD)
        xs = arena[:, 6144:6656]
        xsT = arena[:, 6656:7168].rearrange("p (c t) -> p c t", c=KD)
        ys = arena[:, 7168:7680]

        x_all = sb("x_all", [P, GROUPS, DIM])
        wosT = sb("wosT", [P, KD, DIM])
        y = sb("y", [P, DIM])
        yT = sb("yT", [P, KD, P])
        kqT = sb("kqT", [P, KD, P])
        v_sb = sb("v_sb", [P, DIM])
        sS = sb("sS", [P, SHEADS, TOK])
        blocks = sb("blocks", [P, SHEADS, P])
        ident = sb("ident", [P, P])
        before = sb("before", [P, P])
        ones = sb("ones", [P, P])
        gate = sb("gate", [P, KD, EXPERTS])
        gcol = sb("gcol", [P, 2, KD])
        ccol = sb("ccol", [P, 2, KC])
        ugain = sb("ugain", [P, KC])
        gate_bias = sb("gate_bias", [P, EXPERTS])
        half = sb("half", [P, 8])
        stats = sb("stats", [P, 6])
        mv = sb("mv", [P, 2])
        rstd = sb("rstd", [P, 1])
        fin_mv = sb("fin_mv", [P, 2, 3])
        cstats = sb("cstats", [P, 3, 6])
        cmv = sb("cmv", [P, 3, 2])
        crstd = sb("crstd", [P, 3])
        mx = sb("mx", [P, HG])
        negm = sb("negm", [P, HG])
        rsum = sb("rsum", [P, HG])
        rinv = sb("rinv", [P, HG])
        smx = sb("smx", [P, SHEADS])
        ssum = sb("ssum", [P, SHEADS])
        logits = sb("logits", [P, EXPERTS])
        top = sb("top", [P, 8])
        topi = sb("topi", [P, 8], U32)
        topf = sb("topf", [P, TOPK])
        hot = sb("hot", [P, TOPK, EXPERTS])
        mask = sb("mask", [P, EXPERTS])
        rank = sb("rank", [P, EXPERTS])
        prod = sb("prod", [P, TOPK, EXPERTS])
        slotf = sb("slotf", [P, TOPK])
        slot_now = sb("slot_now", [P, TOPK], U32)
        next_row = sb("next_row", [P, EXPERTS])
        first_row = sb("first_row", [P, EXPERTS])
        topf_all = sb("topf_all", [P, GROUPS, TOPK])
        slotf_all = sb("slotf_all", [P, GROUPS, TOPK])
        slots = sb("slots", [P, GROUPS, TOPK], U32)
        gs = sb("gs", [P, GROUPS])

        late = blocks[:, :, :].rearrange("p h t -> p (h t)")
        late_used = [0]

        def late_f32(*shape):
            at, size = late_used[0], 1
            for n in shape:
                size *= n
            late_used[0] += size
            piece = late[:, at:at + size]
            names = "abc"[:len(shape)]
            return piece.rearrange(f"p ({' '.join(names)}) -> p {' '.join(names)}", **dict(zip(names, shape)))

        iota_e = sb("iota_e", [P, EXPERTS])
        iota_q = sb("iota_q", [P, TILES])
        iota_j = sb("iota_j", [P, 24])
        count = late_f32(EXPERTS)
        cmpq = late_f32(EXPERTS, TILES)
        tiles = late_f32(EXPERTS)
        spare = late_f32(EXPERTS)
        ends = late_f32(EXPERTS + 1)
        cmpj = late_f32(24, EXPERTS)
        skip = late_f32(24, EXPERTS)
        jobf = late_f32(24)
        rowf = late_f32(24)
        job_e = sb("job_e", [P, 24], I32)
        job_rows = sb("job_rows", [P, 24], I32)
        end_i = sb("end_i", [P, EXPERTS + 1], I32)
        hot_all = late_f32(GROUPS, TOPK, EXPERTS)
        shift = late_f32(EXPERTS)
        shift_all = late_f32(GROUPS, TOPK)
        by_choice = late_f32(GROUPS, TOPK, EXPERTS)
        gp = late_f32(GROUPS, TOPK)
        ge = late_f32(GROUPS)
        pe_all = late_f32(GROUPS, EXPERTS)
        zero1 = sb("zero1", [P, 1])
        pool_mark = sb("pool_mark", [P, 1])
        dve_mark = sb("dve_mark", [P, 1])
        pT8 = wosT[0:EXPERTS, 2:4, :].rearrange("e a (b n) -> e (a b) n", n=P)

        got = s0[:, 0:8192].rearrange("p (t k d) -> p t k d", t=GROUPS, k=TOPK)
        fin = s0[:, 8192:12288].rearrange("p (t d) -> p t d", t=GROUPS)
        lnrow = wosT[:, 0:2, :]
        diags = [[(y[:, :], yT[:, :, :].rearrange("p c t -> p (c t)"), kqT[:, :, :].rearrange("p c t -> p (c t)"),
                   v_sb[:, :])[t // 2][:, (2 * (t % 2) + k) * P:(2 * (t % 2) + k + 1) * P] for k in range(TOPK)] for t in range(GROUPS)]
        b2_sb = sS[0:EXPERTS, :, :].rearrange("e h t -> e (h t)")

        bank = [stack.enter_context(nc.psum_tensor(f"bank{i}", [P, 512], F32)) for i in range(8)]
        TP, M, BK = bank[4], [bank[5], bank[6]], bank[7]

        x0_in = sem("x0_in")
        x_in, wk_in, wq_in, wv_in, wo_in = sem("x_in"), sem("wk_in"), sem("wq_in"), sem("wv_in"), sem("wo_in")
        qkv_in, wos_in, cols_in, rows_in, gate_in = sem("qkv_in"), sem("wos_in"), sem("cols_in"), sem("rows_in"), sem("gate_in")
        ctx_in = [sem(f"ctx_in{b}") for b in range(GB)]
        xs_zeroed = sem("xs_zeroed")
        consts, ident_ok, zeros_ok, memset_ok = sem("consts"), sem("ident_ok"), sem("zeros_ok"), sem("memset_ok")
        setup_full, setup_free = sem("setup_full"), [sem(f"setup_free{i}") for i in range(2)]
        ln_step, ln_var, ln_rstd = sem("ln_step"), sem("ln_var"), sem("ln_rstd")
        cn_step, cn_var, cn_rstd, cn_done = sem("cn_step"), sem("cn_var"), sem("cn_rstd"), sem("cn_done")
        xn_done, y_done, x1_done, x2_done = sem("xn_done"), sem("y_done"), sem("x1_done"), sem("x2_done")
        tp_full, tp_free = sem("tp_full"), sem("tp_free")
        m_full, m_free = sem("m_full"), [sem(f"m_free{i}") for i in range(2)]
        qk_full, qk_out = sem("qk_full"), [sem(f"qk_out{i}") for i in range(2)]
        pt3_full, pt3_out = sem("pt3_full"), sem("pt3_out")
        n_high_done, n_low_done, p_high_done, ugain_ok = sem("n_high_done"), sem("n_low_done"), sem("p_high_done"), sem("ugain_ok")
        b_full, b_free = sem("b_full"), sem("b_free")
        s_full, max_done, neg_done, exp_done = sem("s_full"), sem("max_done"), sem("neg_done"), sem("exp_done")
        rinv_done, norm_done = sem("rinv_done"), sem("norm_done")
        ss_step, ss_ready, sexp_done, wb_done = sem("ss_step"), sem("ss_ready"), sem("sexp_done"), sem("wb_done")

        cmv_ok = sem("cmv_ok")
        slots_final = sem("slots_final")
        y2_free, rows_seen = sem("y2_free"), sem("rows_seen")
        rt_step, mask_done, exps_ready, gexp_done = sem("rt_step"), sem("mask_done"), sem("exps_ready"), sem("gexp_done")
        slots_ready, jobs_ready, scattered = sem("slots_ready"), sem("jobs_ready"), sem("scattered")
        experts_in = sem("experts_in")
        w_even, w_odd = sem("w_even"), sem("w_odd")
        xs_in, xt_full, xt_out = sem("xs_in"), sem("xt_full"), sem("xt_out")
        h_full, h_biased, h_act = sem("h_full"), sem("h_biased"), sem("h_act")
        hT_full, hT_out, mm2_done, ys_out, ys_stored = sem("hT_full"), sem("hT_out"), sem("mm2_done"), sem("ys_out"), sem("ys_stored")
        pw_ready, pw_full, pw_out, xb_done = sem("pw_ready"), sem("pw_full"), sem("pw_out"), sem("xb_done")
        diags_done = sem("diags_done")
        gathered = [sem(f"gathered{t}") for t in range(GROUPS)]
        mix_full, mix_used, fin_step, fin_var = sem("mix_full"), sem("mix_used"), sem("fin_step"), sem("fin_var")

        fin_rstd, fin_done, stored = sem("fin_rstd"), sem("fin_done"), sem("stored")

        block = stack.enter_context(nc.Block())

        ctx_rows = ctx_768.rearrange("b m c -> (b m) c")
        x_rows = x.rearrange("b t d -> (b t) d")
        out_rows = out.rearrange("b t d -> (b t) d")

        def ln_before(g):
            if isinstance(g, int):
                return 2 if g == 0 else 4 * g + 1 - (2 if g == GROUPS else 0)
            return 4 * g + 1

        def tp(g, at):
            return TP_FIRST + TP_FILLS * g + TP_AT[at]

        def ss_bank(g, hh):
            return bank[hh] if isinstance(g, int) and g == GROUPS - 1 else BK

        def ut_at(b, c):
            return UT_AT + 4 * b + 1 + c

        def pt_place(g, b, k):
            if k == 1:
                return M[0], m_full, M_FILLS * g + UT_AT + 4 * b + 1, m_free[0]
            if b < GB - 1:
                return TP, tp_full, tp(g, ("pt", b, k)) + 1, tp_free
            return bank[k], pt3_full, 2 * g + k // 2 + 1, pt3_out

        Y, XT = bank[4], bank[5]

        def expert_load(eng, e, slot, done):
            one = bass.ds(e, 1)
            eng.dma_start(moe_w[:, slot, 0:8192].rearrange("p (c f) -> p c f", c=KD),
                          w1[one, :, :].rearrange("e (c p) f -> p (e c) f", p=P)).then_inc(done, 16)
            eng.dma_start(moe_w[:, slot, 8192:16384].rearrange("p (c d) -> p c d", c=KF),
                          w2[one, :, :].rearrange("e (c p) d -> p (e c) d", p=P)).then_inc(done, 16)
            eng.dma_start(b1_rows[:, slot * FF:(slot + 1) * FF], b1[one, :].to_broadcast([P, FF])).then_inc(done, 16)

        def moe_loads(sp):
            sp.wait_ge(b_full, B_FILLS * GROUPS)
            sp.dma_start(lnrow[:, 0, :], ln_g.rearrange("(o d) -> o d", o=1).to_broadcast([P, DIM])).then_inc(rows_in, 16)
            sp.dma_start(lnrow[:, 1, :], ln_b.rearrange("(o d) -> o d", o=1).to_broadcast([P, DIM])).then_inc(rows_in, 16)
            sp.dma_start(b2_sb[:, :], b2[:, :]).then_inc(rows_in, 16)

            def rows_of(j):
                return sp.value_load(job_rows[0:1, bass.ds(j, 1)], min_val=0, max_val=ROWS // P - 1)

            def xs_load(j):
                sp.dma_start(xs, xs_dram[bass.ds(rows_of(j) * P, P), :]).then_inc(xs_in, 16)

            def ys_store(j):
                sp.wait_ge(ys_out, j + 1)
                sp.dma_start(ys_dram[bass.ds(j * P, P), :], ys).then_inc(ys_stored, 16)

            sp.wait_ge(jobs_ready, 1)
            sp.wait_ge(scattered, 16 * GROUPS * TOPK)
            xs_load(0)
            sp.wait_ge(xt_full, 1)
            xs_load(1)
            with sp.Fori(2, JOBS) as j:
                sp.wait_ge(xt_full, j)
                xs_load(j)
                ys_store(j - 2)
            ys_store(JOBS - 2)
            ys_store(JOBS - 1)
            for t in range(GROUPS):
                sp.wait_ge(fin_done, t + 1)
                sp.dma_start(out_rows[t * P:(t + 1) * P, :], fin[:, t, :]).then_inc(stored, 16)
            sp.wait_ge(stored, 16 * GROUPS)

        def expert_landed(pool, e, slot):
            if not isinstance(e, int) or e > 0:
                pool.wait_ge(experts_in, e)
            pool.wait_ge((w_even, w_odd)[slot], 48 * ((e - slot) // 2 + 1))
            nc.gpsimd.tensor_tensor(pool_mark[:, :], half[:, 0:1], half[:, 0:1], ALU.add).then_inc(experts_in, 1)

        def moe_pool(pool):
            pool.wait_ge(rows_seen, GROUPS)
            expert_landed(pool, 0, 0)
            pool.wait_ge(jobs_ready, 1)
            with pool.Fori(1, EXPERTS // 2) as i:
                for slot, done in ((0, w_even), (1, w_odd)):
                    e = 2 * i + slot
                    expert_landed(pool, e - 1, 1 - slot)
                    ended = pool.value_load(end_i[0:1, bass.ds(e - 1, 1)], min_val=1, max_val=1 + FB * JOBS)
                    pool.wait_ge(mm2_done, ended)
                    expert_load(pool, e, slot, done)
            expert_landed(pool, EXPERTS - 1, 1)
            pool.wait_ge(slots_final, 1)
            pool.wait_ge(ys_stored, 16 * JOBS)
            for t in range(GROUPS):
                for k in range(TOPK):
                    nc.gpsimd.indirect_dma_start(
                        out=got[:, t, k, :], out_offset=None, in_=ys_dram[:, :],
                        in_offset=bass.IndirectOffsetOnAxis(ap=slots[:, t, k:k + 1], axis=0)).then_inc(gathered[t], 16)
                if t >= 4:
                    fin_pow(pool, t - 4)
            for t in range(GROUPS - 4, GROUPS):
                fin_pow(pool, t)

        def fin_pow(pool, t):
            pool.wait_ge(fin_var, t + 1)
            nc.gpsimd.tensor_tensor(fin_mv[:, t % 2, 2:3], fin_mv[:, t % 2, 1:2], half[:, 0:1], ALU.pow).then_inc(fin_rstd, 1)

        def moe_act(act):
            act.wait_ge(exps_ready, 1)
            nc.scalar.activation(ge[:, :], gs[:, :], ACT.Exp).then_inc(gexp_done, 1)

            def xt_copy(j):
                act.wait_ge(xt_full, j + 1)
                if not isinstance(j, int) or j > 0:
                    act.wait_ge(h_full, FB * j)
                nc.scalar.copy(xsT.rearrange("p c t -> p (c t)"), XT[:, :]).then_inc(xt_out, 1)

            def gelu(j, fb):
                act.wait_ge(h_biased, FB * j + fb + 1)
                nc.scalar.activation(h_sb[:, fb % 2, :], h_sb[:, fb % 2, :], ACT.Gelu).then_inc(h_act, 1)

            xt_copy(0)
            with act.Fori(0, JOBS - 1) as j:
                for fb in range(FB):
                    gelu(j, fb)
                xt_copy(j + 1)
            for fb in range(FB):
                gelu(JOBS - 1, fb)

        def moe_dve(dve):
            dve.wait_ge(b_free, 1 + B_FILLS * GROUPS)
            link = chain(dve, rt_step, RT_LINKS * GROUPS)
            nc.vector.memset(ends[:, 0:1], 0.0).then_inc(exps_ready, 1)
            link(nc.vector.tensor_tensor(count[:, :], next_row[:, :], first_row[:, :], ALU.subtract))
            eq = [P, EXPERTS, TILES]
            link(nc.vector.tensor_tensor(cmpq[:, :, :], count[:, :].unsqueeze(2).to_broadcast(eq),
                                         iota_q[:, :].unsqueeze(1).to_broadcast(eq), ALU.is_gt))
            link(nc.vector.reduce_sum(tiles[:, :], cmpq[:, :, :], AX))
            nc.vector.tensor_scalar(spare[:, :], tiles[:, :], -1.0, float(TILES), ALU.mult, ALU.add)
            for e in range(EXPERTS):
                link(nc.vector.tensor_tensor(ends[:, e + 1:e + 2], ends[:, e:e + 1], tiles[:, e:e + 1], ALU.add))
            je = [P, 24, EXPERTS]
            link(nc.vector.tensor_tensor(cmpj[:, :, :], iota_j[:, :].unsqueeze(2).to_broadcast(je),
                                         ends[:, 1:EXPERTS + 1].unsqueeze(1).to_broadcast(je), ALU.is_ge))
            nc.vector.tensor_tensor(skip[:, :, :], cmpj[:, :, :], spare[:, :].unsqueeze(1).to_broadcast(je), ALU.mult)
            link(nc.vector.reduce_sum(jobf[:, :], cmpj[:, :, :], AX))
            link(nc.vector.reduce_sum(rowf[:, :], skip[:, :, :], AX))
            link(nc.vector.tensor_tensor(rowf[:, :], rowf[:, :], iota_j[:, :], ALU.add))
            nc.vector.tensor_scalar(end_i[:, :], ends[:, :], float(FB), 1.0, ALU.mult, ALU.add)
            nc.vector.tensor_scalar(job_e[:, :], jobf[:, :], float(EXPERTS - 1), None, ALU.min)
            link(nc.vector.tensor_scalar(job_rows[:, :], rowf[:, :], float(EXPERTS * TILES), None, ALU.min))
            nc.vector.memset(zero1[:, :], 0.0).then_inc(jobs_ready, 1)
            dve.wait_ge(gexp_done, 1)
            te = [P, GROUPS, EXPERTS]
            link(nc.vector.tensor_scalar(gs[:, :], ge[:, :], 1.0, None, ALU.add))
            tk = [P, GROUPS * TOPK, EXPERTS]
            nc.vector.tensor_tensor(hot_all[:, :, :, :].rearrange("p t k e -> p (t k) e"),
                                    iota_e[:, :].unsqueeze(1).to_broadcast(tk),
                                    topf_all[:, :, :].rearrange("p t k -> p (t k)").unsqueeze(2).to_broadcast(tk), ALU.is_equal)
            link(nc.vector.reciprocal(gp[:, :, 0], gs[:, :]))
            link(nc.vector.scalar_tensor_tensor(out=shift[:, :], in0=ends[:, 0:EXPERTS], scalar=float(P), in1=first_row[:, :],
                                                op0=ALU.mult, op1=ALU.subtract))
            link(nc.vector.tensor_tensor(by_choice[:, :, :, :].rearrange("p t k e -> p (t k) e"),
                                         hot_all[:, :, :, :].rearrange("p t k e -> p (t k) e"),
                                         shift[:, :].unsqueeze(1).to_broadcast(tk), ALU.mult))
            link(nc.vector.reduce_sum(shift_all[:, :, :], by_choice[:, :, :, :], AX))
            nc.vector.tensor_tensor(slots[:, :, :], slotf_all[:, :, :], shift_all[:, :, :], ALU.add).then_inc(slots_final, 1)
            link(nc.vector.tensor_tensor(gp[:, :, 1], ge[:, :], gp[:, :, 0], ALU.mult))
            for k in range(TOPK):
                last = nc.vector.tensor_tensor(by_choice[:, :, k, :], hot_all[:, :, k, :],
                                               gp[:, :, k:k + 1].to_broadcast(te), ALU.mult)
            link(last)
            nc.vector.tensor_tensor(pe_all[:, :, :], by_choice[:, :, 0, :], by_choice[:, :, 1, :], ALU.add).then_inc(pw_ready, 1)
            def bias(j, fb, slot):
                dve.wait_ge(h_full, FB * j + fb + 1)
                if fb >= 2 or not isinstance(j, int) or j > 0:
                    dve.wait_ge(hT_full, FB * j + fb - 1)
                nc.vector.tensor_tensor(h_sb[:, fb % 2, :], bank[fb % 2][:, :],
                                        b1_rows[:, bass.ds(slot * FF + fb * 512, 512)], ALU.add).then_inc(h_biased, 1)

            def hT_copy(j, fb):
                dve.wait_ge(hT_full, FB * j + fb + 1)
                if fb >= 2 or not isinstance(j, int) or j > 0:
                    dve.wait_ge(mm2_done, 1 + FB * j + fb - 1)
                nc.vector.tensor_copy(hT_sb[:, fb % 2, :, :].rearrange("p c t -> p (c t)"), bank[2 + fb % 2][:, :]).then_inc(hT_out, 1)

            def y_copy(j):
                dve.wait_ge(mm2_done, 1 + FB * (j + 1))
                if not isinstance(j, int) or j > 0:
                    dve.wait_ge(ys_stored, 16 * j)
                nc.vector.tensor_copy(ys, Y[:, :]).then_inc(ys_out, 1)

            def job(j, first):
                slot = dve.value_load(job_e[0:1, bass.ds(j, 1)], min_val=0, max_val=EXPERTS - 1) % 2
                bias(j, 0, slot)
                if not first:
                    hT_copy(j - 1, 3)
                bias(j, 1, slot)
                hT_copy(j, 0)
                if not first:
                    y_copy(j - 1)
                bias(j, 2, slot)
                hT_copy(j, 1)
                bias(j, 3, slot)
                hT_copy(j, 2)

            job(0, True)
            dve.wait_ge(rows_in, 48)
            for t in range(GROUPS):
                last = nc.vector.tensor_tensor(x_all[:, t, :], x_all[:, t, :], lnrow[:, 1, :], ALU.add)
            last.then_inc(xb_done, 1)
            job(1, False)
            for t in range(GROUPS):
                for k in range(TOPK):
                    last = nc.vector.tensor_scalar(diags[t][k], ident[:, :], gp[:, t, k:k + 1], None, ALU.mult)
            last.then_inc(diags_done, 1)
            with dve.Fori(2, JOBS) as j:
                job(j, False)
            hT_copy(JOBS - 1, 3)
            y_copy(JOBS - 1)

            dve.wait_ge(pw_full, 1)
            for i in range(2):
                last = nc.vector.tensor_copy(pT8[:, 4 * i:4 * i + 4, :].rearrange("e t n -> e (t n)"), bank[2 + i][0:EXPERTS, :])
            last.then_inc(pw_out, 1)
            dve.wait_ge(xb_done, 1)
            link = chain(dve, fin_step, 0)

            def fin_out(t):
                dve.wait_ge(mix_used, t + 1)
                dve.wait_ge(fin_rstd, t + 1)
                nc.vector.scalar_tensor_tensor(out=fin[:, t, :], in0=fin[:, t, :], scalar=fin_mv[:, t % 2, 2:3], in1=x_all[:, t, :],
                                               op0=ALU.mult, op1=ALU.add).then_inc(fin_done, 1)

            for t in range(GROUPS):
                mixed, m = bank[t], fin_mv[:, t % 2]
                dve.wait_ge(mix_full, t + 1)
                link(nc.vector.bn_stats(stats[:, :], mixed[:, :]))
                link(nc.vector.bn_aggr(m[:, 0:2], stats[:, :]))
                nc.vector.tensor_scalar(m[:, 1:2], m[:, 1:2], EPS, None, ALU.add).then_inc(fin_var, 1)
                if t > 0:
                    fin_out(t - 1)
                nc.vector.scalar_tensor_tensor(out=fin[:, t, :], in0=mixed[:, :], scalar=m[:, 0:1], in1=lnrow[:, 0, :],
                                               op0=ALU.subtract, op1=ALU.mult).then_inc(mix_used, 1)
            fin_out(GROUPS - 1)

        def moe_pe(pe):
            def xt_fill(j):
                pe.wait_ge(xs_in, 16 * (j + 1))
                if not isinstance(j, int) or j > 0:
                    pe.wait_ge(xt_out, j)
                for c in range(KD):
                    last = nc.tensor.transpose(XT[:, c * P:(c + 1) * P], xs[:, c * P:(c + 1) * P], ident[:, :])
                    if c == 0 and isinstance(j, int) and j == 0:
                        last.then_inc(mm2_done, 1)
                last.then_inc(xt_full, 1)

            def mm1(j, fb, e):
                if fb == 0:
                    pe.wait_ge(xt_out, j + 1)
                    pe.wait_ge(experts_in, e + 1)
                if fb >= 2 or not isinstance(j, int) or j > 0:
                    pe.wait_ge(h_biased, FB * j + fb - 1)
                for k in range(KD):
                    last = nc.tensor.matmul(bank[fb % 2][:, :], xsT[:, k, :],
                                            moe_flat[:, bass.ds((e % 2) * 16384 + k * FF + fb * 512, 512)],
                                            start=(k == 0), stop=(k == KD - 1))
                last.then_inc(h_full, 1)

            def hT_fill(j, fb):
                pe.wait_ge(h_act, FB * j + fb + 1)
                if fb >= 2 or not isinstance(j, int) or j > 0:
                    pe.wait_ge(hT_out, FB * j + fb - 1)
                for c in range(4):
                    last = nc.tensor.transpose(bank[2 + fb % 2][:, c * P:(c + 1) * P], h_sb[:, fb % 2, c * P:(c + 1) * P], ident[:, :])
                last.then_inc(hT_full, 1)

            def mm2(j, fb, e):
                pe.wait_ge(hT_out, FB * j + fb + 1)
                if fb == 0 and (not isinstance(j, int) or j > 0):
                    pe.wait_ge(ys_out, j)
                for c in range(4):
                    last = nc.tensor.matmul(Y[:, :], hT_sb[:, fb % 2, c, :],
                                            moe_flat[:, bass.ds((e % 2) * 16384 + 8192 + (4 * fb + c) * DIM, DIM)],
                                            start=(fb == 0 and c == 0), stop=(fb == 3 and c == 3))
                last.then_inc(mm2_done, 1)

            def job(j, first, last):
                e = pe.value_load(job_e[0:1, bass.ds(j, 1)], min_val=0, max_val=EXPERTS - 1)
                mm1(j, 0, e)
                if not first:
                    before_e = pe.value_load(job_e[0:1, bass.ds(j - 1, 1)], min_val=0, max_val=EXPERTS - 1)
                    hT_fill(j - 1, 3)
                    mm2(j - 1, 2, before_e)
                mm1(j, 1, e)
                hT_fill(j, 0)
                if not first:
                    mm2(j - 1, 3, before_e)
                mm1(j, 2, e)
                hT_fill(j, 1)
                mm2(j, 0, e)
                mm1(j, 3, e)
                if not last:
                    xt_fill(j + 1)
                hT_fill(j, 2)
                mm2(j, 1, e)
                return e

            pe.wait_ge(jobs_ready, 1)
            xt_fill(0)
            job(0, True, False)
            with pe.Fori(1, JOBS - 1) as j:
                job(j, False, False)
            e = job(JOBS - 1, False, True)
            hT_fill(JOBS - 1, 3)
            mm2(JOBS - 1, 2, e)
            mm2(JOBS - 1, 3, e)
            pe.wait_ge(rows_in, 48)
            pe.wait_ge(h_biased, FB * JOBS)
            pe.wait_ge(hT_out, FB * JOBS)
            pe.wait_ge(pw_ready, 1)
            for t in range(GROUPS):
                last = nc.tensor.transpose(bank[2 + t // 4][0:EXPERTS, (t % 4) * P:(t % 4 + 1) * P], pe_all[:, t, :], ident[:, :])
            last.then_inc(pw_full, 1)
            pe.wait_ge(pw_out, 1)
            pe.wait_ge(diags_done, 1)
            pe.wait_ge(ys_out, JOBS)
            for t in range(GROUPS):
                nc.tensor.matmul(bank[t][:, :], pT8[:, t, :], b2_sb[:, :], start=True, stop=False)
            for t in range(GROUPS):
                pe.wait_ge(gathered[t], 16 * TOPK)
                nc.tensor.matmul(bank[t][:, :], diags[t][0], got[:, t, 0, :], start=False, stop=False)
                nc.tensor.matmul(bank[t][:, :], diags[t][1], got[:, t, 1, :], start=False, stop=True).then_inc(mix_full, 1)

        def ctx_load(sp, g, b):
            row = (g * GB + b) * KEYS
            sp.dma_start(ctx[0:85, b, :, :].rearrange("p k c -> p (k c)"),
                         ctx_rows[bass.ds(row, 255), :].rearrange("(p k) c -> p (k c)", k=3)).then_inc(ctx_in[b], 16)
            sp.dma_start(ctx[85:86, b, 0:2, :].rearrange("p k c -> p (k c)"),
                         ctx_rows[bass.ds(row + 255, 2), :].rearrange("(p k) c -> p (k c)", k=2)).then_inc(ctx_in[b], 16)

        @block.sync
        def _(sp):
            def zero_rows(e):
                n = TILES if e < EXPERTS else 1
                sp.dma_start(xs_dram[e * TOKENS:e * TOKENS + n * P, :].rearrange("(j p) d -> p j d", p=P),
                             blocks[:, 0:4, :].rearrange("p h t -> p (h t)").unsqueeze(1).to_broadcast([P, n, DIM])).then_inc(xs_zeroed, 16)

            sp.dma_start(x_all[:, 0, :], x_rows[0:P, :]).then_inc(x0_in, 16)
            sp.dma_start(wq, Wq.rearrange("(c p) n -> p c n", p=P)).then_inc(wq_in, 16)
            ctx_load(sp, 0, 0)
            sp.dma_start(wk_rows, Wk.rearrange("(c p) n -> p c n", p=P)).then_inc(wk_in, 16)
            sp.dma_start(qkv_rows, W_qkv.rearrange("(c p) n -> p c n", p=P)).then_inc(qkv_in, 16)
            sp.dma_start(wos_rows, W_o.rearrange("(c p) n -> p c n", p=P)).then_inc(wos_in, 16)
            ctx_load(sp, 0, 1)
            ctx_load(sp, 0, 2)
            sp.dma_start(x_all[:, 1:GROUPS, :],
                         x_rows[P:, :].rearrange("(g p) d -> p g d", p=P)).then_inc(x_in, 16)
            ctx_load(sp, 0, 3)
            sp.dma_start(wv, Wv.rearrange("(c p) n -> p c n", p=P)).then_inc(wv_in, 16)
            sp.dma_start(wo, Wo.rearrange("(m p) n -> p m n", p=P)).then_inc(wo_in, 16)
            sp.dma_start(gate[:, :, :], gate_w.rearrange("(c p) e -> p c e", p=P)).then_inc(gate_in, 16)
            sp.dma_start(gate_bias[:, :], gate_b.rearrange("(o e) -> o e", o=1).to_broadcast([P, EXPERTS])).then_inc(gate_in, 16)
            sp.wait_ge(zeros_ok, 1)
            for e in range(ZERO_FIRST):
                zero_rows(e)
            for b in range(GB):
                sp.wait_ge(m_full, ut_at(b, 2) + 1)
                ctx_load(sp, 1, b)
                for e in range(ZERO_FIRST + 2 * b, min(ZERO_FIRST + 2 * b + 2, EXPERTS + 1)):
                    zero_rows(e)
            with sp.Fori(2, GROUPS) as g:
                for b in range(GB):
                    sp.wait_ge(m_full, M_FILLS * (g - 1) + ut_at(b, 2) + 1)
                    ctx_load(sp, g, b)
            moe_loads(sp)

        @block.gpsimd
        def _(pool):
            nc.gpsimd.memset(ones[:, :], 1.0).then_inc(memset_ok, 1)
            nc.gpsimd.memset(half[:, :], -0.5).then_inc(memset_ok, 1)
            pool.wait_ge(memset_ok, 2)
            nc.gpsimd.affine_select(out=ident[:, :], in_=ones[:, :], compare_op=ALU.is_equal, fill=0.0, base=0,
                                    pattern=[[-1, P]], channel_multiplier=1).then_inc(ident_ok, 1)
            nc.gpsimd.affine_select(out=before[:, :], in_=ones[:, :], compare_op=ALU.is_gt, fill=0.0, base=0,
                                    pattern=[[1, P]], channel_multiplier=-1).then_inc(consts, 1)
            nc.gpsimd.iota(iota_e[:, :], pattern=[[1, EXPERTS]], base=0, channel_multiplier=0,
                           allow_small_or_imprecise_dtypes=True).then_inc(consts, 1)
            for rows in (first_row, next_row):
                nc.gpsimd.iota(rows[:, :], pattern=[[TOKENS, EXPERTS]], base=0, channel_multiplier=0,
                               allow_small_or_imprecise_dtypes=True).then_inc(consts, 1)
            nc.gpsimd.iota(iota_q[:, :], pattern=[[P, TILES]], base=0, channel_multiplier=0,
                           allow_small_or_imprecise_dtypes=True).then_inc(consts, 1)
            nc.gpsimd.iota(iota_j[:, :], pattern=[[1, 24]], base=0, channel_multiplier=0,
                           allow_small_or_imprecise_dtypes=True).then_inc(consts, 1)

            def ln_pow(n):
                pool.wait_ge(ln_var, n + 1)
                nc.gpsimd.tensor_tensor(rstd[:, :], mv[:, 1:2], half[:, 0:1], ALU.pow).then_inc(ln_rstd, 1)

            def cn_pow(n):
                pool.wait_ge(cn_var, n + 1)
                nc.gpsimd.tensor_tensor(crstd[0:86, :], cmv[0:86, :, 1], half[0:86, 0:3], ALU.pow).then_inc(cn_rstd, 1)

            def body(g, do_a, do_b, nxt):
                ln = ln_before(g)
                if nxt:
                    ln_pow(ln)
                if do_b:
                    mark_free(g - 1)
                if isinstance(g, int) and g == 0:
                    cn_pow(2)
                if do_a:
                    cn_pow(GB * g + 3)
                if nxt:
                    cn_pow(GB * g + 4)
                    cn_pow(GB * g + 5)
                    cn_pow(GB * g + 6)
                    ln_pow(ln + 1)
                    ln = ln + 2
                if do_b:
                    ln_pow(ln)
                    ln = ln + 1
                if do_a:
                    ln_pow(ln)
                if do_b:
                    scatter(g - 1)

            def mark_free(n):
                if not isinstance(n, int) or n > 0:
                    pool.wait_ge(scattered, 16 * TOPK * n)
                    pool.wait_ge(rows_seen, n)
                nc.gpsimd.tensor_tensor(pool_mark[:, :], half[:, 0:1], half[:, 0:1], ALU.add).then_inc(y2_free, 1)

            def scatter(g):
                pool.wait_ge(slots_ready, g + 1)
                nc.gpsimd.tensor_tensor(pool_mark[:, :], half[:, 0:1], half[:, 0:1], ALU.add).then_inc(rows_seen, 1)
                for k in range(TOPK):
                    nc.gpsimd.indirect_dma_start(
                        out=xs_dram[:, :], out_offset=bass.IndirectOffsetOnAxis(ap=slot_now[:, k:k + 1], axis=0),
                        in_=y2[:, :], in_offset=None).then_inc(scattered, 16)

            ln_pow(0)
            ln_pow(1)
            cn_pow(0)
            cn_pow(1)
            body(0, True, False, True)
            pool.wait_ge(xs_zeroed, 16 * (EXPERTS + 1))
            body(1, True, True, True)
            with pool.Fori(2, GROUPS - 1) as g:
                body(g, True, True, True)
            body(GROUPS - 1, True, True, False)
            pool.wait_ge(m_full, M_FILLS * GROUPS)
            expert_load(pool, 0, 0, w_even)
            mark_free(GROUPS - 1)
            ln_pow(ln_before(GROUPS))
            scatter(GROUPS - 1)
            pool.wait_ge(b_full, B_FILLS * (GROUPS - 1) + KQ_AT + 1)
            pool.wait_ge(xs_in, 16)
            expert_load(pool, 1, 1, w_odd)
            moe_pool(pool)

        def setup_out(eng, copy, n):
            dst = (wkT[:, n, :] if n < 8 else wqkvT[:, n - 8, :] if n < 12 else wosT[:, n - 12, :])
            eng.wait_ge(setup_full, n + 1)
            copy(dst, bank[n % 4][:, 0:dst.shape[1]]).then_inc(setup_free[n % 2], 1)

        def qk_copy(eng, copy, g, i, par):
            hq, c = i // KC, i % KC
            dst = qkT[:, c, :, :].rearrange("p b (h two t) -> p h two b t", two=2, t=TOK)[:, 4 * hq:4 * hq + 4, par]
            eng.wait_ge(qk_full, 2 * QK_PAIRS * g + 2 * i + par + 1)
            copy(dst, bank[(2 * i + par) % 4][:, :].rearrange("p (h b t) -> p h b t", h=4, b=GB)).then_inc(qk_out[par], 1)

        @block.scalar
        def _(act):
            with nc.allow_non_contiguous_dma(reason="a few columns"):
                act.dma_start(gcol[:, 0, :], g_x.rearrange("(c p) -> p c", p=P)).then_inc(cols_in, 16)
                act.dma_start(gcol[:, 1, :], b_x.rearrange("(c p) -> p c", p=P)).then_inc(cols_in, 16)
                act.dma_start(ccol[:, 0, :], g_c.rearrange("(c p) -> p c", p=P)).then_inc(cols_in, 16)
                act.dma_start(ccol[:, 1, :], b_c.rearrange("(c p) -> p c", p=P)).then_inc(cols_in, 16)
            act.wait_ge(cols_in, 64)
            nc.scalar.activation(ugain[:, :], ccol[:, 0, :], ACT.Identity, scale=1.0 / (N_SCALE * P_SCALE)).then_inc(ugain_ok, 1)

            def xn_out(n):
                act.wait_ge(tp_full, n + 1)
                for c in range(KD):
                    last = nc.scalar.activation(xnT[:, c, :], TP[:, c * P:(c + 1) * P], ACT.Identity,
                                                bias=gcol[:, 1, c:c + 1], scale=gcol[:, 0, c:c + 1])
                last.then_inc(tp_free, 1)

            def ct_out(n, b, c):
                act.wait_ge(tp_full, n + 1)
                nc.scalar.activation(cnT[:, b % 2, c, :], TP[:, 0:KEYS], ACT.Identity,
                                     bias=ccol[:, 1, c:c + 1], scale=ccol[:, 0, c:c + 1]).then_inc(tp_free, 1)

            def m_copy(g, at, dst, src):
                act.wait_ge(m_full, M_FILLS * g + at + 1)
                nc.scalar.copy(dst, src).then_inc(m_free[at % 2], 1)

            def exps(g, b):
                bt = GB * g + b
                for h in range(HG):
                    act.wait_ge(neg_done, HG * bt + h + 1)
                    nc.scalar.activation(probs[:, h, :], bank[h][:, 0:KEYS], ACT.Exp, bias=negm[:, h:h + 1],
                                         scale=XSCALE, accum_out=rsum[:, h:h + 1]).then_inc(exp_done, 1)

            def ut_out(g, b, c):
                at = ut_at(b, c)
                act.wait_ge(m_full, M_FILLS * g + at + 1)
                nc.scalar.activation(uT[:, c, :, b, :], M[at % 2][:, :].rearrange("p (h t) -> p h t", t=TOK), ACT.Identity,
                                     bias=ccol[:, 1, c:c + 1], scale=ugain[:, c:c + 1]).then_inc(m_free[at % 2], 1)

            def n_hi(g, b):
                act.wait_ge(cn_done, GB * g + b + 1)
                for k in range(3):
                    last = nc.scalar.activation(n_high[0:PART[k], b % 2, k, :], ctx[0:PART[k], b, k, :], ACT.Identity, scale=N_SCALE)
                last.then_inc(n_high_done, 1)

            def pt_hi(g, b, k):
                src, full, count, _ = pt_place(g, b, k)
                act.wait_ge(full, count)
                nc.scalar.copy(pT_high[0:PART[k], k, :], src[0:PART[k], :]).then_inc(p_high_done, 1)

            def b_copy(g, at, dst):
                act.wait_ge(b_full, B_FILLS * g + at + 1)
                nc.scalar.copy(dst, BK[:, :]).then_inc(b_free, 1)

            def body(g, do_a, do_b, nxt):
                if do_a:
                    m_copy(g, QT_AT + 1, qT[:, 4:8, :].rearrange("p m t -> p (m t)"), M[1][:, :])
                if isinstance(g, int) and g == 0:
                    for n in range(1, 16, 2):
                        if n == 9:
                            for c in range(KC):
                                ct_out(1 + c, 0, c)
                        setup_out(act, nc.scalar.copy, n)
                for i in range(QK_PAIRS):
                    if do_a:
                        qk_copy(act, nc.scalar.copy, g, i, 1)
                    if i == 3 and do_b:
                        b_copy(g - 1, KQ_AT, kqT[:, :, :].rearrange("p c t -> p (c t)"))
                if do_b:
                    b_copy(g - 1, V_AT, v_sb[:, :])
                for b in range(GB + 1):
                    if do_a:
                        if b < GB:
                            n_hi(g, b)
                        for k in range(3):
                            if b == 0:
                                ct_out(tp(g, ("ct", 1, k)), 1, k)
                            else:
                                pt_hi(g, b - 1, k)
                        if b < GB:
                            exps(g, b)
                    for c in range(KC):
                        if do_a:
                            if 1 <= b < 3 or (b == GB and nxt):
                                nb = b + 1 if b < GB else GB
                                ct_out(tp(g, ("ct", nb, c)), nb, c)
                            if b >= 1:
                                ut_out(g, b - 1, c)
                        if do_b and b == GB and c == 1:
                            b_copy(g - 1, PV_AT, kqT[:, :, :].rearrange("p c t -> p (c t)"))
                    if do_b and b == 2:
                        act.wait_ge(ss_ready, g)
                        nc.scalar.activation(sS[:, :, :], sS[:, :, :], ACT.Exp, scale=SSCALE).then_inc(sexp_done, 1)
                if do_a:
                    m_copy(g, O_AT + 1, oT[:, 4:8, :].rearrange("p m t -> p (m t)"), M[1][:, :])
                if nxt:
                    xn_out(tp(g, "xn"))

            xn_out(0)
            body(0, True, False, True)
            with act.Fori(1, GROUPS - 1) as g:
                body(g, True, True, True)
            body(GROUPS - 1, True, True, False)
            body(GROUPS, False, True, False)
            moe_act(act)

        @block.vector
        def _(dve):
            nc.vector.memset(blocks[:, :, :], 0.0).then_inc(zeros_ok, 1)
            nc.vector.memset(cmv[:, :, :], 1.0).then_inc(cmv_ok, 1)
            nc.vector.memset(dve_mark[:, :], 0.0).then_inc(b_free, 1)
            dve.wait_ge(cmv_ok, 1)

            def carry_wait():
                nc.vector.memset(zero1[:, :], 0.0)

            def layernorm(n, src, dst, done):
                link = chain(dve, ln_step, 2 * n)
                carry_wait()
                link(nc.vector.bn_stats(stats[:, :], src))
                carry_wait()
                link(nc.vector.bn_aggr(mv[:, :], stats[:, :]))
                nc.vector.tensor_scalar(mv[:, 1:2], mv[:, 1:2], EPS, None, ALU.add).then_inc(ln_var, 1)
                dve.wait_ge(ln_rstd, n + 1)
                nc.vector.tensor_scalar(dst, src, mv[:, 0:1], rstd[:, 0:1], ALU.subtract, ALU.mult).then_inc(done, 1)

            def xn_norm(n, g, second):
                if second:
                    dve.wait_ge(xn_done, 2 * g + 1)
                    layernorm(n, xn, xn, xn_done)
                else:
                    layernorm(n, x_all[:, bass.ds(g, 1), :].rearrange("p g d -> p (g d)"), xn, xn_done)

            def cn_stats(g, b):
                bt, slot = GB * g + b, b % GB
                dve.wait_ge(ctx_in[slot], 32 * (g + b // GB + 1))
                for k in range(3):
                    last = nc.vector.bn_stats(cstats[0:PART[k], k, :], ctx[0:PART[k], slot, k, :])
                link = chain(dve, cn_step, 2 * bt)
                link(last)
                carry_wait()
                for k in range(3):
                    last = nc.vector.bn_aggr(cmv[0:PART[k], k, :], cstats[0:PART[k], k, :])
                link(last)
                nc.vector.tensor_scalar(cmv[0:86, :, 1], cmv[0:86, :, 1], EPS, None, ALU.add).then_inc(cn_var, 1)

            def cn_apply(g, b):
                bt, slot = GB * g + b, b % GB
                dve.wait_ge(cn_rstd, bt + 1)
                for k in range(3):
                    c = ctx[0:PART[k], slot, k, :]
                    last = nc.vector.tensor_scalar(c, c, cmv[0:PART[k], k, 0:1], crstd[0:PART[k], k:k + 1],
                                                   ALU.subtract, ALU.mult)
                last.then_inc(cn_done, 1)

            def m_copy(g, at, dst, src):
                dve.wait_ge(m_full, M_FILLS * g + at + 1)
                nc.vector.tensor_copy(dst, src).then_inc(m_free[at % 2], 1)

            def b_copy(g, at, dst, src=BK[:, :]):
                dve.wait_ge(b_full, B_FILLS * g + at + 1)
                nc.vector.tensor_copy(dst, src).then_inc(b_free, 1)

            def row_max(g, b, h):
                n = HG * (GB * g + b) + h
                dve.wait_ge(s_full, n + 1)
                nc.vector.reduce_max(mx[:, h:h + 1], bank[h][:, 0:KEYS], AX).then_inc(max_done, 1)
                dve.wait_ge(max_done, n + 1)
                nc.vector.tensor_scalar(negm[:, h:h + 1], mx[:, h:h + 1], -XSCALE, None, ALU.mult).then_inc(neg_done, 1)

            def norm_probs(g, b):
                bt = GB * g + b
                dve.wait_ge(exp_done, HG * (bt + 1))
                nc.vector.reciprocal(rinv[:, :], rsum[:, :]).then_inc(rinv_done, 1)
                dve.wait_ge(rinv_done, bt + 1)
                for h in range(HG):
                    last = nc.vector.tensor_scalar(probs[:, h, :], probs[:, h, :], rinv[:, h:h + 1], P_SCALE, ALU.mult, ALU.mult)
                last.then_inc(norm_done, 1)

            def pt_lo(g, b, k):
                dve.wait_ge(p_high_done, 3 * (GB * g + b) + k + 1)
                src, _, _, emptied = pt_place(g, b, k)
                nc.vector.tensor_tensor(pT_low[0:PART[k], k, :], src[0:PART[k], :], pT_high[0:PART[k], k, :],
                                        ALU.subtract).then_inc(emptied, 1)

            def n_lo(g, b):
                dve.wait_ge(n_high_done, GB * g + b + 1)
                for k in range(3):
                    last = nc.vector.scalar_tensor_tensor(out=n_low[0:PART[k], b, k, :], in0=ctx[0:PART[k], b, k, :],
                                                          scalar=N_SCALE, in1=n_high[0:PART[k], b % 2, k, :],
                                                          op0=ALU.mult, op1=ALU.subtract)
                last.then_inc(n_low_done, 1)

            def ss_out(g, hh):
                src = ss_bank(g, hh)
                dve.wait_ge(b_full, B_FILLS * g + SS_AT + hh + 1)
                for q in range(GB):
                    rows = slice(TOK * q, TOK * (q + 1))
                    last = nc.vector.tensor_copy(
                        sS[rows, :, :].rearrange("p (m h) j -> p m h j", h=4)[:, :, hh, :],
                        src[rows, :].rearrange("p (m j) -> p m j", m=4)[:, :, TOK * q:TOK * (q + 1)])
                last.then_inc(b_free, 1)

            def ss_sub(g):
                dve.wait_ge(b_free, 1 + B_FILLS * g + SS_AT + 4)
                link = chain(dve, ss_step, 4 * g)
                link(nc.vector.tensor_reduce(smx[:, :], sS[:, :, :], AX, ALU.max))
                nc.vector.tensor_tensor(sS[:, :, :], sS[:, :, :], smx[:, :].unsqueeze(2).to_broadcast([P, SHEADS, TOK]),
                                        ALU.subtract).then_inc(ss_ready, 1)

            def ss_norm(g):
                dve.wait_ge(sexp_done, g + 1)
                link = chain(dve, ss_step, 4 * g + 1)
                link(nc.vector.reduce_sum(ssum[:, :], sS[:, :, :], AX))
                link(nc.vector.reciprocal(ssum[:, :], ssum[:, :]))
                link(nc.vector.tensor_tensor(sS[:, :, :], sS[:, :, :], ssum[:, :].unsqueeze(2).to_broadcast([P, SHEADS, TOK]),
                                             ALU.mult))
                for q in range(GB):
                    rows = slice(TOK * q, TOK * (q + 1))
                    last = nc.vector.transpose(blocks[rows, :, TOK * q:TOK * (q + 1)], sS[rows, :, :])
                last.then_inc(wb_done, 1)

            def body(g, do_a, do_b, nxt):
                ln = ln_before(g)
                x_prev = x_all[:, bass.ds(g - 1, 1), :].rearrange("p g d -> p (g d)") if do_b else None
                if do_a:
                    m_copy(g, QT_AT, qT[:, 0:4, :].rearrange("p m t -> p (m t)"), M[0][:, :])
                if isinstance(g, int) and g == 0:
                    for n in range(0, 16, 2):
                        setup_out(dve, nc.vector.tensor_copy, n)
                    cn_stats(0, 1)
                    cn_apply(0, 1)
                for i in range(QK_PAIRS):
                    if do_a:
                        qk_copy(dve, nc.vector.tensor_copy, g, i, 0)
                    if i == 1 and do_b:
                        b_copy(g - 1, YT_AT, yT[:, :, :].rearrange("p c t -> p (c t)"))
                if isinstance(g, int) and g == 0:
                    dve.wait_ge(x_in, 16)
                if nxt:
                    xn_norm(ln, g + 1, 0)
                if do_a:
                    n_lo(g, 0)
                for b in range(GB):
                    ahead = (do_a and b == 1) or (nxt and b >= 2)
                    if do_a:
                        for k in range(HG):
                            if b >= 1 and k < 3:
                                pt_lo(g, b - 1, k)
                            row_max(g, b, k)
                    if do_b and b == 2:
                        ss_out(g - 1, 3)
                    if do_a and b > 0:
                        n_lo(g, b)
                    if ahead:
                        cn_stats(g, b + 2)
                    if do_b and b == 1:
                        ss_out(g - 1, 1)
                    if do_a:
                        norm_probs(g, b)
                    if do_b and b == 0:
                        ss_out(g - 1, 0)
                    if ahead:
                        cn_apply(g, b + 2)
                    if isinstance(g, int) and g == 0 and b == 0:
                        cn_stats(0, 2)
                        cn_apply(0, 2)
                    if do_b and b == 1:
                        ss_out(g - 1, 2)
                    if do_b and b == 2:
                        ss_sub(g - 1)
                if do_a:
                    for k in range(3):
                        pt_lo(g, GB - 1, k)
                if do_b:
                    ss_norm(g - 1)
                if nxt:
                    cn_stats(g, 6)
                    cn_apply(g, 6)
                    xn_norm(ln + 1, g + 1, 1)
                    ln = ln + 2
                if do_b:
                    dve.wait_ge(b_full, B_FILLS * (g - 1) + WS_AT + 1)
                    nc.vector.tensor_tensor(x_prev, x_prev, BK[:, :], ALU.add).then_inc(b_free, 1)
                    dve.wait_ge(b_free, 1 + B_FILLS * (g - 1) + WS_AT + 1)
                    dve.wait_ge(y2_free, g)
                    layernorm(ln, x_prev, y2[:, :], y_done)
                    ln = ln + 1
                if do_a:
                    m_copy(g, O_AT, oT[:, 0:4, :].rearrange("p m t -> p (m t)"), M[0][:, :])
                if do_b:
                    b_copy(g - 1, YT2_AT, yT[:, :, :].rearrange("p c t -> p (c t)"))
                if do_a:
                    x1_add(g, 0)
                if do_b:
                    dve.wait_ge(b_full, B_FILLS * (g - 1) + LG_AT + 1)
                    nc.vector.tensor_tensor(logits[:, :], BK[:, 0:EXPERTS], gate_bias[:, :], ALU.add).then_inc(b_free, 1)
                    choose(g - 1)
                if do_a:
                    x1_add(g, 1)
                    for i in range(2):
                        dve.wait_ge(m_free[i], (M_FILLS // 2) * (g + 1))
                    layernorm(ln, x_all[:, bass.ds(g, 1), :].rearrange("p g d -> p (g d)"), y[:, :], y_done)
                if do_b:
                    place(g - 1)

            def choose(g):
                dve.wait_ge(b_free, 1 + B_FILLS * g + LG_AT + 1)
                link = chain(dve, rt_step, RT_LINKS * g)
                link(nc.vector.tensor_scalar(logits[:, :], logits[:, :], 1.0 / TEMP, None, ALU.mult))
                carry_wait()
                link(nc.vector.max(top[:, :], logits[:, :]))
                carry_wait()
                link(nc.vector.max_index(topi[:, :], top[:, :], logits[:, :]))
                nc.vector.tensor_tensor(gs[:, bass.ds(g, 1)], top[:, 1:2], top[:, 0:1], ALU.subtract)
                link(nc.vector.tensor_copy(topf[:, :], topi[:, 0:TOPK]))
                ke = [P, TOPK, EXPERTS]
                link(nc.vector.tensor_tensor(hot[:, :, :], iota_e[:, :].unsqueeze(1).to_broadcast(ke),
                                             topf[:, :].unsqueeze(2).to_broadcast(ke), ALU.is_equal))
                nc.vector.tensor_tensor(mask[:, :], hot[:, 0, :], hot[:, 1, :], ALU.add).then_inc(mask_done, 1)
                nc.vector.tensor_copy(topf_all[:, bass.ds(g, 1), :].rearrange("p g k -> p (g k)"), topf[:, :])

            def place(g):
                dve.wait_ge(b_full, B_FILLS * g + RK_AT + 1)
                nc.vector.tensor_tensor(rank[:, :], BK[:, 0:EXPERTS], next_row[:, :], ALU.add)
                nc.vector.tensor_tensor(next_row[:, :], BK[:, EXPERTS:2 * EXPERTS], next_row[:, :], ALU.add).then_inc(b_free, 1)
                dve.wait_ge(b_free, 1 + B_FILLS * (g + 1))
                link = chain(dve, rt_step, RT_LINKS * g + 5)
                link(nc.vector.tensor_tensor(prod[:, :, :], hot[:, :, :], rank[:, :].unsqueeze(1).to_broadcast([P, TOPK, EXPERTS]), ALU.mult))
                link(nc.vector.reduce_sum(slotf[:, :], prod[:, :, :], AX))
                nc.vector.tensor_copy(slotf_all[:, bass.ds(g, 1), :].rearrange("p g k -> p (g k)"), slotf[:, :])
                nc.vector.tensor_copy(slot_now[:, :], slotf[:, :]).then_inc(slots_ready, 1)

            def x1_add(g, j):
                dve.wait_ge(m_full, M_FILLS * g + WO_AT + j + 1)
                x_now = x_all[:, bass.ds(g, 1), j * 256:(j + 1) * 256].rearrange("p g d -> p (g d)")
                nc.vector.tensor_tensor(x_now, x_now, M[j][:, 0:256], ALU.add).then_inc(m_free[j], 1)

            dve.wait_ge(x0_in, 16)
            xn_norm(0, 0, 0)
            xn_norm(1, 0, 1)
            cn_stats(0, 0)
            cn_apply(0, 0)
            body(0, True, False, True)
            dve.wait_ge(gate_in, 32)
            dve.wait_ge(consts, 6)
            dve.wait_ge(xs_zeroed, 16 * (EXPERTS + 1))
            with dve.Fori(1, GROUPS - 1) as g:
                body(g, True, True, True)
            body(GROUPS - 1, True, True, False)
            body(GROUPS, False, True, False)
            moe_dve(dve)

        @block.tensor
        def _(pe):
            def setup_fill(n):
                if n >= 4:
                    pe.wait_ge(setup_free[n % 2], (n - 4) // 2 + 1)
                if n < 8:
                    for c in range(KC):
                        last = nc.tensor.transpose(bank[n % 4][:, c * P:(c + 1) * P], wk_rows[:, c, n * P:(n + 1) * P], ident[:, :])
                else:
                    rows, m = (qkv_rows, n - 8) if n < 12 else (wos_rows, n - 12)
                    for c in range(KD):
                        last = nc.tensor.transpose(bank[n % 4][:, c * P:(c + 1) * P], rows[:, c, m * P:(m + 1) * P], ident[:, :])
                last.then_inc(setup_full, 1)

            def m_open(g, at):
                at_least(pe, m_free[at % 2], (M_FILLS // 2) * g + at // 2)
                return M[at % 2]

            def m_ready(g, at):
                pe.wait_ge(m_free[at % 2], (M_FILLS // 2) * g + at // 2 + 1)

            def b_open(g, at):
                pe.wait_ge(b_free, 1 + B_FILLS * g + at)

            def q_proj(g, i):
                ps = m_open(g, QT_AT + i)
                for m in range(4):
                    for k in range(KD):
                        last = nc.tensor.matmul(ps[:, m * P:(m + 1) * P], wq[:, k, (4 * i + m) * P:(4 * i + m + 1) * P],
                                                xnT[:, k, :], start=(k == 0), stop=(k == KD - 1))
                last.then_inc(m_full, 1)

            def qk_proj(g, i):
                hq, c = i // KC, i % KC
                if i == 0 and isinstance(g, int) and g == 0:
                    for n in range(2):
                        pe.wait_ge(setup_free[n], 8)
                if i < 2:
                    at_least(pe, exp_done, HG * GB * g)
                    at_least(pe, pt3_out, 2 * g)
                else:
                    for par in range(2):
                        pe.wait_ge(qk_out[par], QK_PAIRS * g + i - 1)
                if c == 0:
                    m_ready(g, QT_AT + hq)
                for s in range(4):
                    for par in range(2):
                        rows = slice(HDIM * par, HDIM * (par + 1))
                        last = nc.tensor.matmul(bank[(2 * i + par) % 4][:, s * P:(s + 1) * P],
                                                wkT[rows, 4 * hq + s, c * P:(c + 1) * P],
                                                qT[rows, 4 * hq + s, :], start=True, stop=True)
                        if s == 3:
                            last.then_inc(qk_full, 1)

            def scores(g, b, h):
                bt = GB * g + b
                if h == 0:
                    at_least(pe, tp_free, (TP_FIRST + TP_FILLS * g) if b == 0 else tp(g, ("ct", b, 2)) + 1)
                if b > 0:
                    pe.wait_ge(exp_done, HG * (bt - 1) + h + 1)
                elif h == 0:
                    for par in range(2):
                        pe.wait_ge(qk_out[par], QK_PAIRS * (g + 1))
                for c in range(KC):
                    last = nc.tensor.matmul(bank[h][:, 0:KEYS], qkT[:, c, b, h * P:(h + 1) * P], cnT[:, b % 2, c, :],
                                            start=(c == 0), stop=(c == KC - 1))
                last.then_inc(s_full, 1)

            def ct_fill(n, bt, b, c):
                pe.wait_ge(tp_free, n)
                if c == 0:
                    pe.wait_ge(cn_done, bt + 1)
                for k in range(3):
                    last = nc.tensor.transpose(TP[:, KOFF[k]:KOFF[k] + PART[k]], ctx[0:PART[k], b % GB, k, c * P:(c + 1) * P],
                                               ident[0:PART[k], 0:PART[k]])
                last.then_inc(tp_full, 1)

            def pt_fill(g, b, k):
                into, full, count, _ = pt_place(g, b, k)
                if k == 1:
                    m_open(g, UT_AT + 4 * b)
                elif b < GB - 1:
                    pe.wait_ge(tp_free, count - 1)
                if k == 0:
                    pe.wait_ge(norm_done, GB * g + b + 1)
                for h in range(HG):
                    last = nc.tensor.transpose(into[0:PART[k], h * P:(h + 1) * P], probs[:, h, KOFF[k]:KOFF[k] + PART[k]], ident[:, :])
                last.then_inc(full, 1)

            def av(g, b, c):
                at, n = ut_at(b, c), GB * g + b
                ps = m_open(g, at)
                if c == 0:
                    pe.wait_ge(p_high_done, 3 * (n + 1))
                    pe.wait_ge(n_low_done, n + 1)
                for i, (n_part, p_part) in enumerate(((n_high[:, b % 2], pT_high), (n_low[:, b], pT_high), (n_high[:, b % 2], pT_low))):
                    if c == 0 and i == 2:
                        m_ready(g, UT_AT + 4 * b)
                        if b < GB - 1:
                            pe.wait_ge(tp_free, tp(g, ("pt", b, 2)) + 1)
                        else:
                            pe.wait_ge(pt3_out, 2 * (g + 1))
                    for k in range(3):
                        last = nc.tensor.matmul(ps[:, :], n_part[0:PART[k], k, c * P:(c + 1) * P], p_part[0:PART[k], k, :],
                                                start=(k == 0 and i == 0), stop=(k == 2 and i == 2))
                last.then_inc(m_full, 1)

            def o_proj(g, i):
                ps = m_open(g, O_AT + i)
                if i == 0:
                    m_ready(g, ut_at(GB - 1, 1))
                    m_ready(g, ut_at(GB - 1, 2))
                for s in range(4):
                    for par in range(2):
                        h = 2 * (4 * i + s) + par
                        for c in range(KC):
                            last = nc.tensor.matmul(ps[HDIM * par:HDIM * (par + 1), s * P:(s + 1) * P],
                                                    wv[:, c, h * HDIM:(h + 1) * HDIM],
                                                    uT[:, c, h, :, :].rearrange("p b t -> p (b t)"),
                                                    start=(c == 0), stop=(c == KC - 1))
                last.then_inc(m_full, 1)

            def wo_proj(g, j):
                ps = m_open(g, WO_AT + j)
                if j == 0:
                    m_ready(g, O_AT)
                    m_ready(g, O_AT + 1)
                for m in range(KI):
                    last = nc.tensor.matmul(ps[:, 0:256], oT[:, m, :], wo[:, m, j * 256:(j + 1) * 256],
                                            start=(m == 0), stop=(m == KI - 1))
                last.then_inc(m_full, 1)

            def xn_fill(n, count):
                pe.wait_ge(tp_free, n)
                pe.wait_ge(xn_done, count)
                for c in range(KD):
                    last = nc.tensor.transpose(TP[:, c * P:(c + 1) * P], xn[:, c * P:(c + 1) * P], ident[:, :])
                last.then_inc(tp_full, 1)

            def y_fill(g, at, count, src):
                b_open(g, at)
                pe.wait_ge(y_done, count)
                for c in range(KD):
                    last = nc.tensor.transpose(BK[:, c * P:(c + 1) * P], src[:, c * P:(c + 1) * P], ident[:, :])
                last.then_inc(b_full, 1)

            def kq_fill(g):
                b_open(g, KQ_AT)
                for m in range(KD):
                    for k in range(KD):
                        last = nc.tensor.matmul(BK[:, m * P:(m + 1) * P], wqkvT[:, k, m * P:(m + 1) * P], yT[:, k, :],
                                                start=(k == 0), stop=(k == KD - 1))
                last.then_inc(b_full, 1)

            def v_fill(g):
                b_open(g, V_AT)
                for m in range(KD):
                    last = nc.tensor.transpose(BK[:, m * P:(m + 1) * P], kqT[:, m, :], ident[:, :])
                last.then_inc(b_full, 1)

            def ss_fill(g, hh):
                b_open(g, SS_AT + (0 if ss_bank(g, hh) is not BK else hh))
                rows = slice(SDIM * hh, SDIM * (hh + 1))
                for m in range(4):
                    last = nc.tensor.matmul(ss_bank(g, hh)[:, m * P:(m + 1) * P], kqT[rows, m, :], kqT[rows, m, :], start=True, stop=True,
                                            tile_position=(SDIM * hh, 0))
                last.then_inc(b_full, 1)

            def pv_fill(g):
                b_open(g, PV_AT)
                pe.wait_ge(wb_done, g + 1)
                for m in range(4):
                    for hh in range(4):
                        h = 4 * m + hh
                        last = nc.tensor.matmul(BK[SDIM * hh:SDIM * (hh + 1), m * P:(m + 1) * P],
                                                v_sb[:, h * SDIM:(h + 1) * SDIM], blocks[:, h, :], start=True, stop=True,
                                                tile_position=(0, SDIM * hh))
                last.then_inc(b_full, 1)

            def ws_fill(g):
                b_open(g, WS_AT)
                for k in range(KD):
                    last = nc.tensor.matmul(BK[:, :], kqT[:, k, :], wosT[:, k, :], start=(k == 0), stop=(k == KD - 1))
                last.then_inc(b_full, 1)

            def lg_fill(g):
                b_open(g, LG_AT)
                for k in range(KD):
                    last = nc.tensor.matmul(BK[:, 0:EXPERTS], yT[:, k, :], gate[:, k, :], start=(k == 0), stop=(k == KD - 1))
                last.then_inc(b_full, 1)

            def rk_fill(g):
                b_open(g, RK_AT)
                pe.wait_ge(mask_done, g + 1)
                nc.tensor.matmul(BK[:, 0:EXPERTS], before[:, :], mask[:, :], start=True, stop=True)
                nc.tensor.matmul(BK[:, EXPERTS:2 * EXPERTS], ones[:, :], mask[:, :], start=True, stop=True).then_inc(b_full, 1)

            def body(g, do_a, do_b, nxt):
                if do_a:
                    at_least(pe, tp_free, 1 if isinstance(g, int) and g == 0 else TP_FIRST + TP_FILLS * g)
                    q_proj(g, 0)
                    q_proj(g, 1)
                if isinstance(g, int) and g == 0:
                    pe.wait_ge(wk_in, 16)
                    for n in range(8):
                        setup_fill(n)
                    for c in range(KC):
                        ct_fill(1 + c, 0, 0, c)
                    pe.wait_ge(qkv_in, 16)
                    pe.wait_ge(wos_in, 16)
                    for n in range(8, 16):
                        setup_fill(n)
                for i in range(QK_PAIRS):
                    if do_a:
                        qk_proj(g, i)
                    if do_b and i == 1:
                        y_fill(g - 1, YT_AT, 2 * (g - 1) + 1, y)
                    if do_b and i == 3:
                        kq_fill(g - 1)
                if do_b:
                    v_fill(g - 1)
                for b in range(GB + 1):
                    if do_a:
                        for h in range(HG):
                            if b < GB:
                                scores(g, b, h)
                            if b == 0 and h < 3:
                                ct_fill(tp(g, ("ct", 1, h)), GB * g + 1, 1, h)
                            if b >= 1 and h < 3:
                                pt_fill(g, b - 1, h)
                    if do_b and b == 0:
                        ss_fill(g - 1, 0)
                    if do_b and b == 2:
                        ss_fill(g - 1, 3)
                    for c in range(KC):
                        if do_a and (1 <= b < 3 or (b == GB and nxt)):
                            nb = b + 1 if b < GB else GB
                            ct_fill(tp(g, ("ct", nb, c)), GB * g + nb, nb, c)
                        if do_a and b >= 1:
                            av(g, b - 1, c)
                        if do_b and b == 1 and c != 1:
                            ss_fill(g - 1, 1 + c // 2)
                        if do_b and b == GB and c == 1:
                            pv_fill(g - 1)
                if do_b:
                    ws_fill(g - 1)
                if isinstance(g, int) and g == 0:
                    pe.wait_ge(wv_in, 16)
                    pe.wait_ge(wo_in, 16)
                    pe.wait_ge(gate_in, 32)
                if do_a:
                    o_proj(g, 0)
                    o_proj(g, 1)
                if nxt:
                    xn_fill(tp(g, "xn"), 2 * (g + 2))
                if do_b:
                    y_fill(g - 1, YT2_AT, 2 * g, y2)
                if do_a:
                    wo_proj(g, 0)
                if do_b:
                    lg_fill(g - 1)
                if do_a:
                    wo_proj(g, 1)
                if do_b:
                    rk_fill(g - 1)

            pe.wait_ge(ident_ok, 1)
            xn_fill(0, 2)
            pe.wait_ge(wq_in, 16)
            body(0, True, False, True)
            with pe.Fori(1, GROUPS - 1) as g:
                body(g, True, True, True)
            body(GROUPS - 1, True, True, False)
            body(GROUPS, False, True, False)
            moe_pe(pe)


_INS = ['x', 'ctx_768', 'L0_xattn_g_x', 'L0_xattn_b_x', 'L0_xattn_g_c', 'L0_xattn_b_c', 'L0_xattn_Wq', 'L0_xattn_Wk',
        'L0_xattn_Wv', 'L0_xattn_Wo', 'L0_attn_W_qkv', 'L0_attn_W_o', 'L0_ffn_gate_w', 'L0_ffn_gate_b', 'L0_ffn_w1',
        'L0_ffn_b1', 'L0_ffn_w2', 'L0_ffn_b2', 'L0_ffn_ln_g', 'L0_ffn_ln_b']


def kernel(**inputs):
    import numpy as _np
    import concourse.bacc as _bacc
    from concourse.bass_utils import run_bass_kernel_spmd as _run

    nc = _bacc.Bacc("TRN2", target_bir_lowering=False, num_devices=1)
    arrays, args = {}, []
    for name in _INS:
        a = _np.ascontiguousarray(inputs[name])
        arrays[f"in_{name}_dram"] = a
        args.append(nc.dram_tensor(f"in_{name}_dram", a.shape, mybir.dt.from_np(a.dtype), kind="ExternalInput").ap())
    out = nc.dram_tensor("out_dram", (BATCH, TOK, DIM), F32, kind="ExternalOutput").ap()
    perceiver_layer(nc, *args, out)
    r = _run(nc, [arrays], core_ids=[0])
    return r.results[0]["out_dram"]
```
